# Optimizing a Trainium2 kernel written in Bass

```python
import numpy as np
import jax
import jax.numpy as jnp

def _softmax(x, axis=-1):
    return jax.nn.softmax(x, axis=axis)

def _gelu(x):
    return jax.nn.gelu(x, approximate=True)

def _silu(x):
    return jax.nn.silu(x)

def _sigmoid(x):
    return jax.nn.sigmoid(x)

def _layernorm(x, axis=-1, eps=1e-05):
    m = jnp.mean(x, axis=axis, keepdims=True)
    v = jnp.var(x, axis=axis, keepdims=True)
    return (x - m) / jnp.sqrt(v + eps)

def _scatter_add(tgt, idx, src, axis=0):
    return tgt.at[idx].add(src)

def _segment_sum(src, seg, n):
    return jax.ops.segment_sum(src, seg, n)
kernel_name = 'mk_audio_tower_d2_tok_audfeat768_r4_07124c'

def setup_inputs(seed: int=0):
    np.random.seed(seed)
    _w = jnp.asarray

    def _rec_inputs():
        import jax
        import jax.numpy as jnp
        _rk = jax.random.key(seed)
        x = -0.000222058 + 0.999998 * jax.random.normal(jax.random.fold_in(_rk, 1), (16, 750, 192), jnp.float32)
        return x
    x = _rec_inputs()

    def _L0_tok_setup():
        import jax, jax.numpy as jnp
        import numpy as np
        B, S, D, K = (8, 1024, 192, 7)
        EPS = 1e-05
        key = jax.random.key(seed)
        k0, k1, k2, k3, k4 = jax.random.split(key, 5)
        return {'x': jax.random.normal(k0, (B, S, D), jnp.float32), 'w_dw': jax.random.normal(k1, (D, 1, K), jnp.float32) * 0.2, 'b_dw': jax.random.normal(k2, (D,), jnp.float32) * 0.02, 'w_pw': jax.random.normal(k3, (D, D, 1), jnp.float32) * 0.03, 'b_pw': jax.random.normal(k4, (D,), jnp.float32) * 0.02, 'gamma': jnp.ones((D,), jnp.float32), 'beta': jnp.zeros((D,), jnp.float32)}
    _L0_tok_all = _L0_tok_setup()
    _L0_tok_in = {k: v for k, v in _L0_tok_all.items() if k in ('w_dw', 'b_dw', 'w_pw', 'b_pw', 'gamma', 'beta')}
    del _L0_tok_all

    def _L0_attn_setup():
        import jax, jax.numpy as jnp
        import numpy as np
        NUM_HEADS = 12
        MAX_REL = 64
        key = jax.random.key(seed)
        k1, k2, k3, k4 = jax.random.split(key, 4)
        B, N, C = (4, 256, 192)
        x = jax.random.normal(k1, (B, N, C), dtype=jnp.float32)
        qkv_w = jax.random.normal(k2, (3 * C, C), dtype=jnp.float32) * 0.02
        proj_w = jax.random.normal(k3, (C, C), dtype=jnp.float32) * 0.02
        proj_b = jnp.zeros((C,), dtype=jnp.float32)
        rel_table = jax.random.normal(k4, (2 * MAX_REL + 1, NUM_HEADS), dtype=jnp.float32) * 0.02
        return {'x': x, 'qkv_w': qkv_w, 'proj_w': proj_w, 'proj_b': proj_b, 'rel_table': rel_table}
    _L0_attn_all = _L0_attn_setup()
    _L0_attn_in = {k: v for k, v in _L0_attn_all.items() if k in ('qkv_w', 'proj_w', 'proj_b', 'rel_table')}
    del _L0_attn_all

    def _L0_ffn_setup():
        import math
        import jax, jax.numpy as jnp
        import numpy as np
        B, L, D = (8, 1024, 192)
        E = 16
        TOP_K = 2
        F_EXP = 4 * D
        F_SH = F_EXP * 2 // 4
        key = jax.random.key(seed)
        ks = jax.random.split(key, 8)
        s = lambda fan_in: 1.0 / math.sqrt(fan_in)
        return {'hidden_states': jax.random.normal(ks[0], (B, L, D), jnp.float32), 'gate_weight': jax.random.uniform(ks[1], (E, D), jnp.float32, -s(D), s(D)), 'Wg': jax.random.uniform(ks[2], (E, F_EXP, D), jnp.float32, -s(D), s(D)), 'Wu': jax.random.uniform(ks[3], (E, F_EXP, D), jnp.float32, -s(D), s(D)), 'Wd': jax.random.uniform(ks[4], (E, D, F_EXP), jnp.float32, -s(F_EXP), s(F_EXP)), 'Ws_g': jax.random.uniform(ks[5], (F_SH, D), jnp.float32, -s(D), s(D)), 'Ws_u': jax.random.uniform(ks[6], (F_SH, D), jnp.float32, -s(D), s(D)), 'Ws_d': jax.random.uniform(ks[7], (D, F_SH), jnp.float32, -s(F_SH), s(F_SH))}
    _L0_ffn_all = _L0_ffn_setup()
    _L0_ffn_in = {k: v for k, v in _L0_ffn_all.items() if k in ('gate_weight', 'Wg', 'Wu', 'Wd', 'Ws_g', 'Ws_u', 'Ws_d')}
    del _L0_ffn_all

    def _L1_attn_setup():
        import jax, jax.numpy as jnp
        import numpy as np
        NUM_HEADS = 12
        EPS = 1e-06
        key = jax.random.key(seed)
        k1, k2, k3, k4 = jax.random.split(key, 4)
        N, B, D = (1025, 8, 192)
        x = jax.random.normal(k1, (N, B, D), dtype=jnp.float32)
        w_qkv = jax.random.normal(k2, (3 * D, D), dtype=jnp.float32) * D ** (-0.5)
        w_proj = jax.random.normal(k3, (D, D), dtype=jnp.float32) * D ** (-0.5)
        b_proj = jax.random.normal(k4, (D,), dtype=jnp.float32) * 0.01
        return {'x': x, 'w_qkv': w_qkv, 'w_proj': w_proj, 'b_proj': b_proj}
    _L1_attn_all = _L1_attn_setup()
    _L1_attn_in = {k: v for k, v in _L1_attn_all.items() if k in ('w_qkv', 'w_proj', 'b_proj')}
    del _L1_attn_all

    def _L1_ffn_setup():
        import jax, jax.numpy as jnp
        import numpy as np
        D_MODEL = 192
        D_FF = 768
        NUM_EXPERTS = 8
        EXPERT_CAPACITY = 256
        key = jax.random.key(seed)
        k0, k1, k2, k3 = jax.random.split(key, 4)
        hidden_states = jax.random.normal(k0, (2, 256, D_MODEL), dtype=jnp.float32)
        router_w = jax.random.normal(k1, (D_MODEL, NUM_EXPERTS), dtype=jnp.float32) * D_MODEL ** (-0.5)
        wi = jax.random.normal(k2, (NUM_EXPERTS, D_MODEL, D_FF), dtype=jnp.float32) * D_MODEL ** (-0.5)
        wo = jax.random.normal(k3, (NUM_EXPERTS, D_FF, D_MODEL), dtype=jnp.float32) * D_FF ** (-0.5)
        return {'hidden_states': hidden_states, 'router_w': router_w, 'wi': wi, 'wo': wo}
    _L1_ffn_all = _L1_ffn_setup()
    _L1_ffn_in = {k: v for k, v in _L1_ffn_all.items() if k in ('router_w', 'wi', 'wo')}
    del _L1_ffn_all
    return {'x': x, 'L0_tok_w_dw': _L0_tok_in['w_dw'], 'L0_tok_b_dw': _L0_tok_in['b_dw'], 'L0_tok_w_pw': _L0_tok_in['w_pw'], 'L0_tok_b_pw': _L0_tok_in['b_pw'], 'L0_tok_gamma': _L0_tok_in['gamma'], 'L0_tok_beta': _L0_tok_in['beta'], 'L0_attn_qkv_w': _L0_attn_in['qkv_w'], 'L0_attn_proj_w': _L0_attn_in['proj_w'], 'L0_attn_proj_b': _L0_attn_in['proj_b'], 'L0_attn_rel_table': _L0_attn_in['rel_table'], 'L0_ffn_gate_weight': _L0_ffn_in['gate_weight'], 'L0_ffn_Wg': _L0_ffn_in['Wg'], 'L0_ffn_Wu': _L0_ffn_in['Wu'], 'L0_ffn_Wd': _L0_ffn_in['Wd'], 'L0_ffn_Ws_g': _L0_ffn_in['Ws_g'], 'L0_ffn_Ws_u': _L0_ffn_in['Ws_u'], 'L0_ffn_Ws_d': _L0_ffn_in['Ws_d'], 'L1_attn_w_qkv': _L1_attn_in['w_qkv'], 'L1_attn_w_proj': _L1_attn_in['w_proj'], 'L1_attn_b_proj': _L1_attn_in['b_proj'], 'L1_ffn_router_w': _L1_ffn_in['router_w'], 'L1_ffn_wi': _L1_ffn_in['wi'], 'L1_ffn_wo': _L1_ffn_in['wo']}

def reference(x, L0_tok_w_dw, L0_tok_b_dw, L0_tok_w_pw, L0_tok_b_pw, L0_tok_gamma, L0_tok_beta, L0_attn_qkv_w, L0_attn_proj_w, L0_attn_proj_b, L0_attn_rel_table, L0_ffn_gate_weight, L0_ffn_Wg, L0_ffn_Wu, L0_ffn_Wd, L0_ffn_Ws_g, L0_ffn_Ws_u, L0_ffn_Ws_d, L1_attn_w_qkv, L1_attn_w_proj, L1_attn_b_proj, L1_ffn_router_w, L1_ffn_wi, L1_ffn_wo):
    import jax
    import jax.numpy as jnp

    def _L0_tok_ref(x, w_dw, b_dw, w_pw, b_pw, gamma, beta):
        import jax, jax.numpy as jnp
        import numpy as np
        B, S, D, K = (8, 1024, 192, 7)
        EPS = 1e-05
        d = w_dw.shape[0]
        h = jnp.transpose(x, (0, 2, 1))
        h = jax.lax.conv_general_dilated(h, w_dw, window_strides=(1,), padding='SAME', dimension_numbers=('NCH', 'OIH', 'NCH'), feature_group_count=d) + b_dw[None, :, None]
        h = jnp.einsum('od,bds->bos', w_pw[:, :, 0], h) + b_pw[None, :, None]
        h = jax.nn.relu(h)
        h = jax.lax.reduce_window(h, -jnp.inf, jax.lax.max, (1, 1, 2), (1, 1, 2), 'VALID')
        h = jnp.transpose(h, (0, 2, 1))
        y = jnp.real(jnp.fft.fft2(h))
        mu = jnp.mean(y, axis=-1, keepdims=True)
        var = jnp.var(y, axis=-1, keepdims=True)
        return (y - mu) * jax.lax.rsqrt(var + EPS) * gamma + beta

    def _L0_attn_ref(x, qkv_w, proj_w, proj_b, rel_table):
        import jax, jax.numpy as jnp
        import numpy as np
        NUM_HEADS = 12
        MAX_REL = 64
        B, N, C = x.shape
        H = NUM_HEADS
        D = C // H
        scale = D ** (-0.5)
        qkv = (x @ qkv_w.T).reshape(B, N, 3, H, D).transpose(2, 0, 3, 1, 4)
        q, k, v = (qkv[0], qkv[1], qkv[2])
        attn = jnp.einsum('bhnd,bhmd->bhnm', q, k) * scale
        idx = jnp.clip(jnp.arange(N)[None, :] - jnp.arange(N)[:, None] + MAX_REL, 0, 2 * MAX_REL)
        pos_bias = rel_table[idx]
        attn = attn + pos_bias.transpose(2, 0, 1)[None]
        attn = jax.nn.softmax(attn, axis=-1)
        out = jnp.einsum('bhnm,bhmd->bnhd', attn, v).reshape(B, N, C)
        return out @ proj_w.T + proj_b

    def _L0_ffn_ref(hidden_states, gate_weight, Wg, Wu, Wd, Ws_g, Ws_u, Ws_d):
        import math
        import jax, jax.numpy as jnp
        import numpy as np
        B, L, D = (8, 1024, 192)
        E = 16
        TOP_K = 2
        F_EXP = 4 * D
        F_SH = F_EXP * 2 // 4
        b, l, d = hidden_states.shape
        n = b * l
        x = hidden_states.reshape(n, d)
        scores = jax.nn.sigmoid(x @ gate_weight.T)
        capacity = math.ceil(n / E * TOP_K)
        topk_score, topk_ids = jax.lax.top_k(scores.T, capacity)
        xg = x[topk_ids]
        gate = jax.nn.silu(jnp.einsum('ecd,efd->ecf', xg, Wg))
        up = jnp.einsum('ecd,efd->ecf', xg, Wu)
        out = jnp.einsum('ecf,edf->ecd', gate * up, Wd)
        out = out * topk_score[..., None]
        y = jnp.zeros((n, d), x.dtype).at[topk_ids.reshape(-1)].add(out.reshape(-1, d))
        y = y.reshape(b, l, d)
        shared = jax.nn.silu(hidden_states @ Ws_g.T) * (hidden_states @ Ws_u.T) @ Ws_d.T
        return y + shared

    def _L1_attn_ref(x, w_qkv, w_proj, b_proj):
        import jax, jax.numpy as jnp
        import numpy as np
        NUM_HEADS = 12
        EPS = 1e-06
        N, B, D = x.shape
        H = NUM_HEADS
        hd = D // H
        scale = hd ** (-0.5)
        scale_vv = scale * 1.0
        xb = jnp.transpose(x, (1, 0, 2))
        qkv = xb @ w_qkv.T
        qkv = qkv.reshape(B, N, 3, H, hd).transpose(2, 0, 3, 1, 4)
        q, k, v = (qkv[0], qkv[1], qkv[2])
        scores0 = jnp.einsum('bhqd,bhkd->bhqk', q[:, :, :1], k) * scale
        attn0 = jax.nn.softmax(scores0, axis=-1)
        out0 = jnp.einsum('bhqk,bhkd->bhqd', attn0, v)
        vn = v / jnp.maximum(jnp.linalg.norm(v, axis=-1, keepdims=True), EPS)
        scores_vv = jnp.einsum('bhqd,bhkd->bhqk', vn[:, :, 1:], vn) * scale_vv
        attn_vv = jax.nn.softmax(scores_vv, axis=-1)
        out_vv = jnp.einsum('bhqk,bhkd->bhqd', attn_vv, v)
        out = jnp.concatenate([out0, out_vv], axis=2)
        out = out.transpose(0, 2, 1, 3).reshape(B, N, D)
        out = out @ w_proj.T + b_proj
        return jnp.transpose(out, (1, 0, 2))

    def _L1_ffn_ref(hidden_states, router_w, wi, wo):
        import jax, jax.numpy as jnp
        import numpy as np
        D_MODEL = 192
        D_FF = 768
        NUM_EXPERTS = 8
        EXPERT_CAPACITY = 256
        B, S, d = hidden_states.shape
        E = router_w.shape[1]
        x = hidden_states.reshape(-1, d)
        logits = x.astype(jnp.float32) @ router_w.astype(jnp.float32)
        probs = jax.nn.softmax(logits, axis=-1).astype(x.dtype)
        p = jnp.max(probs, axis=-1)
        e_idx = jnp.argmax(probs, axis=-1)
        mask = jax.nn.one_hot(e_idx, E, dtype=x.dtype)
        token_priority = jnp.cumsum(mask[:, None, :], axis=-2)[:, 0, :]
        mask = mask * (token_priority <= EXPERT_CAPACITY).astype(x.dtype)
        combine = mask * p[:, None]

        def body(acc, ew):
            Wi_e, Wo_e, w_e = ew
            h = jax.nn.relu(x @ Wi_e) @ Wo_e
            return (acc + w_e[:, None] * h, None)
        out, _ = jax.lax.scan(body, jnp.zeros_like(x), (wi, wo, combine.T))
        return out.reshape(B, S, d)
    h = _L0_tok_ref(x, L0_tok_w_dw, L0_tok_b_dw, L0_tok_w_pw, L0_tok_b_pw, L0_tok_gamma, L0_tok_beta)
    h = h + _L0_attn_ref(_layernorm(h, axis=-1), L0_attn_qkv_w, L0_attn_proj_w, L0_attn_proj_b, L0_attn_rel_table)
    h = h + _L0_ffn_ref(_layernorm(h, axis=-1), L0_ffn_gate_weight, L0_ffn_Wg, L0_ffn_Wu, L0_ffn_Wd, L0_ffn_Ws_g, L0_ffn_Ws_u, L0_ffn_Ws_d)
    h = h + _L1_attn_ref(_layernorm(h, axis=-1), L1_attn_w_qkv, L1_attn_w_proj, L1_attn_b_proj)
    h = h + _L1_ffn_ref(_layernorm(h, axis=-1), L1_ffn_router_w, L1_ffn_wi, L1_ffn_wo)
    return h

_drawn_inputs = setup_inputs


def setup_inputs(seed=0):
    import zlib

    import numpy as np

    out = dict(_drawn_inputs(seed))
    spreads = {'L0_tok_gamma': (1.0, 0.2), 'L0_tok_beta': (0.0, 0.1), 'L0_attn_proj_b': (0.0, 0.1)}
    factors = {'L0_attn_qkv_w': 2.792,
     'L0_attn_proj_w': 2.733,
     'L0_attn_rel_table': 32.342,
     'L1_attn_b_proj': 3.16}
    for name, (base, spread) in spreads.items():
        noise = np.random.default_rng([zlib.crc32(name.encode()), seed]).standard_normal(out[name].shape)
        drawn = base * np.exp(spread * noise) if base else spread * noise
        out[name] = jnp.asarray(drawn.astype(out[name].dtype))
    for name, factor in factors.items():
        out[name] = (out[name] * factor).astype(out[name].dtype)
    return out
```

```python
from contextlib import ExitStack

import numpy as np

import concourse.bass as bass
from concourse import mybir

F32 = mybir.dt.float32
BF16 = mybir.dt.bfloat16
I32 = mybir.dt.int32
U32 = mybir.dt.uint32
ALU = mybir.AluOpType
ACT = mybir.ActivationFunctionType
AX = mybir.AxisListType

B = 16
S_IN = 750
S = S_IN // 2
D = 192
DH = D // 2
H = 12
HD = D // H
K = 7
PAD = K // 2
TT = 125
NT = S // TT
SP = (-(-S // 8) + 1) * 8
EPS = 1e-5
SCALE = HD ** -0.5
NG = H // 4
VA = HD + 1
UNITS = H * NT
EXP = 16
XROW = D + EXP
FSH = 384
NFS = FSH // 128
RELW = S + (NT - 1) * TT
XS_W = 388
XS_TILES = 56


def ge(eng, sem, n):
    if isinstance(n, int) and n <= 0:
        return
    eng.wait_ge(sem, n)


def clear(nc, sems):
    with nc.Block() as block:
        @block.gpsimd
        def _(pool):
            numbers = sorted(s.num for s in sems)
            at = 0
            for n in range(1, len(numbers) + 1):
                if n == len(numbers) or numbers[n] != numbers[n - 1] + 1:
                    pool.sem_clear(range(numbers[at], numbers[n - 1] + 1))
                    at = n


POST_SLOT = {
    "ot0": 4, "ot1": 4, "pj0": 6, "pj1": 6, "pj2": 7, "x1t0": 11, "x1t1": 11, "gate": 12,
    "sg0": 13, "su0": 13, "sg1": 14, "su1": 14, "sct": 15, "sg2": 15, "su2": 16,
    "sd0": 18, "sd1": 18, "sd2": 19,
}
PRE_SLOT = {
    "pw00": 20, "pw01": 20, "pw10": 21, "pw11": 21, "dfa0": 23, "dfa1": 23, "dfa2": 24,
    "dfb0": 25, "dfb1": 26, "dfb2": 26, "xt0": 31, "xt1": 31,
    "q0": 32, "k0": 32, "v0": 33, "v1": 33, "v2": 33, "q1": 34, "k1": 34, "q2": 35, "k2": 35,
}
ORDER = list(POST_SLOT) + list(PRE_SLOT)
BANK = {name: n % 2 for n, name in enumerate(ORDER)}
ON_ACT = {"dfa0", "dfa1", "dfa2", "dfb0", "dfb1", "dfb2", "xt0", "x1t0", "ot0", "gate",
          "q0", "q1", "q2"}


class Round:

    def __init__(self, b, par, attn, tail, pre, post, prev):
        self.b, self.par, self.attn, self.tail, self.pre, self.post, self.prev = b, par, attn, tail, pre, post, prev

    def has(self, name):
        return self.post if name in POST_SLOT else self.pre

    def batch(self, name):
        return self.b - 1 if name in POST_SLOT else self.b + 1

    def before(self, name):
        n = ORDER.index(name)
        for m in range(n - 1, -1, -1):
            if BANK[ORDER[m]] == BANK[name] and self.has(ORDER[m]):
                return ORDER[m], self.batch(ORDER[m]) + 1
        if self.prev is None:
            return None
        for m in range(len(ORDER) - 1, -1, -1):
            if BANK[ORDER[m]] == BANK[name] and self.prev.has(ORDER[m]):
                return ORDER[m], self.batch(ORDER[m])
        return None


def phase1(nc, d, psS, psT, psO, psM, rounds=B):
    with ExitStack() as ctx:
        def sb(name, shape, dt=F32):
            return ctx.enter_context(nc.sbuf_tensor(name, shape, dt))

        sems = []

        def sem(name):
            sems.append(ctx.enter_context(nc.semaphore(name)))
            return sems[-1]

        ident = sb("ident", [128, 128])
        wdw = sb("wdw", [DH, 2, K])
        bdw = sb("bdw", [DH, 2])
        wpw = sb("wpw", [DH, 2, D])
        bpw = sb("bpw", [DH, 2])
        dftd = sb("dftd", [DH, 2, 2 * D])
        dftc = sb("dftc", [TT, NT, S])
        dfts = sb("dfts", [TT, NT, S])
        gam = sb("gam", [TT, D])
        bet = sb("bet", [TT, D])
        pjb = sb("pjb", [TT, D])
        wq = sb("wq", [DH, 2, NG, 128])
        wk = sb("wk", [DH, 2, NG, 128])
        wv = sb("wv", [DH, 2, D])
        wpj = sb("wpj", [DH, 2, D])
        rel = sb("rel", [TT, H, RELW])
        wgt = sb("wgt", [DH, 2, EXP])
        wsg = sb("wsg", [DH, 2, FSH])
        wsu = sb("wsu", [DH, 2, FSH])
        wsd = sb("wsd", [128, NFS, D])
        mhalf = sb("mhalf", [128, NT])
        epst = sb("epst", [128, NT])
        xin = sb("xin", [DH, 2, S_IN + 2 * PAD])
        conv = sb("conv", [DH, 2, S_IN])
        pooled = sb("pooled", [DH, 2, S])
        hT = sb("hT", [DH, 2, S])
        gdft = sb("gdft", [TT, NT, 2 * D])
        y = sb("y", [TT, NT, D])
        st1 = sb("st1", [TT, NT, 6])
        mv1 = sb("mv1", [TT, NT, 2])
        rs1 = sb("rs1", [TT, NT])
        yn = sb("yn", [TT, NT, D])
        h = sb("h", [TT, NT, D])
        hb = sb("hb", [TT, 2, NT, D])
        st2 = sb("st2", [TT, NT, 6])
        mv2 = sb("mv2", [TT, NT, 2])
        rs2 = sb("rs2", [TT, NT])
        xn = sb("xn", [TT, NT, D])
        xnT = sb("xnT", [DH, 2, S])
        qT = sb("qT", [128, 2, NG, S])
        kT = sb("kT", [128, 2, NG, S])
        va = sb("va", [TT, 2, NT, H, VA])
        added = sb("added", [TT, 3, S])
        nmax = sb("nmax", [TT, 3])
        prob = sb("prob", [TT, 3, S])
        probT = sb("probT", [TT, 2, S])
        oraw = sb("oraw", [TT, NT, H, VA])
        rsum = sb("rsum", [TT, NT, H])
        on = sb("on", [TT, NT, D])
        oT = sb("oT", [DH, 2, S])
        h1 = sb("h1", [TT, NT, D])
        st3 = sb("st3", [TT, NT, 6])
        mv3 = sb("mv3", [TT, NT, 2])
        rs3 = sb("rs3", [TT, NT])
        xrow = sb("xrow", [TT, NT, XROW])
        x1T = sb("x1T", [DH, 2, S])
        esc = sb("esc", [EXP, S])
        esc1 = sb("esc1", [EXP, S])
        sc = sb("sc", [128, S])
        th = sb("th", [128, S])
        ga = sb("ga", [128, S])
        hs = sb("hs", [128, NFS, S])
        h2 = sb("h2", [TT, NT, D])
        spare = sb("spare", [TT, 6])
        zero = sb("zero", [128, (SP - S) * XROW])

        ld_w, ld_x = sem("ld_w"), sem("ld_x")
        set_up = sem("set_up")
        rel_neg, va_one = sem("rel_neg"), sem("va_one")
        ready = {j: sem(f"{j}_ready") for j in ORDER}
        done = {j: sem(f"{j}_done") for j in ORDER}
        s_ready, add_done, exp_done = sem("s_ready"), sem("add_done"), sem("exp_done")
        t_ready, pt_done, av_done = sem("t_ready"), sem("pt_done"), sem("av_done")
        conv_done, relu_done = sem("conv_done"), sem("relu_done")
        st1_done, rs1_done, yn_done, h_done, hb_done = sem("st1_done"), sem("rs1_done"), sem("yn_done"), sem("h_done"), sem("hb_done")
        st2_done, rs2_done, xn_done = sem("st2_done"), sem("rs2_done"), sem("xn_done")
        o_read, o_sum, on_done = sem("o_read"), sem("o_sum"), sem("on_done")
        st3_done, rs3_done, x1_done = sem("st3_done"), sem("rs3_done"), sem("x1_done")
        th_done, esc_done, sc_done = sem("th_done"), sem("esc_done"), sem("sc_done")
        out_st, out_x1, out_h3, out_z = sem("out_st"), sem("out_x1"), sem("out_h3"), sem("out_z")
        z_set = sem("z_set")

        WEIGHTS = [(wdw, "wdw"), (bdw, "bdw"), (wpw, "wpw"), (bpw, "bpw"), (dftd, "dftd"), (dftc, "dftc"),
                   (dfts, "dfts"), (gam, "gam"), (bet, "bet"), (wq, "wq"), (wk, "wk"), (wv, "wv"),
                   (pjb, "pjb"), (wpj, "wpj"), (rel, "rel"), (wgt, "wgt"), (wsg, "wsg"), (wsu, "wsu"), (wsd, "wsd")]
        W_ALL = 16 * len(WEIGHTS)

        def run(eng, body):
            first = Round(-1, 1, False, False, True, False, None)
            body(first)
            second = Round(0, 0, True, False, True, False, first)
            body(second)
            body(Round(1, 1, True, True, True, True, second))
            with eng.Fori(0, (rounds - 4) // 2) as i:
                for n in range(2):
                    body(Round(i * 2 + 2 + n, n, True, True, True, True, second))
            inner = Round(rounds - 2, 0, True, True, True, True, second)
            body(inner)
            last = Round(rounds - 1, 1, True, True, False, True, inner)
            body(last)
            body(Round(rounds, 0, False, True, False, True, last))

        def units(r, slot, lag):
            u = slot - lag
            if u >= 0:
                return (r.b, u, r.par) if r.attn else None
            return (r.b - 1, u + UNITS, 1 - r.par) if r.tail else None

        blocks = ctx.enter_context(ExitStack())
        block = blocks.enter_context(nc.Block())

        @block.sync
        def _(sp):
            for t, name in WEIGHTS:
                sp.dma_start(t[:], d[name]).then_inc(ld_w, 16)
            sp.wait_ge(z_set, 1)
            for z in range(XS_TILES):
                sp.dma_start(d["xs"][z * 128:(z + 1) * 128, :], zero[:, 0:XS_W]).then_inc(out_z, 16)
            sp.dma_start(d["h3"][:, S:SP, :], zero[0:B, 0:(SP - S) * D].rearrange("p (s c) -> p s c", c=D)).then_inc(out_z, 16)
            sp.dma_start(d["x1"][:, S:SP, :], zero[0:B, :].rearrange("p (s c) -> p s c", c=XROW)).then_inc(out_z, 16)

            def body(r):
                if r.pre:
                    ge(sp, conv_done, r.b + 1)
                    sp.dma_start(xin[:], d["x"][r.b + 1]).then_inc(ld_x, 16)
                if r.post:
                    b = r.b - 1
                    sp.wait_ge(sc_done, b + 1)
                    sp.dma_start(d["st"][:, b, :], sc[0:EXP, :]).then_inc(out_st, 16)
                    sp.wait_ge(done["sct"], b + 1)
                    sp.dma_start(d["x1"][b, 0:S, :].rearrange("(t p) c -> p t c", p=TT), xrow[:]).then_inc(out_x1, 16)
                    sp.wait_ge(done["sd2"], b + 1)
                    sp.dma_start(d["h3"][b, 0:S, :].rearrange("(t p) c -> p t c", p=TT), h2[:]).then_inc(out_h3, 16)
            run(sp, body)
            sp.wait_ge(out_st, 16 * rounds)
            sp.wait_ge(out_x1, 16 * rounds)
            sp.wait_ge(out_h3, 16 * rounds)
            sp.wait_ge(out_z, 16 * (XS_TILES + 2))

        @block.gpsimd
        def _(pool):
            pool.memset(ident[:], 0.0)
            pool.memset(mhalf[:], -0.5)
            pool.memset(epst[:], EPS)
            pool.memset(sc[:], 0.0)
            pool.memset(zero[:], 0.0)
            pool.drain().then_inc(z_set, 1)
            pool.affine_select(out=ident[:], in_=ident[:], compare_op=ALU.not_equal, fill=1.0, base=0,
                               pattern=[[-1, 128]], channel_multiplier=1)
            for p in range(2):
                pool.memset(va[:, p], 1.0)
            pool.drain().then_inc(set_up, 1)

            def rstd(var, rs):
                pool.tensor_tensor(rs[:], var, epst[0:TT, :], ALU.add)
                pool.drain()
                return pool.tensor_tensor(rs[:], rs[:], mhalf[0:TT, :], ALU.pow)

            def body(r):
                if r.post:
                    b = r.b - 1
                    par = 1 - r.par
                    ge(pool, ready["ot1"], b)
                    pool.wait_ge(o_sum, b + 1)
                    pool.tensor_tensor(on[:].rearrange("p t (h e) -> p (t h) e", e=HD),
                                       oraw[:].rearrange("p t h e -> p (t h) e")[:, :, 0:HD],
                                       rsum[:].rearrange("p t h -> p (t h)").unsqueeze(2).broadcast_to([TT, NT * H, HD]),
                                       ALU.mult).then_inc(on_done, 1)
                    pool.wait_ge(st3_done, b + 1)
                    rstd(mv3[:, :, 1], rs3).then_inc(rs3_done, 1)
                if r.pre:
                    b = r.b + 1
                    par = 1 - r.par
                    pool.wait_ge(st1_done, b + 1)
                    rstd(mv1[:, :, 1], rs1).then_inc(rs1_done, 1)
                    pool.wait_ge(yn_done, b + 1)
                    ge(pool, xn_done, b)
                    pool.tensor_tensor(yn[:], yn[:], gam[:].unsqueeze(1).broadcast_to([TT, NT, D]), ALU.mult)
                    pool.drain()
                    pool.tensor_tensor(h[:], yn[:], bet[:].unsqueeze(1).broadcast_to([TT, NT, D]), ALU.add)
                    pool.drain().then_inc(h_done, 1)
                    ge(pool, done["pj2"], b - 1)
                    pool.tensor_tensor(hb[:, par], h[:], pjb[:].unsqueeze(1).broadcast_to([TT, NT, D]),
                                       ALU.add).then_inc(hb_done, 1)
                    pool.wait_ge(st2_done, b + 1)
                    rstd(mv2[:, :, 1], rs2).then_inc(rs2_done, 1)
            pool.wait_ge(ld_w, W_ALL)
            run(pool, body)

        @block.tensor
        def _(pe):
            pe.wait_ge(ld_w, W_ALL)
            pe.wait_ge(set_up, 1)
            pe.wait_ge(rel_neg, 1)

            def scores(b, u, par):
                hh, qt = divmod(u, NT)
                g, q = divmod(hh, 4)
                n = b * UNITS + u
                if u == 0:
                    pe.wait_ge(done["k0"], b + 1)
                    pe.wait_ge(done["q0"], b + 1)
                if qt == 0 and q == 0 and g > 0:
                    pe.wait_ge(done[f"k{g}"], b + 1)
                    pe.wait_ge(done[f"q{g}"], b + 1)
                ge(pe, add_done, n - 1)
                pe.matmul(psS[0:TT, u % 2, 0:S], qT[32 * q:32 * q + HD, par, g, qt * TT:(qt + 1) * TT],
                          kT[32 * q:32 * q + HD, par, g, :], start=True, stop=True).then_inc(s_ready, 1)

            def turn(b, u, par):
                n = b * UNITS + u
                ge(pe, pt_done, n - 1)
                pe.wait_ge(exp_done, n + 1)
                for kt in range(NT):
                    mm = pe.transpose(psT[0:TT, u % 2, kt * TT:(kt + 1) * TT], prob[:, u % 3, kt * TT:(kt + 1) * TT],
                                      ident[0:TT, 0:TT])
                mm.then_inc(t_ready, 1)

            def values(b, u, par):
                hh, qt = divmod(u, NT)
                if u == 0:
                    ge(pe, o_read, b)
                    pe.wait_ge(done["v2"], b + 1)
                    pe.wait_ge(done["v1"], b + 1)
                    pe.wait_ge(done["v0"], b + 1)
                pe.wait_ge(pt_done, b * UNITS + u + 1)
                o = psO[0:TT, qt // 2, (qt % 2) * H * VA + hh * VA:(qt % 2) * H * VA + (hh + 1) * VA]
                for kt in range(NT):
                    mm = pe.matmul(o, probT[:, u % 2, kt * TT:(kt + 1) * TT], va[:, par, kt, hh, :],
                                   start=(kt == 0), stop=(kt == NT - 1))
                mm.then_inc(av_done, 1)

            def by_halves(out, lhs, rhs, parts=2):
                for k in range(parts):
                    mm = pe.matmul(out, lhs(k), rhs(k), start=(k == 0), stop=(k == parts - 1))
                return mm

            def job(r, name):
                b = r.batch(name)
                bank = psM[:, BANK[name], :]
                last = r.before(name)
                if last is not None:
                    ge(pe, done[last[0]], last[1])
                kind, n = name[:-1], int(name[-1]) if name[-1].isdigit() else 0
                tt = slice(n * TT, (n + 1) * TT)
                if name.startswith("pw"):
                    oh, sh = int(name[2]), int(name[3])
                    if n == 0 and oh == 0:
                        pe.wait_ge(conv_done, b + 1)
                    lo, hi = (0, S + 1) if sh == 0 else (S + 1, S_IN)
                    mm = by_halves(bank[0:DH, 0:hi - lo], lambda k: wpw[:, k, oh * DH:(oh + 1) * DH],
                                   lambda k: conv[:, k, lo:hi])
                elif kind == "dfa":
                    if n == 0:
                        pe.wait_ge(relu_done, 2 * b + 2)
                    mm = by_halves(bank[0:TT, 0:2 * D], lambda k: hT[:, k, tt], lambda k: dftd[:, k, :])
                elif kind == "dfb":
                    if n == 0:
                        for j in range(3):
                            pe.wait_ge(done[f"dfa{j}"], b + 1)
                    for k in range(NT):
                        pe.matmul(bank[0:TT, 0:D], dftc[:, k, tt], gdft[:, k, 0:D], start=(k == 0), stop=False)
                        mm = pe.matmul(bank[0:TT, 0:D], dfts[:, k, tt], gdft[:, k, D:2 * D], start=False,
                                       stop=(k == NT - 1))
                elif kind in ("xt", "x1t", "ot"):
                    src = {"xt": xn, "x1t": xrow, "ot": on}[kind]
                    pe.wait_ge({"xt": xn_done, "x1t": x1_done, "ot": on_done}[kind], b + 1)
                    for t in range(NT):
                        mm = pe.transpose(bank[0:DH, t * TT:(t + 1) * TT], src[:, t, n * DH:(n + 1) * DH],
                                          ident[0:TT, 0:TT])
                elif kind in ("q", "k"):
                    if name == "q0":
                        pe.wait_ge(done["xt0"], b + 1)
                        pe.wait_ge(done["xt1"], b + 1)
                    w = wq if kind == "q" else wk
                    mm = by_halves(bank[:, 0:S], lambda k: w[:, k, n, :], lambda k: xnT[:, k, :])
                elif kind == "v":
                    mm = by_halves(bank[0:TT, 0:D], lambda k: xnT[:, k, tt], lambda k: wv[:, k, :])
                elif kind == "pj":
                    if n == 0:
                        pe.wait_ge(done["ot0"], b + 1)
                        pe.wait_ge(done["ot1"], b + 1)
                    mm = by_halves(bank[0:TT, 0:D], lambda k: oT[:, k, tt], lambda k: wpj[:, k, :])
                elif name == "gate":
                    pe.wait_ge(done["x1t0"], b + 1)
                    pe.wait_ge(done["x1t1"], b + 1)
                    mm = by_halves(bank[0:EXP, 0:S], lambda k: wgt[:, k, :], lambda k: x1T[:, k, :])
                elif name == "sct":
                    pe.wait_ge(sc_done, b + 1)
                    for t in range(NT):
                        mm = pe.transpose(bank[0:TT, t * 128:(t + 1) * 128], sc[:, t * TT:(t + 1) * TT],
                                          ident[:, :])
                elif kind in ("sg", "su"):
                    w = wsg if kind == "sg" else wsu
                    mm = by_halves(bank[:, 0:S], lambda k: w[:, k, n * 128:(n + 1) * 128], lambda k: x1T[:, k, :])
                else:
                    if n == 0:
                        for j in range(3):
                            pe.wait_ge(done[f"su{j}"], b + 1)
                    mm = by_halves(bank[0:TT, 0:D], lambda k: hs[:, k, tt], lambda k: wsd[:, k, :], NFS)
                mm.then_inc(ready[name], 1)

            def body(r):
                for s in range(UNITS):
                    for lag, step in ((0, scores), (2, turn), (3, values)):
                        at = units(r, s, lag)
                        if at is not None:
                            step(*at)
                    for name in ORDER:
                        if r.has(name) and {**POST_SLOT, **PRE_SLOT}[name] == s:
                            job(r, name)
            run(pe, body)

        @block.scalar
        def _(act):
            def exps(b, u, par):
                n = b * UNITS + u
                ge(act, t_ready, n - 2)
                act.wait_ge(add_done, n + 1)
                act.activation(prob[:, u % 3, :], added[:, u % 3, :], ACT.Exp, bias=nmax[:, u % 3:u % 3 + 1],
                               scale=-1.0).then_inc(exp_done, 1)

            def turned(b, u, par):
                n = b * UNITS + u
                ge(act, av_done, n - 1)
                act.wait_ge(t_ready, n + 1)
                act.copy(probT[:, u % 2, :], psT[0:TT, u % 2, 0:S]).then_inc(pt_done, 1)

            def relu(b, oh):
                act.wait_ge(done[f"pw{oh}1"], b + 1)
                if oh == 0:
                    ge(act, ready["dfa2"], b)
                act.activation(hT[:, oh, :], pooled[:, oh, :], ACT.Relu, bias=bpw[:, oh:oh + 1]).then_inc(relu_done, 1)

            def empty(r, name):
                b = r.batch(name)
                bank = psM[:, BANK[name], :]
                kind, n = name[:-1], int(name[-1]) if name[-1].isdigit() else 0
                tt = slice(n * TT, (n + 1) * TT)
                act.wait_ge(ready[name], b + 1)
                if kind == "dfa":
                    if n == 0:
                        ge(act, ready["dfb2"], b)
                    i = act.copy(gdft[:, n, :], bank[0:TT, 0:2 * D])
                elif kind == "dfb":
                    if n == 0:
                        ge(act, yn_done, b)
                    i = act.copy(y[:, n, :], bank[0:TT, 0:D])
                elif name == "xt0":
                    ge(act, ready["k2"], b)
                    i = act.copy(xnT[:, 0, :], bank[0:DH, 0:S])
                elif name == "x1t0":
                    ge(act, ready["su2"], b)
                    i = act.copy(x1T[:, 0, :], bank[0:DH, 0:S])
                elif name == "ot0":
                    ge(act, ready["pj2"], b)
                    i = act.copy(oT[:, 0, :], bank[0:DH, 0:S])
                elif kind == "q":
                    if n == 0:
                        ge(act, s_ready, (b - 1) * UNITS)
                    i = act.mul(qT[:, 1 - r.par, n, :], bank[:, 0:S], -SCALE)
                elif name == "gate":
                    ge(act, sc_done, b)
                    i = act.activation(esc[:], bank[0:EXP, 0:S], ACT.Exp, scale=-1.0)
                i.then_inc(done[name], 1)

            def tanh(b, n):
                act.wait_ge(ready[f"sg{n}"], b + 1)
                if n > 0:
                    act.wait_ge(done[f"sg{n - 1}"], b + 1)
                else:
                    ge(act, done["sg2"], b)
                act.activation(th[:], psM[:, BANK[f"sg{n}"], 0:S], ACT.Tanh, scale=0.5).then_inc(th_done, 1)

            def body(r):
                for s in range(UNITS):
                    at = units(r, s, 1)
                    if at is not None:
                        exps(*at)
                    at = units(r, s, 2)
                    if at is not None:
                        turned(*at)
                    for name in ORDER:
                        if r.has(name) and {**POST_SLOT, **PRE_SLOT}[name] == s:
                            if name in ON_ACT:
                                empty(r, name)
                            elif name.startswith("sg"):
                                tanh(r.batch(name), int(name[2]))
                            if name in ("pw01", "pw11"):
                                relu(r.batch(name), int(name[2]))
            act.wait_ge(ld_w, W_ALL)
            run(act, body)

        @block.vector
        def _(dve):
            dve.wait_ge(ld_w, W_ALL)
            dve.tensor_scalar(rel[:], rel[:], -1.0, None, ALU.mult).then_inc(rel_neg, 1)
            dve.wait_ge(rel_neg, 1)
            dve.wait_ge(set_up, 1)

            def add(b, u, par):
                hh, qt = divmod(u, NT)
                n = b * UNITS + u
                lo = (NT - 1 - qt) * TT
                dve.tensor_tensor_reduce(out=added[:, u % 3, :], in0=psS[0:TT, u % 2, 0:S],
                                         in1=rel[:, hh, lo:lo + S], scale=1.0, scalar=3.0e38, op0=ALU.add,
                                         op1=ALU.min, accum_out=nmax[:, u % 3:u % 3 + 1]).then_inc(add_done, 1)

            def add_waits(b, u, par):
                n = b * UNITS + u
                dve.wait_ge(s_ready, n + 1)
                ge(dve, exp_done, n - 2)

            def tap(b, k):
                if k == 0:
                    ge(dve, ready["pw11"], b)
                    dve.wait_ge(ld_x, 16 * b + 16)
                for half in range(2):
                    x = xin[:, half, k:k + S_IN]
                    w = wdw[:, half, k:k + 1]
                    if k == 0:
                        dve.tensor_scalar(conv[:, half, :], x, w, bdw[:, half:half + 1], ALU.mult, ALU.add)
                    else:
                        dve.scalar_tensor_tensor(out=conv[:, half, :], in0=x, scalar=w, in1=conv[:, half, :],
                                                 op0=ALU.mult, op1=ALU.add)
                i = dve.drain()
                if k == K - 1:
                    i.then_inc(conv_done, 1)

            def stats(src, st, mv, signal, before=()):
                for s, n in before:
                    ge(dve, s, n)
                for t in range(NT):
                    dve.bn_stats(st[:, t, :], src(t))
                dve.drain()
                for t in range(NT):
                    i = dve.bn_aggr(mv[:, t, :], st[:, t, :])
                i.then_inc(signal, 1)

            def norm(dst, src, mv, rs, signal):
                for t in range(NT):
                    i = dve.tensor_scalar(dst(t), src(t), mv[:, t, 0:1], rs[:, t:t + 1], ALU.subtract, ALU.mult)
                i.then_inc(signal, 1)

            def empty(r, name):
                b = r.batch(name)
                bank = psM[:, BANK[name], :]
                kind, n = name[:-1], int(name[-1]) if name[-1].isdigit() else 0
                dve.wait_ge(ready[name], b + 1)
                par = 1 - r.par
                if name.startswith("pw"):
                    oh, sh = int(name[2]), int(name[3])
                    if sh == 0:
                        ge(dve, relu_done, 2 * b)
                    lo, hi = (0, S + 1) if sh == 0 else (S + 1, S_IN)
                    i = dve.tensor_reduce(pooled[:, oh, lo // 2:hi // 2],
                                          bank[0:DH, 0:hi - lo].rearrange("p (s w) -> p s w", w=2), AX.X, ALU.max)
                elif name == "xt1":
                    ge(dve, ready["k2"], b)
                    i = dve.tensor_copy(xnT[:, 1, :], bank[0:DH, 0:S])
                elif name == "x1t1":
                    ge(dve, ready["su2"], b)
                    i = dve.tensor_copy(x1T[:, 1, :], bank[0:DH, 0:S])
                elif name == "ot1":
                    ge(dve, ready["pj2"], b)
                    i = dve.tensor_copy(oT[:, 1, :], bank[0:DH, 0:S])
                elif kind == "k":
                    if n == 0:
                        ge(dve, s_ready, (b - 1) * UNITS)
                    i = dve.tensor_copy(kT[:, par, n, :], bank[:, 0:S])
                elif kind == "v":
                    if n == 0:
                        ge(dve, av_done, (b - 1) * UNITS)
                    i = dve.tensor_copy(va[:, par, n, :, 0:HD], bank[0:TT, 0:D].rearrange("p (h e) -> p h e", e=HD))
                elif kind == "pj":
                    if n == 0:
                        dve.wait_ge(hb_done, b + 1)
                        ge(dve, done["sd2"], b)
                    i = dve.tensor_tensor(h1[:, n, :], bank[0:TT, 0:D], hb[:, par, n, :], ALU.add)
                elif name == "sct":
                    ge(dve, out_x1, 16 * b)
                    i = dve.tensor_copy(xrow[:, :, D:XROW], bank[0:TT, 0:NT * 128].rearrange("p (t e) -> p t e", e=128)[:, :, 0:EXP])
                elif kind == "sg":
                    dve.wait_ge(th_done, 3 * b + n + 1)
                    i = dve.scalar_tensor_tensor(out=ga[:], in0=th[:], scalar=1.0, in1=bank[:, 0:S],
                                                 op0=ALU.add, op1=ALU.mult)
                elif kind == "su":
                    if n == 0:
                        ge(dve, ready["sd2"], b)
                    dve.wait_ge(done[f"sg{n}"], b + 1)
                    i = dve.scalar_tensor_tensor(out=hs[:, n, :], in0=ga[:], scalar=0.5, in1=bank[:, 0:S],
                                                 op0=ALU.mult, op1=ALU.mult)
                else:
                    if n == 0:
                        ge(dve, out_h3, 16 * b)
                    i = dve.tensor_tensor(h2[:, n, :], bank[0:TT, 0:D], h1[:, n, :], ALU.add)
                i.then_inc(done[name], 1)

            def read_o(b):
                dve.wait_ge(av_done, (b + 1) * UNITS)
                ge(dve, on_done, b)
                dve.tensor_copy(oraw[:, 0:2].rearrange("p t h e -> p (t h e)"), psO[0:TT, 0, 0:2 * H * VA])
                dve.tensor_copy(oraw[:, 2].rearrange("p h e -> p (h e)"), psO[0:TT, 1, 0:H * VA])
                dve.drain().then_inc(o_read, 1)
                dve.reciprocal(rsum[:], oraw[:, :, :, HD]).then_inc(o_sum, 1)

            def body(r):
                for s in range(UNITS):
                    for name in ORDER:
                        if r.has(name) and {**POST_SLOT, **PRE_SLOT}[name] == s - 1 and name not in ON_ACT:
                            empty(r, name)
                    at = units(r, s, 0)
                    if at is not None:
                        add_waits(*at)
                        dve.memset(spare[:, s % 6:s % 6 + 1], 0.0)
                        add(*at)
                    if r.post:
                        b = r.b - 1
                        if s == 3:
                            read_o(b)
                        if s == 8:
                            for j in range(3):
                                dve.wait_ge(done[f"pj{j}"], b + 1)
                            stats(lambda t: h1[:, t, :], st3, mv3, st3_done)
                        if s == 9:
                            dve.wait_ge(rs3_done, b + 1)
                            ge(dve, out_x1, 16 * b)
                            norm(lambda t: xrow[:, t, 0:D], lambda t: h1[:, t, :], mv3, rs3, x1_done)
                        if s == 14:
                            dve.wait_ge(done["gate"], b + 1)
                            ge(dve, out_st, 16 * b)
                            dve.tensor_scalar(esc1[:], esc[:], 1.0, None, ALU.add)
                            dve.drain()
                            dve.reciprocal(sc[0:EXP, :], esc1[:]).then_inc(sc_done, 1)
                    if r.pre:
                        b = r.b + 1
                        if 5 <= s < 5 + 2 * K and s % 2 == 1:
                            tap(b, (s - 5) // 2)
                        if s == 28:
                            for j in range(3):
                                dve.wait_ge(done[f"dfb{j}"], b + 1)
                            ge(dve, rs1_done, b)
                            stats(lambda t: y[:, t, :], st1, mv1, st1_done)
                        if s == 29:
                            dve.wait_ge(rs1_done, b + 1)
                            ge(dve, h_done, b)
                            norm(lambda t: yn[:, t, :], lambda t: y[:, t, :], mv1, rs1, yn_done)
                        if s == 30:
                            dve.wait_ge(h_done, b + 1)
                            stats(lambda t: h[:, t, :], st2, mv2, st2_done)
                            dve.wait_ge(rs2_done, b + 1)
                            ge(dve, hb_done, b + 1)
                            ge(dve, ready["xt1"], b)
                            norm(lambda t: xn[:, t, :], lambda t: h[:, t, :], mv2, rs2, xn_done)
                for name in ORDER:
                    if r.has(name) and {**POST_SLOT, **PRE_SLOT}[name] == UNITS - 1 and name not in ON_ACT:
                        empty(r, name)
            run(dve, body)
        blocks.close()
        clear(nc, sems)





CAP = B * S * 2 // EXP
NC8 = 128 // EXP
CH = B * S // NC8
TC = CH // TT
LO = 32
HI = -(-CAP // LO)
SLOTS = HI * LO
NJ = CAP // TT
NONE = 9999.0
TOP_BIT = 29


def phase2(nc, d, gidx, psS, psT, psO, psM):
    with ExitStack() as ctx:
        def sb(name, shape, dt=F32):
            return ctx.enter_context(nc.sbuf_tensor(name, shape, dt))

        sems = []

        def sem(name):
            sems.append(ctx.enter_context(nc.semaphore(name)))
            return sems[-1]

        sco = sb("sco", [128, CH])
        junk = sb("junk", [128, CH], BF16)
        blk = sb("blk", [128, 128])
        ltri = sb("ltri", [128, 128])
        ident2 = sb("ident2", [128, 128])
        tabA = sb("tabA", [TT, TC, NC8])
        tabB = sb("tabB", [TT, TC, NC8])
        ihi = sb("ihi", [TT, HI], BF16)
        ilo = sb("ilo", [TT, LO], BF16)
        cur = sb("cur", [128, 1], I32)
        cand = sb("cand", [128, 1], I32)
        bit = sb("bit", [128, 1], I32)
        bitf = sb("bitf", [128, 1])
        take = sb("take", [128, 1], I32)
        cnt = sb("cnt", [128, 1])
        gt = sb("gt", [128, CH])
        eq = sb("eq", [128, CH])
        eqs = sb("eqs", [128, CH])
        cols = sb("cols", [128, 2])
        thr = sb("thr", [128, 1])
        sel = sb("sel", [128, CH])
        rank = sb("rank", [128, CH])
        off = sb("off", [128, 1])
        slot = sb("slot", [128, CH], I32)
        shi = sb("shi", [128, CH], I32)
        slo = sb("slo", [128, CH], I32)
        shif = sb("shif", [128, CH])
        slof = sb("slof", [128, CH])
        posT = sb("posT", [TT, 2, TC, 128], BF16)
        zer = sb("zer", [TT, 512], BF16)
        ohh = sb("ohh", [TT, 2, 128, HI], BF16)
        ohl = sb("ohl", [TT, 2, 128, LO], BF16)
        vals = sb("vals", [TT, 2, 128, 2, LO], BF16)
        lst = sb("lst_sb", [HI, EXP, LO], I32)
        listA = sb("listA", [HI, EXP, LO])

        ld, pool_set, cnt_done, tot_done = sem("ld2"), sem("pool_set"), sem("cnt_done"), sem("tot_done")
        cols_done, sums_done, rank_done, off_done = sem("cols_done"), sem("sums_done"), sem("rank_done"), sem("off_done")
        slot_done, turned, pos_done = sem("slot_done"), sem("turned2"), sem("pos_done")
        hot_done, valB_done, valA_done, list_acc, list_done = sem("hot_done"), sem("valB_done"), sem("valA_done"), sem("list_acc"), sem("list_done")
        lst_out, idx_in, dve_set = sem("lst_out"), sem("idx_in"), sem("dve_set")
        blocks = ctx.enter_context(ExitStack())
        block = blocks.enter_context(nc.Block())

        @block.sync
        def _(sp):
            sp.dma_start(sco[:], d["st"].rearrange("e b s -> e (b s)").rearrange("e (c j) -> (e c) j", c=NC8)).then_inc(ld, 16)
            for t, name in ((blk, "blk"), (ltri, "ltri"), (ident2, "idn"), (tabA, "tabA"), (tabB, "tabB")):
                sp.dma_start(t[:], d[name]).then_inc(ld, 16)
            sp.wait_ge(list_done, 1)
            sp.dma_start(d["lst"].rearrange("e (h l) -> h e l", l=LO), lst[:]).then_inc(lst_out, 16)
            sp.wait_ge(lst_out, 16)
            sp.dma_start(gidx[:], d["lst"][:, 0:CAP].rearrange("e (p j) -> p e j", p=TT)).then_inc(idx_in, 16)
            sp.wait_ge(idx_in, 16)

        @block.gpsimd
        def _(pool):
            pool.iota(ihi[:], [[1, HI]], base=0, channel_multiplier=0, allow_small_or_imprecise_dtypes=True)
            pool.iota(ilo[:], [[1, LO]], base=0, channel_multiplier=0, allow_small_or_imprecise_dtypes=True)
            pool.memset(zer[:], 0.0)
            pool.drain().then_inc(pool_set, 1)
            pool.wait_ge(ld, 16 * 6)
            for t in range(TC):
                pool.wait_ge(hot_done, t + 1)
                ge(pool, list_acc, t - 1)
                for c in range(NC8):
                    i = pool.tensor_tensor(
                        vals[:, t % 2].rearrange("p (e c) v l -> p e c v l", c=NC8)[:, :, c, 0, :],
                        ohl[:, t % 2].rearrange("p (e c) l -> p e c l", c=NC8)[:, :, c, :],
                        tabA[:, t, c:c + 1].unsqueeze(2).broadcast_to([TT, EXP, LO]), ALU.mult)
                i.then_inc(valA_done, 1)

        @block.tensor
        def _(pe):
            pe.wait_ge(ld, 16 * 6)
            with pe.Fori(0, TOP_BIT + 1) as i:
                pe.wait_ge(cnt_done, i + 1)
                pe.matmul(psM[:, 0, 0:1], blk[:], cnt[:], start=True, stop=True).then_inc(tot_done, 1)
            pe.wait_ge(cols_done, 1)
            pe.matmul(psM[:, 1, 0:1], blk[:], cols[:, 0:1], start=True, stop=True)
            pe.matmul(psM[:, 1, 1:2], ltri[:], cols[:, 1:2], start=True, stop=True).then_inc(sums_done, 1)
            pe.wait_ge(rank_done, 1)
            pe.matmul(psM[:, 1, 2:3], ltri[:], rank[:, CH - 1:CH], start=True, stop=True).then_inc(off_done, 1)
            pe.wait_ge(slot_done, 1)
            pe.wait_ge(pool_set, 1)
            for n in range(2):
                pe.matmul(psO[0:HI, n, :], zer[:, 0:HI], zer[:, :], start=True, stop=False, skip_group_check=True)
            for t in range(TC):
                ge(pe, pos_done, t - 1)
                pe.transpose(psS[0:TT, t % 2, 0:128], shif[:, t * TT:(t + 1) * TT], ident2[:])
                pe.transpose(psS[0:TT, t % 2, 128:256], slof[:, t * TT:(t + 1) * TT], ident2[:]).then_inc(turned, 1)
            for t in range(TC):
                pe.wait_ge(valB_done, t + 1)
                pe.wait_ge(valA_done, t + 1)
                for e in range(EXP):
                    for c in range(NC8):
                        mm = pe.matmul(psO[0:HI, e // 8, (e % 8) * 2 * LO:(e % 8 + 1) * 2 * LO], ohh[:, t % 2, e * NC8 + c, :],
                                       vals[:, t % 2, e * NC8 + c].rearrange("p v l -> p (v l)"),
                                       start=False, stop=(t == TC - 1 and c == NC8 - 1), skip_group_check=True)
                mm.then_inc(list_acc, 1)

        @block.vector
        def _(dve):
            dve.wait_ge(ld, 16 * 6)
            dve.memset(cur[:], 0)
            dve.memset(bit[:], 1 << TOP_BIT)
            dve.memset(cand[:], 1 << TOP_BIT)
            dve.memset(bitf[:], float(1 << TOP_BIT))
            dve.drain()
            with dve.Fori(0, TOP_BIT + 1) as i:
                dve.tensor_scalar(junk[:], sco[:], cand[:].bitcast(F32), None, ALU.is_ge, ALU.add, accum_out=cnt[:])
                dve.drain().then_inc(cnt_done, 1)
                dve.tensor_scalar(bit[:], bit[:], 1, None, ALU.logical_shift_right)
                dve.wait_ge(tot_done, i + 1)
                dve.tensor_scalar(take[:], psM[:, 0, 0:1], float(CAP), bitf[:], ALU.is_ge, ALU.mult)
                dve.drain()
                dve.tensor_tensor(cur[:], cur[:], take[:], ALU.bitwise_or)
                dve.tensor_scalar(bitf[:], bitf[:], 0.5, None, ALU.mult)
                dve.drain()
                dve.tensor_tensor(cand[:], cur[:], bit[:], ALU.bitwise_or)
                dve.drain()
            dve.tensor_scalar(gt[:], sco[:], cur[:].bitcast(F32), None, ALU.is_gt, ALU.add, accum_out=cols[:, 0:1])
            dve.tensor_scalar(eq[:], sco[:], cur[:].bitcast(F32), None, ALU.is_equal)
            dve.drain()
            dve.tensor_tensor_scan(eqs[:], eq[:], eq[:], 0.0, ALU.add, ALU.max)
            dve.drain()
            dve.tensor_copy(cols[:, 1:2], eqs[:, CH - 1:CH]).then_inc(cols_done, 1)
            dve.wait_ge(sums_done, 1)
            dve.tensor_scalar(thr[:], psM[:, 1, 0:1], -1.0, float(CAP), ALU.mult, ALU.add)
            dve.drain()
            dve.tensor_tensor(thr[:], thr[:], psM[:, 1, 1:2], ALU.subtract)
            dve.drain()
            dve.scalar_tensor_tensor(out=sel[:], in0=eqs[:], scalar=thr[:], in1=eq[:], op0=ALU.is_le, op1=ALU.mult)
            dve.drain()
            dve.tensor_tensor(sel[:], sel[:], gt[:], ALU.add)
            dve.drain()
            dve.tensor_tensor_scan(rank[:], sel[:], sel[:], 0.0, ALU.add, ALU.max).then_inc(rank_done, 1)
            dve.wait_ge(off_done, 1)
            dve.tensor_scalar(off[:], psM[:, 1, 2:3], -1.0 - NONE, None, ALU.add)
            dve.drain()
            dve.scalar_tensor_tensor(out=rank[:], in0=rank[:], scalar=off[:], in1=sel[:], op0=ALU.add, op1=ALU.mult)
            dve.drain()
            dve.tensor_scalar(slot[:], rank[:], NONE, None, ALU.add)
            dve.drain()
            dve.tensor_scalar(shi[:], slot[:], LO.bit_length() - 1, None, ALU.logical_shift_right)
            dve.tensor_scalar(slo[:], slot[:], LO - 1, None, ALU.bitwise_and)
            dve.drain()
            dve.tensor_copy(shif[:], shi[:])
            dve.tensor_copy(slof[:], slo[:])
            dve.drain().then_inc(slot_done, 1)
            for t in range(TC):
                dve.wait_ge(turned, t + 1)
                dve.tensor_copy(posT[:, :, t, :], psS[0:TT, t % 2, 0:256].rearrange("p (v n) -> p v n", v=2)).then_inc(pos_done, 1)
            dve.wait_ge(pool_set, 1)
            dve.wait_ge(pos_done, TC)

            def hot(t, which, iota, n, out):
                return dve.tensor_tensor(out, posT[:, which, t, :].unsqueeze(2).broadcast_to([TT, 128, n]),
                                         iota.unsqueeze(1).broadcast_to([TT, 128, n]), ALU.is_equal)

            for t in range(TC):
                ge(dve, valA_done, t - 1)
                hot(t, 1, ilo[:], LO, ohl[:, t % 2]).then_inc(hot_done, 1)
                ge(dve, list_acc, t - 1)
                hot(t, 0, ihi[:], HI, ohh[:, t % 2])
                dve.wait_ge(hot_done, t + 1)
                dve.tensor_tensor(
                    vals[:, t % 2].rearrange("p (e c) v l -> p e c v l", c=NC8)[:, :, :, 1, :],
                    ohl[:, t % 2].rearrange("p (e c) l -> p e c l", c=NC8),
                    tabB[:, t, :].unsqueeze(1).unsqueeze(3).broadcast_to([TT, EXP, NC8, LO]), ALU.mult)
                dve.drain().then_inc(valB_done, 1)
            dve.wait_ge(list_acc, TC)
            acc = psO[0:HI, :, :].rearrange("p n (e v l) -> p (n e) v l", v=2, l=LO)
            dve.tensor_scalar(listA[:], acc[:, :, 0, :], 128.0, None, ALU.mult)
            dve.drain()
            dve.tensor_tensor(lst[:], listA[:], acc[:, :, 1, :], ALU.add).then_inc(list_done, 1)
        blocks.close()
        clear(nc, sems)


F = 768
NF = F // 128
NH = 2
HT = CAP // NH
JH = NJ // NH


def phase3(nc, d, gidx, wi, wo, w_in, psS, psT, psO, psM):
    with ExitStack() as ctx:
        def sb(name, shape, dt=F32):
            return ctx.enter_context(nc.sbuf_tensor(name, shape, dt))

        sems = []

        def sem(name):
            sems.append(ctx.enter_context(nc.semaphore(name)))
            return sems[-1]

        ident3 = sb("ident3", [128, 128])
        wg = sb("wg_sb", [DH, 2, 2, F])
        wu = sb("wu_sb", [DH, 2, 2, F])
        wd = sb("wd_sb", [128, 2, NF, D])
        idx = sb("idx", [TT, 2, NJ], I32)
        xg = sb("xg", [TT, 2, NJ, XROW])
        spare = sb("spare3", [TT, 6, 2])
        scr = sb("scr", [TT, 2, NJ])
        xgT = sb("xgT", [DH, 2, CAP])
        sg = sb("sg_sb", [128, 2, HT])
        hid = sb("hid", [128, NF, CAP])
        yo = sb("yo", [TT, 2, NJ, D])

        ldi, ldw = sem("ldi"), [sem("ldw0"), sem("ldw1")]
        idx_done, scr_done, added = sem("idx_done"), sem("scr_done"), sem("added3")
        gathered = [sem("gathered0"), sem("gathered1")]
        xt_ready, xt_done = sem("xt_ready"), sem("xt_done")
        g_ready, sg_done, hid_done = sem("g_ready"), sem("sg_done"), sem("hid_done")
        y_ready, y_done = sem("y_ready"), sem("y_done")
        NX = 2 * NH
        NP = NF * NH
        blocks = ctx.enter_context(ExitStack())
        block = blocks.enter_context(nc.Block())

        @block.sync
        def _(sp):
            sp.dma_start(ident3[:], d["idn"]).then_inc(ldi, 16)

            def load(e, par):
                sp.dma_start(wg[:, par], d["wg"][e]).then_inc(ldw[par], 16)
                sp.dma_start(wu[:, par], d["wu"][e]).then_inc(ldw[par], 16)
                sp.dma_start(wd[:, par], d["wd"][e]).then_inc(ldw[par], 16)

            load(0, 0)
            load(1, 1)
            with sp.Fori(1, EXP // 2) as i:
                for par in range(2):
                    sp.wait_ge(y_ready, (i * 2 + par - 1) * NJ)
                    load(i * 2 + par, par)
            sp.dma_start(wi[:], d["wi"]).then_inc(w_in, 16)
            sp.dma_start(wo[:], d["wo"]).then_inc(w_in, 16)

        @block.gpsimd
        def _(pool):
            def held(n):
                pool.tensor_tensor(spare[:, n, 1:2], spare[:, n, 0:1], spare[:, n, 0:1], ALU.add)

            pool.memset(spare[:], 0.0)

            def fetch(pair, par):
                e = pair * 2 + par
                """Copy expert e's indices to a fixed place and gather its rows."""
                ge(pool, gathered[par], pair * 16 * NJ)
                pool.tensor_copy(idx[:, par, :], gidx[:, e, :]).then_inc(idx_done, 1)
                pool.wait_ge(idx_done, e + 1)
                ge(pool, xt_done, (e - 1) * NX)
                held(par)
                for j in range(NJ):
                    pool.indirect_dma_start(out=xg[:, par, j, :], out_offset=None,
                                            in_=d["x1"].rearrange("b s c -> (b s) c"),
                                            in_offset=bass.IndirectOffsetOnAxis(ap=idx[:, par, j:j + 1], axis=0)
                                            ).then_inc(gathered[par], 16)

            def scores(pair, par):
                e = pair * 2 + par
                """The scores, for expert e's column of the gathered rows."""
                pool.wait_ge(gathered[par], (pair + 1) * 16 * NJ)
                ge(pool, y_done, (e - 1) * NJ)
                pool.tensor_copy(scr[:, par, :], xg[:, par, :, bass.ds(D + e, 1)].rearrange("p j o -> p (j o)")).then_inc(scr_done, 1)

            def scatter(e, par):
                for j in range(NJ):
                    if j % JH == 0:
                        pool.wait_ge(y_done, e * NJ + j + JH)
                        ge(pool, added, e * NJ * 16)
                        held(2 + 2 * par + j // JH)
                    pool.indirect_dma_start(out=d["h3"].rearrange("b s c -> (b s) c"),
                                            out_offset=bass.IndirectOffsetOnAxis(ap=idx[:, par, j:j + 1], axis=0),
                                            in_=yo[:, par, j, :], in_offset=None, compute_op=ALU.add
                                            ).then_inc(added, 16)

            def pair(i, more):
                for par in range(2):
                    e = i * 2 + par
                    scores(i, par)
                    scatter(e, par)
                    if more:
                        pool.wait_ge(added, (e + 1) * NJ * 16)
                        fetch(i + 1, par)

            fetch(0, 0)
            fetch(0, 1)
            pair(0, True)
            with pool.Fori(1, EXP // 2 - 1) as i:
                pair(i, True)
            pair(EXP // 2 - 1, False)
            pool.wait_ge(added, EXP * NJ * 16)

        @block.tensor
        def _(pe):
            pe.wait_ge(ldi, 16)

            def turn(pair, par):
                e = pair * 2 + par
                """Gathered rows to channels by tokens."""
                pe.wait_ge(gathered[par], (pair + 1) * 16 * NJ)
                for nh in range(NH):
                    for half in range(2):
                        n = e * NX + nh * 2 + half
                        ge(pe, xt_done, n - 1)
                        for j in range(JH):
                            mm = pe.transpose(psO[0:DH, half, j * TT:(j + 1) * TT],
                                              xg[:, par, nh * JH + j, half * DH:(half + 1) * DH], ident3[0:TT, 0:TT])
                        mm.then_inc(xt_ready, 1)

            def expert(pair, par):
                e = pair * 2 + par
                pe.wait_ge(xt_done, (e + 1) * NX)
                pe.wait_ge(ldw[par], (pair + 1) * 48)
                for nh in range(NH):
                    for f in range(NF):
                        n = e * NP + nh * NF + f
                        k = (nh * NF + f) % 2
                        ge(pe, sg_done, n - 1)
                        for half in range(2):
                            pe.matmul(psS[:, k, 0:HT], wg[:, par, half, f * 128:(f + 1) * 128],
                                      xgT[:, half, nh * HT:(nh + 1) * HT], start=(half == 0), stop=(half == 1))
                        ge(pe, hid_done, n - 1)
                        for half in range(2):
                            mm = pe.matmul(psT[:, k, 0:HT], wu[:, par, half, f * 128:(f + 1) * 128],
                                           xgT[:, half, nh * HT:(nh + 1) * HT], start=(half == 0), stop=(half == 1))
                        mm.then_inc(g_ready, 1)

            def down(e, par):
                for j in range(NJ):
                    n = e * NJ + j
                    if j == 0:
                        pe.wait_ge(hid_done, e * NP + NF)
                    if j == JH:
                        pe.wait_ge(hid_done, (e + 1) * NP)
                    ge(pe, y_done, n - 1)
                    for f in range(NF):
                        mm = pe.matmul(psM[0:TT, j % 2, 0:D], hid[:, f, j * TT:(j + 1) * TT], wd[:, par, f, :],
                                       start=(f == 0), stop=(f == NF - 1))
                    mm.then_inc(y_ready, 1)

            def pair(i, more):
                expert(i, 0)
                turn(i, 1)
                down(i * 2, 0)
                expert(i, 1)
                if more:
                    turn(i + 1, 0)
                down(i * 2 + 1, 1)

            turn(0, 0)
            pair(0, True)
            with pe.Fori(1, EXP // 2 - 1) as i:
                pair(i, True)
            pair(EXP // 2 - 1, False)

        @block.scalar
        def _(act):
            def gates(e):
                for n in range(NP):
                    act.wait_ge(g_ready, e * NP + n + 1)
                    ge(act, hid_done, e * NP + max(n - 1, 0))
                    act.activation(sg[:, n % 2, :], psS[:, n % 2, 0:HT], ACT.Silu).then_inc(sg_done, 1)

            gates(0)
            with act.Fori(1, EXP) as e:
                gates(e)

        @block.vector
        def _(dve):
            def xt_copies(e):
                for n in range(NX):
                    nh, half = divmod(n, 2)
                    dve.wait_ge(xt_ready, e * NX + n + 1)
                    if n == 0:
                        ge(dve, g_ready, e * NP)
                    dve.tensor_copy(xgT[:, half, nh * HT:(nh + 1) * HT], psO[0:DH, half, 0:HT]).then_inc(xt_done, 1)

            def hidden(e):
                for n in range(NP):
                    nh, f = divmod(n, NF)
                    dve.wait_ge(sg_done, e * NP + n + 1)
                    if n == 0:
                        ge(dve, y_ready, e * NJ)
                    dve.tensor_tensor(hid[:, f, nh * HT:(nh + 1) * HT], sg[:, n % 2, :], psT[:, n % 2, 0:HT],
                                      ALU.mult).then_inc(hid_done, 1)

            def outs(e, par):
                dve.wait_ge(scr_done, e + 1)
                for j in range(NJ):
                    dve.wait_ge(y_ready, e * NJ + j + 1)
                    if j == 0:
                        ge(dve, added, (e - 1) * NJ * 16)
                    dve.tensor_scalar(yo[:, par, j, :], psM[0:TT, j % 2, 0:D], scr[:, par, j:j + 1], None,
                                      ALU.mult).then_inc(y_done, 1)

            def pair(i, more):
                hidden(i * 2)
                xt_copies(i * 2 + 1)
                outs(i * 2, 0)
                hidden(i * 2 + 1)
                if more:
                    xt_copies(i * 2 + 2)
                outs(i * 2 + 1, 1)

            xt_copies(0)
            pair(0, True)
            with dve.Fori(1, EXP // 2 - 1) as i:
                pair(i, True)
            pair(EXP // 2 - 1, False)
        blocks.close()
        clear(nc, sems)


S8 = 8
TL = -(-S // S8)
NR = 8
ROW = XS_W
C_H, C_P, C_V = D, 2 * D, 2 * D + 1
VEPS = 1e-12


def phase4(nc, d, rows, hot8, psS, psT, psO, psM):
    with ExitStack() as ctx:
        def sb(name, shape, dt=F32):
            return ctx.enter_context(nc.sbuf_tensor(name, shape, dt))

        sems = []

        def sem(name):
            sems.append(ctx.enter_context(nc.semaphore(name)))
            return sems[-1]

        ident = sb("ident4", [128, 128])
        wq1 = sb("wq1_sb", [DH, 2, D])
        wkv = sb("wkv_sb", [DH, 2, 2 * D])
        wp1 = sb("wp1_sb", [DH, 2, D])
        bp1 = sb("bp1_sb", [128, D])
        wr = sb("wr_sb", [DH, 2, NR])
        mask = sb("mask_sb", [128, 128])
        place = sb("place_sb", [128, TL])
        mh = sb("mh4", [128, H])
        ep = sb("ep4", [128, 1])
        hin = sb("hin", [128, 2, D])
        hb1 = sb("hb1", [128, 4, D])
        sta, mva, rsa = sb("sta", [128, 6]), sb("mva", [128, 2]), sb("rsa", [128, 1])
        xn2 = sb("xn2", [128, D])
        xT = sb("xT4", [DH, 2, 128])
        xq = sb("xq", [DH, 2, 128])
        ksb = sb("ksb", [128, D])
        va = sb("va4", [128, 4, H, 32])
        prod = sb("prod", [128, D])
        s0 = sb("s0", [128, 128])
        sq = sb("sq", [128, D])
        ss = sb("ss", [128, H])
        ssm = sb("ssm", [128, H])
        rn = sb("rn", [128, H])
        vnp = sb("vnp", [128, H, 32])
        vnT = sb("vnT", [128, NG, 128])
        m0 = sb("m0", [H, S8])
        d0 = sb("d0", [H, 128])
        e0 = sb("e0", [128, 128])
        PT = sb("PT", [128, 2, 4, NG, 128])
        oraw = sb("oraw4", [128, NG * 128])
        rs = sb("rs4", [128, H])
        on = sb("on4", [128, D])
        oT = sb("oT4", [DH, 2, 128])
        stc, mvc, rsc = sb("stc", [128, 6]), sb("mvc", [128, 2]), sb("rsc", [128, 1])
        row = sb("row4", [128, 4, ROW])
        x3T = sb("x3T", [DH, 2, 128])
        nlm = sb("nlm", [128, 1])
        er = sb("er", [128, NR])
        es = sb("es", [128, 1])
        eqm = sb("eqm", [128, NR])
        cum = sb("cum", [128, NR])

        names = ["xt", "kv", "q0", "vt", "sc", "et", "av", "back", "ot", "pj", "x3", "lg"]
        ready = {n: sem(f"{n}_rdy4") for n in names}
        ld, pool_set = sem("ld4"), sem("pool_set4")
        h_in, row_out = ([sem(f"{n}{slot}") for slot in range(k)] for n, k in (("h_in", 2), ("row_out", 4)))
        sta_d, rsa_d, xn_d, hb_d = sem("sta_d"), sem("rsa_d"), sem("xn_d"), sem("hb_d")
        xT_d, k_d, v_d, s0_d, sq_d, ss_d, vnp_d = (sem(n) for n in ("xT_d", "k_d", "v_d", "s0_d", "sq_d", "ss_d", "vnp_d"))
        vt_d, d0_d, e0_d, exp_d, mask_p, mask_v, pt_d = (sem(n) for n in ("vt_d", "d0_d", "e0_d", "exp_d", "mask_p", "mask_v", "pt_d"))
        oraw_d, on_d, oT_d, h4_d, stc_d, rsc_d, row_d = (sem(n) for n in ("oraw_d", "on_d", "oT_d", "h4_d", "stc_d", "rsc_d", "row_d"))
        x3_d, lg_m, lg_e, p_d, pl_d = (sem(n) for n in ("x3_d", "lg_m", "lg_e", "p_d", "pl_d"))

        O0, O1, M0, M1 = psO[:, 0, :], psO[:, 1, :], psM[:, 0, :], psM[:, 1, :]
        CONSTS = [(ident, "idn"), (wq1, "wq1"), (wkv, "wkv"), (wp1, "wp1"), (bp1, "bp1"), (wr, "wr"), (mask, "mask"), (place, "place")]

        def run(eng, step):
            for i in range(7):
                step(i, i % 4, True, i >= 1, i >= 2, i >= 3, i >= 4)
            with eng.Fori(0, (TL - 7) // 4) as k:
                for r in range(4):
                    step(k * 4 + 7 + r, (3 + r) % 4, True, True, True, True, True)
            for i in range(TL, TL + 4):
                step(i, i % 4, False, i <= TL, i <= TL + 1, i <= TL + 2, True)

        blocks = ctx.enter_context(ExitStack())
        block = blocks.enter_context(nc.Block())

        @block.sync
        def _(sp):
            def load(i, r):
                sp.dma_start(hin[:, r % 2, :], d["h3"][:, bass.ds(i * S8, S8), :]).then_inc(h_in[r % 2], 16)

            def store(j, q):
                sp.wait_ge(p_d, j + 1)
                sp.wait_ge(pl_d, j + 1)
                sp.dma_start(rows[:, j, :], row[:, q, :]).then_inc(row_out[q], 16)

            for t, name in CONSTS:
                sp.dma_start(t[:], d[name]).then_inc(ld, 16)
            load(0, 0)

            def step(i, r, a, b, e, c, dd):
                if a:
                    ge(sp, hb_d, i)
                    ge(sp, xn_d, i)
                    load(i + 1, (r + 1) % 4)
                if not isinstance(i, int) or i >= 6:
                    store(i - 6, (r + 2) % 4)
            run(sp, step)
            for j in range(TL - 2, TL):
                store(j, j % 4)
            for q in range(4):
                sp.wait_ge(row_out[q], 16 * len(range(q, TL, 4)))

        @block.gpsimd
        def _(pool):
            pool.memset(mh[:], -0.5)
            pool.memset(ep[:], EPS)
            pool.memset(va[:], 0.0)
            pool.drain()
            pool.memset(va[:, :, :, HD:VA], 1.0)
            pool.memset(vnp[:], 0.0)
            pool.memset(s0[:], 0.0)
            pool.memset(e0[:], 0.0)
            pool.memset(row[:], 0.0)
            pool.drain().then_inc(pool_set, 1)
            pool.wait_ge(ld, 16 * len(CONSTS))

            def rstd(var, out):
                pool.tensor_tensor(out, var, ep[:], ALU.add)
                pool.drain()
                return pool.tensor_tensor(out, out, mh[:, 0:1], ALU.pow)

            def first(i):
                pool.wait_ge(sta_d, i + 1)
                rstd(mva[:, 1:2], rsa[:]).then_inc(rsa_d, 1)

            first(0)

            def step(i, r, a, b, e, c, dd):
                if e:
                    j, p = i - 2, r % 2
                    pool.wait_ge(exp_d, 2 * j + 1)
                    pool.tensor_tensor(PT[:, p, 0:2].rearrange("p r g n -> p (r g) n"), PT[:, p, 0:2].rearrange("p r g n -> p (r g) n"),
                                       mask[:].unsqueeze(1).broadcast_to([128, 2 * NG, 128]), ALU.mult).then_inc(mask_p, 1)
                if a:
                    first(i + 1)
                    pool.wait_ge(xn_d, i + 1)
                    ge(pool, h4_d, i - 3)
                    pool.tensor_tensor(hb1[:, r, :], hin[:, r % 2, :], bp1[:], ALU.add).then_inc(hb_d, 1)
                if dd:
                    j = i - 4
                    pool.tensor_copy(row[:, r, C_V:C_V + 1], place[:, bass.ds(j, 1)]).then_inc(pl_d, 1)
                if a:
                    pool.wait_ge(v_d, i + 1)
                    pool.tensor_tensor(sq[:].rearrange("p (h e) -> p h e", e=HD), va[:, r, :, 0:HD], va[:, r, :, 0:HD], ALU.mult).then_inc(sq_d, 1)
                    pool.wait_ge(ss_d, i + 1)
                    pool.tensor_tensor(rn[:], ssm[:], mh[:], ALU.pow)
                    pool.drain()
                    ge(pool, ready["vt"], i)
                    pool.tensor_tensor(vnp[:, :, 0:HD], va[:, r, :, 0:HD], rn[:].unsqueeze(2).broadcast_to([128, H, HD]),
                                       ALU.mult).then_inc(vnp_d, 1)
                if c:
                    pool.wait_ge(stc_d, i - 3 + 1)
                    rstd(mvc[:, 1:2], rsc[:]).then_inc(rsc_d, 1)
            run(pool, step)

        @block.tensor
        def _(pe):
            pe.wait_ge(ld, 16 * len(CONSTS))
            pe.wait_ge(pool_set, 1)

            def two(out, lhs, rhs):
                pe.matmul(out, lhs(0), rhs(0), start=True, stop=False)
                return pe.matmul(out, lhs(1), rhs(1), start=False, stop=True)

            def turn2(out, src):
                pe.transpose(out[0:DH, 0:128], src[:, 0:DH], ident[:])
                return pe.transpose(out[0:DH, 128:256], src[:, DH:D], ident[:])

            def cosines(ps, quads):
                for g in range(NG):
                    for q in quads:
                        v = vnT[32 * q:32 * q + HD, g, :]
                        mm = pe.matmul(ps[:, q % 2, g * 128:(g + 1) * 128], v, v, start=True, stop=True)
                mm.then_inc(ready["sc"], 1)

            def step(i, r, a, b, e, c, dd):
                if c:
                    j, q, p = i - 3, (r + 1) % 4, (r + 1) % 2
                    pe.wait_ge(pt_d, j + 1)
                    ge(pe, h4_d, j)
                    for h in range(H):
                        g, quad = divmod(h, 4)
                        mm = pe.matmul(O0[32 * quad:32 * quad + 32, g * 128:(g + 1) * 128], va[:, q, h, :], PT[:, p, quad, g, :],
                                       start=True, stop=True)
                    mm.then_inc(ready["av"], 1)
                if dd:
                    pe.wait_ge(row_d, i - 4 + 1)
                    ge(pe, x3_d, i - 4)
                    pe.wait_ge(v_d, min(i, TL) if isinstance(i, int) else i)
                    pe.wait_ge(k_d, min(i, TL) if isinstance(i, int) else i)
                    turn2(M0[:, 256:512], row[:, r, :]).then_inc(ready["x3"], 1)
                if a:
                    pe.wait_ge(xn_d, i + 1)
                    ge(pe, v_d, i)
                    ge(pe, k_d, i)
                    turn2(M0, xn2).then_inc(ready["xt"], 1)
                if b:
                    j = i - 1
                    pe.wait_ge(vnp_d, j + 1)
                    pe.wait_ge(s0_d, j + 1)
                    ge(pe, lg_e, i - 4)
                    ge(pe, lg_m, i - 4)
                    for g in range(NG):
                        pe.transpose(O1[:, g * 128:(g + 1) * 128], vnp[:, 4 * g:4 * g + 4, :].rearrange("p h e -> p (h e)"), ident[:])
                    pe.transpose(O1[:, 384:512], s0[:], ident[:]).then_inc(ready["vt"], 1)
                if c:
                    pe.wait_ge(oraw_d, i - 3 + 1)
                    for g in range(NG):
                        mm = pe.transpose(O0[:, g * 128:(g + 1) * 128], oraw[:, g * 128:(g + 1) * 128], ident[:])
                    mm.then_inc(ready["back"], 1)
                if a:
                    pe.wait_ge(xT_d, i + 1)
                    ge(pe, x3_d, i - 4 + 1)
                    two(M0[:, 0:2 * D], lambda k: xT[:, k, :], lambda k: wkv[:, k, :]).then_inc(ready["kv"], 1)
                    ge(pe, pt_d, i - 1)
                    two(M1[:, 0:D], lambda k: xq[:, k, :], lambda k: wq1[:, k, :]).then_inc(ready["q0"], 1)
                if c:
                    pe.wait_ge(on_d, i - 3 + 1)
                    turn2(O0, on).then_inc(ready["ot"], 1)
                if dd:
                    pe.wait_ge(x3_d, i - 4 + 1)
                    if b:
                        pe.wait_ge(d0_d, i - 1 + 1)
                    else:
                        pe.wait_ge(lg_m, i - 4)
                        pe.wait_ge(lg_e, i - 4)
                    two(O1[:, 0:NR], lambda k: x3T[:, k, :], lambda k: wr[:, k, :]).then_inc(ready["lg"], 1)
                if b:
                    pe.wait_ge(vt_d, i - 1 + 1)
                    ge(pe, exp_d, 2 * (i - 1))
                    cosines(psS, (0, 1))
                if c:
                    pe.wait_ge(oT_d, i - 3 + 1)
                    two(O0[:, 0:D], lambda k: oT[:, k, :], lambda k: wp1[:, k, :]).then_inc(ready["pj"], 1)
                if b:
                    cosines(psT, (2, 3))
                    pe.wait_ge(e0_d, i - 1 + 1)
                    if a:
                        pe.wait_ge(s0_d, i + 1)
                    pe.transpose(M1[:, 0:128], e0[:], ident[:]).then_inc(ready["et"], 1)
            run(pe, step)

        @block.scalar
        def _(act):
            def step(i, r, a, b, e, c, dd):
                if e:
                    j = i - 2
                    ge(act, ready["av"], i - 3)
                    for n, ps in ((0, psS), (1, psT)):
                        act.wait_ge(ready["sc"], 2 * j + n + 1)
                        act.activation(PT[:, r % 2, 2 * n:2 * n + 2].rearrange("p r g n -> p r (g n)"), ps[:, :, 0:NG * 128],
                                       ACT.Exp, scale=SCALE).then_inc(exp_d, 1)
                if c:
                    act.wait_ge(ready["av"], i - 3 + 1)
                    ge(act, ready["back"], i - 3)
                    act.copy(oraw[:], O0[:, 0:NG * 128]).then_inc(oraw_d, 1)
                if a:
                    act.wait_ge(ready["xt"], i + 1)
                    ge(act, ready["q0"], i)
                    act.copy(xT[:].rearrange("p k n -> p (k n)"), M0[0:DH, 0:256])
                    act.copy(xq[:].rearrange("p k (b s) -> p k b s", s=S8),
                             M0[0:DH, 0:256].rearrange("p (k n) -> p k n", k=2)[:, :, 0:S8].unsqueeze(2).broadcast_to([DH, 2, B, S8]))
                    act.drain().then_inc(xT_d, 1)
                if dd:
                    act.wait_ge(ready["x3"], i - 4 + 1)
                    ge(act, ready["lg"], i - 4)
                    act.copy(x3T[:].rearrange("p k n -> p (k n)"), M0[0:DH, 256:512]).then_inc(x3_d, 1)
                if b:
                    act.wait_ge(d0_d, i - 1 + 1)
                    ge(act, ready["et"], i - 1)
                    act.activation(e0[0:H, :], d0[:], ACT.Exp, scale=SCALE).then_inc(e0_d, 1)
                if a:
                    act.wait_ge(ready["kv"], i + 1)
                    ge(act, ready["av"], i - 3)
                    act.copy(va[:, r, :, 0:HD], M0[:, D:2 * D].rearrange("p (h e) -> p h e", e=HD)).then_inc(v_d, 1)
                    ge(act, s0_d, i)
                    act.copy(ksb[:], M0[:, 0:D]).then_inc(k_d, 1)
                if c:
                    act.wait_ge(ready["ot"], i - 3 + 1)
                    ge(act, ready["pj"], i - 3)
                    act.copy(oT[:].rearrange("p k n -> p (k n)"), O0[0:DH, 0:256]).then_inc(oT_d, 1)
                if dd:
                    act.wait_ge(lg_m, i - 4 + 1)
                    ge(act, p_d, i - 4)
                    act.activation(er[:], O1[:, 0:NR], ACT.Exp, bias=nlm[:]).then_inc(lg_e, 1)
            run(act, step)

        @block.vector
        def _(dve):
            dve.wait_ge(pool_set, 1)
            dve.wait_ge(ld, 16 * len(CONSTS))

            def stats(i, r, turn):
                dve.wait_ge(h_in[r % 2], turn)
                ge(dve, rsa_d, i)
                dve.bn_stats(sta[:], hin[:, r % 2, :])
                dve.drain()
                dve.bn_aggr(mva[:], sta[:]).then_inc(sta_d, 1)

            def norm(i, r):
                dve.wait_ge(rsa_d, i + 1)
                ge(dve, ready["xt"], i)
                dve.tensor_scalar(xn2[:], hin[:, r % 2, :], mva[:, 0:1], rsa[:], ALU.subtract, ALU.mult).then_inc(xn_d, 1)

            stats(0, 0, 16)
            norm(0, 0)

            def step(i, r, a, b, e, c, dd):
                if dd:
                    j = i - 4
                    dve.wait_ge(rsc_d, j + 1)
                    dve.tensor_scalar(row[:, r, 0:D], row[:, r, C_H:C_H + D], mvc[:, 0:1], rsc[:], ALU.subtract, ALU.mult).then_inc(row_d, 1)
                if a:
                    p = (r + 1) % 2
                    turn = (i + 1 - p) * 8 + 16
                    stats(i + 1, (r + 1) % 4, turn)
                if e:
                    j, p = i - 2, r % 2
                    dve.wait_ge(exp_d, 2 * j + 2)
                    dve.tensor_tensor(PT[:, p, 2:4].rearrange("p r g n -> p (r g) n"), PT[:, p, 2:4].rearrange("p r g n -> p (r g) n"),
                                      mask[:].unsqueeze(1).broadcast_to([128, 2 * NG, 128]), ALU.mult).then_inc(mask_v, 1)
                    dve.wait_ge(mask_v, j + 1)
                    dve.wait_ge(mask_p, j + 1)
                    dve.wait_ge(ready["et"], j + 1)
                    for q in range(4):
                        dve.tensor_tensor(PT[:, p, q, :, 0:S8],
                                          M1[:, 0:H].rearrange("p (g r) -> p g r", r=4)[:, :, q:q + 1].broadcast_to([128, NG, S8]),
                                          mask[:, 0:S8].unsqueeze(1).broadcast_to([128, NG, S8]), ALU.mult)
                    dve.drain().then_inc(pt_d, 1)
                if a:
                    norm(i + 1, (r + 1) % 4)
                if b:
                    j = i - 1
                    dve.wait_ge(ready["vt"], j + 1)
                    ge(dve, ready["sc"], 2 * j)
                    dve.tensor_copy(vnT[:].rearrange("p g n -> p (g n)"), O1[:, 0:NG * 128]).then_inc(vt_d, 1)
                    x = O1[0:H, 384:512].rearrange("p (b s) -> p b s", s=S8)
                    dve.tensor_reduce(m0[:], x.rearrange("p b s -> p s b"), AX.X, ALU.max)
                    dve.drain()
                    ge(dve, e0_d, j)
                    dve.tensor_tensor(d0[:].rearrange("p (b s) -> p b s", s=S8), x, m0[:].unsqueeze(1).broadcast_to([H, B, S8]),
                                      ALU.subtract).then_inc(d0_d, 1)
                if c:
                    j = i - 3
                    dve.wait_ge(ready["back"], j + 1)
                    o = O0[:, 0:NG * 128].rearrange("p (h e) -> p h e", e=32)
                    dve.reciprocal(rs[:], o[:, :, HD])
                    dve.drain()
                    ge(dve, ready["ot"], j)
                    dve.tensor_tensor(on[:].rearrange("p (h e) -> p h e", e=HD), o[:, :, 0:HD],
                                      rs[:].unsqueeze(2).broadcast_to([128, H, HD]), ALU.mult).then_inc(on_d, 1)
                if a:
                    dve.wait_ge(sq_d, i + 1)
                    dve.tensor_reduce(ss[:], sq[:].rearrange("p (h e) -> p h e", e=HD), AX.X, ALU.add)
                    dve.drain()
                    ge(dve, vnp_d, i)
                    dve.tensor_scalar(ssm[:], ss[:], VEPS, None, ALU.max).then_inc(ss_d, 1)
                    dve.wait_ge(k_d, i + 1)
                    dve.wait_ge(ready["q0"], i + 1)
                    dve.tensor_tensor(prod[:], M1[:, 0:D], ksb[:], ALU.mult)
                    dve.drain()
                    ge(dve, ready["vt"], i)
                    dve.tensor_reduce(s0[:, 0:H], prod[:].rearrange("p (h e) -> p h e", e=HD), AX.X, ALU.add).then_inc(s0_d, 1)
                if c:
                    j, q = i - 3, (r + 1) % 4
                    dve.wait_ge(ready["pj"], j + 1)
                    ge(dve, row_out[q], 4 * (j - q))
                    ge(dve, hb_d, j + 1)
                    dve.tensor_tensor(row[:, q, C_H:C_H + D], O0[:, 0:D], hb1[:, q, :], ALU.add).then_inc(h4_d, 1)
                    dve.drain()
                    dve.bn_stats(stc[:], row[:, q, C_H:C_H + D])
                    dve.drain()
                    dve.bn_aggr(mvc[:], stc[:]).then_inc(stc_d, 1)
                if dd:
                    j = i - 4
                    dve.wait_ge(ready["lg"], j + 1)
                    ge(dve, lg_e, j)
                    dve.tensor_reduce(nlm[:], O1[:, 0:NR], AX.X, ALU.max, negate=True)
                    dve.drain()
                    dve.tensor_scalar(eqm[:], O1[:, 0:NR], nlm[:], 0.0, ALU.add, ALU.is_equal).then_inc(lg_m, 1)
                    dve.drain()
                    dve.tensor_tensor_scan(cum[:], eqm[:], eqm[:], 0.0, ALU.add, ALU.max)
                    dve.drain()
                    dve.scalar_tensor_tensor(out=hot8[:, j, :], in0=cum[:], scalar=1.0, in1=eqm[:], op0=ALU.is_le, op1=ALU.mult)
                    dve.wait_ge(lg_e, j + 1)
                    dve.tensor_reduce(es[:], er[:], AX.X, ALU.add)
                    dve.drain()
                    dve.reciprocal(row[:, r, C_P:C_P + 1], es[:]).then_inc(p_d, 1)
            run(dve, step)
        blocks.close()
        clear(nc, sems)


TOK = B * S
LANES = 128
XT5 = XS_TILES


def phase5(nc, d, rows, hot8, wi, wo, w_in, psS, psT, psO, psM):
    with ExitStack() as ctx:
        def sb(name, shape, dt=F32):
            return ctx.enter_context(nc.sbuf_tensor(name, shape, dt))

        def sem(name):
            return ctx.enter_context(nc.semaphore(name))

        ident = sb("ident5", [128, 128])
        before = sb("before", [128, 128])
        ones = sb("ones5", [128, 128])
        tot = sb("tot5", [128, TL, NR])
        inc = sb("inc5", [128, NR, TL])
        cnt = sb("cnt5", [128, NR], I32)
        tls = sb("tls5", [128, NR], I32)
        tlf = sb("tlf5", [128, NR])
        cumt = sb("cumt5", [128, NR])
        base = sb("base5", [128, NR])
        offs = sb("offs5", [128, TL, NR])
        offm = sb("offm5", [128, TL, NR])
        posi = sb("posi5", [128, TL], I32)
        tix = sb("tix5", [128, XT5])
        lte = sb("lte5", [128, XT5, NR])
        tef = sb("tef5", [128, XT5])
        tei = sb("tei5", [128, XT5], I32)
        xr = sb("xr5", [128, 4, ROW])
        xT = sb("xT5", [DH, 2, 128])
        hd = sb("hd5", [128, F])
        hT = sb("hT5", [128, NF, 128])
        spare = sb("spare5", [128, 4, 2])
        yo = sb("yo5", [128, 4, D])
        oidx = sb("oidx5", [128, 4], I32)

        ld, pool_set, sums, cnts, pos_d, te_d = sem("ld5"), sem("pset5"), sem("sums5"), sem("cnts5"), sem("pos_d5"), sem("te_d5")
        sorted_, x_in, out_d = sem("sorted5"), [sem(f"x_in5{n}") for n in range(4)], [sem(f"out_d5{n}") for n in range(4)]
        held = sem("held5")
        xt_r, xt_d, h_r, h_d0, h_d1, t_r, t_d0, t_d1, y_r, y_d = (sem(n + "5") for n in (
            "xt_r", "xt_d", "h_r", "h_d0", "h_d1", "t_r", "t_d0", "t_d1", "y_r", "y_d"))

        def run(eng, step):
            for i in range(8):
                step(i, i % 4, i // 4, True, i >= 1, i >= 2, i >= 3)
            with eng.Fori(2, XT5 // 4) as k:
                for r in range(4):
                    step(k * 4 + r, r, k, True, True, True, True)
            for i in range(XT5, XT5 + 3):
                step(i, i % 4, i // 4, False, i <= XT5, i <= XT5 + 1, True)

        def turn_of(turn, r, lag):
            return turn if r >= lag else turn - 1

        block = ctx.enter_context(nc.Block())

        @block.sync
        def _(sp):
            sp.dma_start(ident[:], d["idn"]).then_inc(ld, 16)
            sp.dma_start(before[:], d["before"]).then_inc(ld, 16)
            sp.wait_ge(sorted_, 16 * TL)

            def step(i, r, turn, a, b, c, dd):
                if a:
                    ge(sp, y_d, i - 3)
                    sp.dma_start(xr[:, r, :], d["xs"][bass.ds(i * 128, 128), :]).then_inc(x_in[r], 16)
            run(sp, step)

        @block.gpsimd
        def _(pool):
            pool.memset(ones[:], 1.0)
            pool.memset(spare[:], 0.0)
            pool.iota(tix[:], [[1, XT5]], base=0, channel_multiplier=0, allow_small_or_imprecise_dtypes=True)
            pool.drain().then_inc(pool_set, 1)
            pool.wait_ge(pos_d, 1)
            for i in range(TL):
                pool.indirect_dma_start(out=d["xs"], out_offset=bass.IndirectOffsetOnAxis(ap=posi[:, i:i + 1], axis=0),
                                        in_=rows[:, i, :], in_offset=None).then_inc(sorted_, 16)

            def step(i, r, turn, a, b, c, dd):
                if dd:
                    q = (r + 1) % 4
                    pool.wait_ge(y_d, i - 3 + 1)
                    ge(pool, held, i - 3)
                    pool.tensor_tensor(spare[:, q, 1:2], spare[:, q, 0:1], spare[:, q, 0:1], ALU.add).then_inc(held, 1)
                    pool.indirect_dma_start(out=d["out"], out_offset=bass.IndirectOffsetOnAxis(ap=oidx[:, q:q + 1], axis=0),
                                            in_=yo[:, q, :], in_offset=None, bounds_check=TOK - 1, oob_is_err=False
                                            ).then_inc(out_d[q], 16)
            run(pool, step)
            for q in range(4):
                pool.wait_ge(out_d[q], 16 * (XT5 // 4))

        @block.tensor
        def _(pe):
            pe.wait_ge(ld, 32)
            pe.wait_ge(pool_set, 1)
            flat = hot8[:].rearrange("p t e -> p (t e)")
            pe.matmul(psS[:, 0, 0:TL * NR], before[:], flat, start=True, stop=True)
            pe.matmul(psT[:, 0, 0:TL * NR], ones[:], flat, start=True, stop=True).then_inc(sums, 1)
            pe.wait_ge(te_d, 1)
            for s, n in w_in:
                pe.wait_ge(s, n)

            def step(i, r, turn, a, b, c, dd):
                if dd:
                    j = i - 3
                    e = pe.value_load(tei[0:1, bass.ds(j, 1)], min_val=0, max_val=NR - 1)
                    pe.wait_ge(t_d0, j + 1)
                    pe.wait_ge(t_d1, j + 1)
                    ge(pe, y_d, j - 1)
                    for f in range(NF):
                        mm = pe.matmul(psO[:, (r + 1) % 2, 0:D], hT[:, f, :], wo[:, f, bass.ds(e * D, D)],
                                       start=(f == 0), stop=(f == NF - 1))
                    mm.then_inc(y_r, 1)
                if c:
                    j = i - 2
                    pe.wait_ge(h_d0, j + 1)
                    pe.wait_ge(h_d1, j + 1)
                    ge(pe, t_d0, j)
                    ge(pe, t_d1, j)
                    for f in range(NF):
                        mm = pe.transpose(psT[:, f // 3, (f % 3) * 128:(f % 3 + 1) * 128], hd[:, f * 128:(f + 1) * 128], ident[:])
                    mm.then_inc(t_r, 1)
                if b:
                    j = i - 1
                    e = pe.value_load(tei[0:1, bass.ds(j, 1)], min_val=0, max_val=NR - 1)
                    pe.wait_ge(xt_d, j + 1)
                    ge(pe, h_d0, j)
                    ge(pe, h_d1, j)
                    for n in range(2):
                        for k in range(2):
                            mm = pe.matmul(psS[:, n, 0:F // 2], xT[:, k, :], wi[:, k, bass.ds(e * F + n * (F // 2), F // 2)],
                                           start=(k == 0), stop=(k == 1))
                    mm.then_inc(h_r, 1)
                if a:
                    pe.wait_ge(x_in[r], 16 * turn + 16)
                    ge(pe, xt_d, i)
                    for k in range(2):
                        mm = pe.transpose(psM[0:DH, 0, k * 128:(k + 1) * 128], xr[:, r, k * DH:(k + 1) * DH], ident[:])
                    mm.then_inc(xt_r, 1)
            run(pe, step)

        @block.scalar
        def _(act):
            def step(i, r, turn, a, b, c, dd):
                if c:
                    act.wait_ge(t_r, i - 2 + 1)
                    ge(act, y_r, i - 2)
                    act.copy(hT[:, 0:3].rearrange("p f n -> p (f n)"), psT[:, 0, 0:3 * 128]).then_inc(t_d0, 1)
                if b:
                    act.wait_ge(h_r, i - 1 + 1)
                    ge(act, t_r, i - 1)
                    act.activation(hd[:, 0:F // 2], psS[:, 0, 0:F // 2], ACT.Relu).then_inc(h_d0, 1)
                if a:
                    act.wait_ge(xt_r, i + 1)
                    ge(act, h_r, i)
                    act.copy(xT[:].rearrange("p k n -> p (k n)"), psM[0:DH, 0, 0:256]).then_inc(xt_d, 1)
            run(act, step)

        @block.vector
        def _(dve):
            dve.wait_ge(pool_set, 1)
            dve.wait_ge(sums, 1)
            dve.tensor_copy(tot[:].rearrange("p t e -> p (t e)"), psT[:, 0, 0:TL * NR])
            dve.drain()
            for e in range(NR):
                dve.tensor_tensor_scan(inc[:, e, :], tot[:, :, e], tot[:, :, e], 0.0, ALU.add, ALU.max)
            dve.drain()
            dve.tensor_scalar(cnt[:], inc[:, :, TL - 1], float(LANES - 1), None, ALU.add)
            dve.drain()
            dve.tensor_scalar(tls[:], cnt[:], LANES.bit_length() - 1, None, ALU.logical_shift_right)
            dve.drain()
            dve.tensor_copy(tlf[:], tls[:])
            dve.drain()
            dve.tensor_tensor_scan(cumt[:], tlf[:], tlf[:], 0.0, ALU.add, ALU.max)
            dve.drain()
            dve.tensor_tensor(base[:], cumt[:], tlf[:], ALU.subtract)
            dve.tensor_tensor(offs[:], inc[:].rearrange("p e t -> p t e"), tot[:], ALU.subtract)
            dve.tensor_tensor(lte[:], cumt[:].unsqueeze(1).broadcast_to([128, XT5, NR]), tix[:].unsqueeze(2).broadcast_to([128, XT5, NR]), ALU.is_le)
            dve.drain()
            dve.tensor_scalar(base[:], base[:], float(LANES), None, ALU.mult)
            dve.tensor_tensor(offs[:].rearrange("p t e -> p (t e)"), offs[:].rearrange("p t e -> p (t e)"), psS[:, 0, 0:TL * NR], ALU.add)
            dve.tensor_reduce(tef[:], lte[:], AX.X, ALU.add)
            dve.drain()
            dve.tensor_tensor(offm[:], offs[:], base[:].unsqueeze(1).broadcast_to([128, TL, NR]), ALU.add)
            dve.tensor_scalar(tei[:], tef[:], float(NR - 1), None, ALU.min)
            dve.drain().then_inc(te_d, 1)
            dve.tensor_tensor(offm[:], offm[:], hot8[:], ALU.mult)
            dve.drain()
            dve.tensor_reduce(offs[:, :, 0], offm[:], AX.X, ALU.add)
            dve.drain()
            dve.tensor_copy(posi[:], offs[:, :, 0]).then_inc(pos_d, 1)

            def step(i, r, turn, a, b, c, dd):
                if dd:
                    j, q = i - 3, (r + 1) % 4
                    dve.wait_ge(y_r, j + 1)
                    ge(dve, out_d[q], 16 * turn_of(turn, r, 3))
                    dve.tensor_scalar(oidx[:, q:q + 1], xr[:, q, C_V:C_V + 1], -1.0, float(TOK), ALU.mult, ALU.add)
                    dve.scalar_tensor_tensor(out=yo[:, q, :], in0=psO[:, q % 2, 0:D], scalar=xr[:, q, C_P:C_P + 1],
                                             in1=xr[:, q, C_H:C_H + D], op0=ALU.mult, op1=ALU.add)
                    dve.drain().then_inc(y_d, 1)
                if c:
                    dve.wait_ge(t_r, i - 2 + 1)
                    ge(dve, y_r, i - 2)
                    dve.tensor_copy(hT[:, 3:6].rearrange("p f n -> p (f n)"), psT[:, 1, 0:3 * 128]).then_inc(t_d1, 1)
                if b:
                    dve.wait_ge(h_r, i - 1 + 1)
                    ge(dve, t_r, i - 1)
                    dve.tensor_scalar(hd[:, F // 2:F], psS[:, 1, 0:F // 2], 0.0, None, ALU.max).then_inc(h_d1, 1)
            run(dve, step)


def program(nc, d):
    with ExitStack() as ctx:
        psS, psT, psO, psM = (ctx.enter_context(nc.psum_tensor(n, [128, 2, 512], F32)) for n in ("psS", "psT", "psO", "psM"))
        phase1(nc, d, psS, psT, psO, psM)
        w_in = ctx.enter_context(nc.semaphore("w_in"))
        wi = ctx.enter_context(nc.sbuf_tensor("wi_sb", [DH, 2, NR * F], F32))
        wo = ctx.enter_context(nc.sbuf_tensor("wo_sb", [128, NF, NR * D], F32))
        with nc.sbuf_tensor("gidx", [TT, EXP, NJ], I32) as gidx:
            phase2(nc, d, gidx, psS, psT, psO, psM)
            phase3(nc, d, gidx, wi, wo, w_in, psS, psT, psO, psM)
        rows = ctx.enter_context(nc.sbuf_tensor("rows", [128, TL, ROW], F32))
        hot8 = ctx.enter_context(nc.sbuf_tensor("hot8", [128, TL, NR], F32))
        phase4(nc, d, rows, hot8, psS, psT, psO, psM)
        phase5(nc, d, rows, hot8, wi, wo, [(w_in, 32)], psS, psT, psO, psM)


def halves(w):
    return np.ascontiguousarray(w.reshape((2, DH) + w.shape[1:]).swapaxes(0, 1))


def blocks(w, p):
    return np.ascontiguousarray(w.reshape((w.shape[0] // p, p) + w.shape[1:]).swapaxes(0, 1))


def quadrants(w):
    o = np.zeros((D, NG, 4, 32), w.dtype)
    o[:, :, :, :HD] = w.T.reshape(D, NG, 4, HD)
    return halves(o.reshape(D, NG, 128))


def waves(n):
    a = 2 * np.pi * (np.outer(np.arange(n), np.arange(n)) % n) / n
    return np.cos(a).astype(np.float32), np.sin(a).astype(np.float32)


def lay_out(a):
    rep = lambda v, n: np.ascontiguousarray(np.broadcast_to(v, (n, v.shape[-1])))
    x = np.zeros((B, DH, 2, S_IN + 2 * PAD), np.float32)
    x[:, :, :, PAD:PAD + S_IN] = a["x"].reshape(B, S_IN, 2, DH).transpose(0, 3, 2, 1)
    cd, sd = waves(D)
    cs, ss = waves(S)
    qkv, qkv1 = a["L0_attn_qkv_w"], a["L1_attn_w_qkv"]
    rel = a["L0_attn_rel_table"]
    reach = rel.shape[0] // 2
    shift = np.arange(RELW)[None, :] - (NT - 1) * TT - np.arange(TT)[:, None]
    d = {
        "x": x,
        "wdw": halves(a["L0_tok_w_dw"][:, 0, :]), "bdw": halves(a["L0_tok_b_dw"]),
        "wpw": halves(a["L0_tok_w_pw"][:, :, 0].T), "bpw": halves(a["L0_tok_b_pw"]),
        "dftd": halves(np.concatenate([cd, sd], 1)), "dftc": blocks(cs, TT), "dfts": blocks(-ss, TT),
        "gam": rep(a["L0_tok_gamma"], TT), "bet": rep(a["L0_tok_beta"], TT), "pjb": rep(a["L0_attn_proj_b"], TT),
        "wq": quadrants(qkv[:D]), "wk": quadrants(qkv[D:2 * D]), "wv": halves(qkv[2 * D:].T),
        "wpj": halves(a["L0_attn_proj_w"].T),
        "rel": np.ascontiguousarray(rel[np.clip(shift + reach, 0, 2 * reach)].transpose(0, 2, 1)),
        "wgt": halves(a["L0_ffn_gate_weight"].T),
        "wsg": halves(a["L0_ffn_Ws_g"].T), "wsu": halves(a["L0_ffn_Ws_u"].T), "wsd": blocks(a["L0_ffn_Ws_d"].T, 128),
        "wg": np.ascontiguousarray(a["L0_ffn_Wg"].transpose(0, 2, 1).reshape(EXP, 2, DH, F).transpose(0, 2, 1, 3)),
        "wu": np.ascontiguousarray(a["L0_ffn_Wu"].transpose(0, 2, 1).reshape(EXP, 2, DH, F).transpose(0, 2, 1, 3)),
        "wd": np.ascontiguousarray(a["L0_ffn_Wd"].transpose(0, 2, 1).reshape(EXP, NF, 128, D).transpose(0, 2, 1, 3)),
        "wq1": halves(qkv1[:D].T), "wkv": halves(qkv1[D:].T), "wp1": halves(a["L1_attn_w_proj"].T),
        "bp1": rep(a["L1_attn_b_proj"], 128), "wr": halves(a["L1_ffn_router_w"]),
        "wi": np.ascontiguousarray(a["L1_ffn_wi"].reshape(NR, 2, DH, F).transpose(2, 1, 0, 3).reshape(DH, 2, NR * F)),
        "wo": np.ascontiguousarray(a["L1_ffn_wo"].reshape(NR, NF, 128, D).transpose(2, 1, 0, 3).reshape(128, NF, NR * D)),
    }
    n = np.arange(128)
    same = n[:, None] // NC8 == n // NC8
    earlier = n[:, None] < n
    f32 = np.float32
    d["blk"] = same.astype(f32)
    d["ltri"] = (same & earlier).astype(f32)
    d["before"] = earlier.astype(f32)
    d["idn"] = np.eye(128, dtype=f32)
    t, c = np.meshgrid(np.arange(TC), np.arange(NC8), indexing="ij")
    r = (2 * c + t // NT) * SP + t % NT * TT
    d["tabA"] = np.broadcast_to(r // 128, (TT, TC, NC8)).astype(f32)
    d["tabB"] = (r % 128 + np.arange(TT)[:, None, None]).astype(f32)
    d["mask"] = (n[:, None] % S8 == n % S8).astype(f32)
    b, s = n[:, None] // S8, n[:, None] % S8 + S8 * np.arange(TL)
    d["place"] = np.where(s < S, TOK - (b * S + s), 0).astype(f32)
    return d


_SCRATCH = [("st", (EXP, B, S), F32), ("x1", (B, SP, XROW), F32), ("h3", (B, SP, D), F32),
            ("xs", (XS_TILES * 128, ROW), F32), ("lst", (EXP, SLOTS), I32)]


def kernel(**inputs):
    import concourse.bacc as bacc
    from concourse.bass_utils import run_bass_kernel_spmd as run

    nc = bacc.Bacc("TRN2", target_bir_lowering=False, num_devices=1)
    arrays = lay_out({k: np.asarray(v) for k, v in inputs.items()})
    arrays = {f"in_{k}_dram": np.ascontiguousarray(v) for k, v in arrays.items()}
    d = {k[3:-5]: nc.dram_tensor(k, v.shape, mybir.dt.from_np(v.dtype), kind="ExternalInput").ap() for k, v in arrays.items()}
    for name, shape, dt in _SCRATCH:
        d[name] = nc.dram_tensor(f"{name}_dram", shape, dt, kind="Internal").ap()
    d["out"] = nc.dram_tensor("out_dram", (B * S, D), F32, kind="ExternalOutput").ap()
    program(nc, d)
    r = run(nc, [arrays], core_ids=[0])
    return np.asarray(r.results[0]["out_dram"]).reshape(B, S, D)
```

```python
from contextlib import ExitStack

import numpy as np

import concourse.bass as bass
from concourse import mybir

F32 = mybir.dt.float32
BF16 = mybir.dt.bfloat16
I32 = mybir.dt.int32
U32 = mybir.dt.uint32
ALU = mybir.AluOpType
ACT = mybir.ActivationFunctionType
AX = mybir.AxisListType

B = 16
S_IN = 750
S = S_IN // 2
D = 192
DH = D // 2
H = 12
HD = D // H
K = 7
PAD = K // 2
TT = 125
NT = S // TT
SP = (-(-S // 8) + 1) * 8
EPS = 1e-5
SCALE = HD ** -0.5
NG = H // 4
PARTS = 3
Q_PART, K_PART = (0, 0, 1, 0, 2, 1), (0, 1, 0, 2, 0, 1)
STACK = len(Q_PART) * HD
HG = 3
OG = H // HG
PT_RING = 6
VA = HD + 1
UNITS = H * NT
EXP = 16
XROW = D + EXP
FSH = 384
NFS = FSH // 128
RELW = S + (NT - 1) * TT
XS_W = 388
XS_TILES = 56
XS_ROWS = XS_TILES * 128 // (B - 2)


def ge(eng, sem, n):
    if isinstance(n, int) and n <= 0:
        return
    eng.wait_ge(sem, n)


def clear(nc, sems):
    with nc.Block() as block:
        @block.gpsimd
        def _(pool):
            numbers = sorted(s.num for s in sems)
            at = 0
            for n in range(1, len(numbers) + 1):
                if n == len(numbers) or numbers[n] != numbers[n - 1] + 1:
                    pool.sem_clear(range(numbers[at], numbers[n - 1] + 1))
                    at = n


POST_SLOT = {
    "ot0": 9, "ot1": 11, "pj0": 13, "pj1": 14, "pj2": 15, "x1t0": 20, "x1t1": 21, "gate": 24,
    "sg0": 26, "su0": 27, "sg1": 28, "su1": 29, "sct": 29, "sg2": 30, "su2": 31,
    "sd0": 33, "sd1": 34, "sd2": 34,
}
PRE_SLOT = {
    "pw00": 1, "pw01": 2, "pw10": 3, "pw11": 4, "dfa0": 6, "dfa1": 7, "dfa2": 8,
    "dfb0": 10, "dfb1": 11, "dfb2": 12, "xt0": 18, "xt1": 18,
    "q0": 19, "k0": 20, "q1": 21, "k1": 22, "v0": 23, "v1": 24, "v2": 25,
}
SLOT = {**POST_SLOT, **PRE_SLOT}
ORDER = sorted(SLOT, key=lambda name: SLOT[name])
BANK = {name: n % 2 for n, name in enumerate(ORDER)}
SPLIT = ["q0", "k0", "q1", "k1", "v0", "v1", "v2"]
ON_ACT = {"dfa0", "dfa1", "dfa2", "dfb0", "dfb1", "dfb2", "xt0", "xt1", "x1t0", "x1t1", "ot0", "ot1", "gate"}
TAP_SLOT = [7, 8, 10, 11, 12, 18, 20, 23, 27, 29, 30, 34]


class Round:

    def __init__(self, b, par, attn, tail, pre, post, conv, prev):
        self.b, self.par, self.attn, self.tail = b, par, attn, tail
        self.pre, self.post, self.conv, self.prev = pre, post, conv, prev

    def has(self, name):
        return self.post if name in POST_SLOT else self.pre

    def batch(self, name):
        return self.b - 1 if name in POST_SLOT else self.b + 1

    def before(self, name):
        n = ORDER.index(name)
        for m in range(n - 1, -1, -1):
            if BANK[ORDER[m]] == BANK[name] and self.has(ORDER[m]):
                return ORDER[m], self.batch(ORDER[m]) + 1
        if self.prev is None:
            return None
        for m in range(len(ORDER) - 1, -1, -1):
            if BANK[ORDER[m]] == BANK[name] and self.prev.has(ORDER[m]):
                return ORDER[m], self.batch(ORDER[m])
        return None


def phase1(nc, d, psS, psT, psO, psM, rounds=B):
    with ExitStack() as ctx:
        def sb(name, shape, dt=F32):
            return ctx.enter_context(nc.sbuf_tensor(name, shape, dt))

        sems = []

        def sem(name):
            sems.append(ctx.enter_context(nc.semaphore(name)))
            return sems[-1]

        ident = sb("ident", [128, 128])
        wdw = sb("wdw", [DH, 2, K])
        bdw = sb("bdw", [DH, 2])
        wpw = sb("wpw", [DH, 2, D])
        bpw = sb("bpw", [DH, 2])
        dftd = sb("dftd", [DH, 2, 2 * D])
        dftc = sb("dftc", [TT, NT, S])
        dfts = sb("dfts", [TT, NT, S])
        gam = sb("gam", [TT, D])
        bet = sb("bet", [TT, D])
        pjb = sb("pjb", [TT, D])
        wq = sb("wq", [DH, 2, D])
        wk = sb("wk", [DH, 2, D])
        wv = sb("wv", [DH, 2, D])
        wpj = sb("wpj", [DH, 2, D])
        rel = sb("rel", [TT, H, RELW])
        wgt = sb("wgt", [DH, 2, EXP])
        wsg = sb("wsg", [DH, 2, FSH])
        wsu = sb("wsu", [DH, 2, FSH])
        wsd = sb("wsd", [128, NFS, D])
        mhalf = sb("mhalf", [128, NT])
        epst = sb("epst", [128, NT])
        xin = sb("xin", [DH, 2, S_IN + 2 * PAD])
        conv = sb("conv", [DH, 2, S_IN])
        pooled = sb("pooled", [DH, 2, S])
        hT = sb("hT", [DH, 2, S])
        gdft = sb("gdft", [TT, NT, 2 * D])
        y = sb("y", [TT, NT, D])
        yn = xn = y
        st1 = sb("st1", [TT, NT, 6])
        mv1 = sb("mv1", [TT, NT, 2])
        rs1 = sb("rs1", [TT, NT])
        h = sb("h", [TT, NT, D])
        hb = sb("hb", [TT, 2, NT, D])
        st2 = sb("st2", [TT, NT, 6])
        mv2 = sb("mv2", [TT, NT, 2])
        rs2 = sb("rs2", [TT, NT])
        xnT = sb("xnT", [DH, 2, S])
        qkp = sb("qkp", [DH, 2, PARTS, 2, S], BF16)
        rest = sb("rest", [TT, 3, S])
        qst = sb("qst", [STACK, 2, H, S], BF16)
        kst = sb("kst", [STACK, 2, H, S], BF16)
        va = sb("va", [TT, 2, NT, H, PARTS, VA], BF16)
        added = sb("added", [TT, 3, S])
        nmax = sb("nmax", [TT, 3])
        prob = sb("prob", [TT, 3, S])
        turned = sb("turned", [TT, 3, NT, TT])
        pT = sb("pT", [TT, PT_RING, PARTS, NT, 128], BF16)
        oraw = sb("oraw", [TT, OG, NT * HG, VA])
        rsum = sb("rsum", [TT, OG, NT * HG])
        on = sb("on", [TT, NT, D])
        oT = sb("oT", [DH, 2, S])
        h1 = sb("h1", [TT, NT, D])
        h2 = h1
        st3 = sb("st3", [TT, NT, 6])
        mv3 = sb("mv3", [TT, NT, 2])
        rs3 = sb("rs3", [TT, NT])
        xrow = sb("xrow", [TT, NT, XROW])
        x1T = sb("x1T", [DH, 2, S])
        esc = sb("esc", [TT, NT, EXP])
        esc1 = sb("esc1", [TT, NT, EXP])
        sc = sb("sc", [EXP, S])
        th = sb("th", [128, S])
        ga = sb("ga", [128, S])
        hs = sb("hs", [128, NFS, S])
        spare = sb("spare", [TT, 6])
        zero = sb("zero", [128, XS_W])

        ld_taps, ld_w, ld_rel, ld_x = (sem(n) for n in ("ld_taps", "ld_w", "ld_rel", "ld_x"))
        set_up = sem("set_up")
        rel_neg, va_one = sem("rel_neg"), sem("va_one")
        ready = {j: sem(f"{j}_ready") for j in ORDER}
        done = {j: sem(f"{j}_done") for j in ORDER}
        s_ready, add_done, exp_done = sem("s_ready"), sem("add_done"), sem("exp_done")
        t_ready, av_done = sem("t_ready"), sem("av_done")
        pt1_done, pt_rest, pt2_done, pt3_done = (sem(n) for n in ("pt1_done", "pt_rest", "pt2_done", "pt3_done"))
        part1_done, part2_done, part3_done = (sem(n) for n in ("part1_done", "part2_done", "part3_done"))
        out_qk, ld_qk = sem("out_qk"), sem("ld_qk")
        tap0_done, conv_done, relu_done = sem("tap0_done"), sem("conv_done"), sem("relu_done")
        st1_done, rs1_done, yn_done, h_done, hb_done = sem("st1_done"), sem("rs1_done"), sem("yn_done"), sem("h_done"), sem("hb_done")
        st2_done, rs2_done, xn_done = sem("st2_done"), sem("rs2_done"), sem("xn_done")
        o_read, o_sum, on_done = sem("o_read"), sem("o_sum"), sem("on_done")
        st3_done, rs3_done, x1_done = sem("st3_done"), sem("rs3_done"), sem("x1_done")
        th_done, esc_done, sc_done = sem("th_done"), sem("esc_done"), sem("sc_done")
        out_st, out_x1, out_h3, out_z = sem("out_st"), sem("out_x1"), sem("out_h3"), sem("out_z")
        z_set = sem("z_set")

        WEIGHTS = [(wpw, "wpw"), (bpw, "bpw"), (dftd, "dftd"), (dftc, "dftc"),
                   (dfts, "dfts"), (gam, "gam"), (bet, "bet"), (wq, "wq"), (wk, "wk"), (wv, "wv"),
                   (pjb, "pjb"), (wpj, "wpj"), (wgt, "wgt"), (wsg, "wsg"), (wsu, "wsu"), (wsd, "wsd")]
        W_ALL = 16 * len(WEIGHTS)

        def run(eng, body):
            body(Round(-2, 0, False, False, False, False, True, None))
            first = Round(-1, 1, False, False, True, False, True, None)
            body(first)
            second = Round(0, 0, True, False, True, False, True, first)
            body(second)
            body(Round(1, 1, True, True, True, True, True, second))
            inner = Round(None, None, True, True, True, True, True, second)
            with eng.Fori(0, (rounds - 4) // 2) as i:
                for n in range(2):
                    body(Round(i * 2 + 2 + n, n, True, True, True, True, True, inner))
            body(Round(rounds - 2, 0, True, True, True, True, False, inner))
            last = Round(rounds - 1, 1, True, True, False, True, False, inner)
            body(last)
            body(Round(rounds, 0, False, True, False, True, False, last))

        def units(r, slot, lag):
            u = slot - lag
            if u >= 0:
                return (r.b, u, r.par) if r.attn else None
            return (r.b - 1, u + UNITS, 1 - r.par) if r.tail else None

        def split_places(name, par):
            kind, n = name[0], int(name[1])
            left = rest[:, SPLIT.index(name) % 3, :]
            if kind == "v":
                parts = [va[:, par, n, :, c, 0:HD] for c in range(PARTS)]
                return *parts, left[0:TT, 0:D].rearrange("p (h e) -> p h e", e=HD)
            return *(qkp[:, "qk".index(kind), c, n, :] for c in range(PARTS)), left[0:DH, 0:S]

        def turned_bank(u):
            return psT[0:TT, u % 2, 0:NT * 128].rearrange("p (t n) -> p t n", n=128)[:, :, 0:TT]

        def split_bank(name):
            bank = psM[:, BANK[name], :]
            if name[0] == "v":
                return bank[0:TT, 0:D].rearrange("p (h e) -> p h e", e=HD)
            return bank[0:DH, 0:S]

        blocks = ctx.enter_context(ExitStack())
        block = blocks.enter_context(nc.Block())

        @block.sync
        def _(sp):
            sp.dma_start(wdw[:], d["wdw"]).then_inc(ld_taps, 16)
            sp.dma_start(bdw[:], d["bdw"]).then_inc(ld_taps, 16)

            def body(r):
                if r.attn and not r.tail:
                    sp.wait_ge(z_set, 1)
                if r.conv:
                    ge(sp, conv_done, r.b + 2)
                    sp.dma_start(xin[:], d["x"][r.b + 2]).then_inc(ld_x, 16)
                if r.conv and r.attn:
                    at = r.b * XS_ROWS
                    sp.dma_start(d["xs"][bass.ds(at, XS_ROWS), :].rearrange("(z p) c -> p z c", p=128),
                                 zero[:].unsqueeze(1).broadcast_to([128, XS_ROWS // 128, XS_W])).then_inc(out_z, 16)
                if r.attn and not r.tail:
                    sp.dma_start(d["h3"][:, S:SP, :], zero[0:B, 0:D].unsqueeze(1).broadcast_to([B, SP - S, D])).then_inc(out_z, 16)
                    sp.dma_start(d["x1"][:, S:SP, :], zero[0:B, 0:XROW].unsqueeze(1).broadcast_to([B, SP - S, XROW])).then_inc(out_z, 16)
                if r.pre:
                    b, par = r.b + 1, 1 - r.par
                    for n in range(2):
                        sp.wait_ge(part3_done, len(SPLIT) * b + 3 + n)
                        sp.dma_start(d["qk"][n].rearrange("t (f c) s -> c (t f) s", c=DH), qkp[:, n].rearrange("c t f s -> c (t f) s")).then_inc(out_qk, 16)
                    sp.wait_ge(out_qk, 32 * b + 32)
                    for place, parts in enumerate(zip(Q_PART, K_PART)):
                        for n, (dst, part) in enumerate(zip((qst, kst), parts)):
                            sp.dma_start(dst[place * HD:(place + 1) * HD, par],
                                         d["qk"][n, part].rearrange("(h e) s -> e h s", e=HD)).then_inc(ld_qk, 16)
                if r.post:
                    b = r.b - 1
                    sp.wait_ge(sc_done, b + 1)
                    sp.dma_start(d["x1"][b, 0:S, :].rearrange("(t p) c -> p t c", p=TT), xrow[:]).then_inc(out_x1, 16)
                    sp.wait_ge(done["sct"], b + 1)
                    sp.dma_start(d["st"][:, b, :], sc[:]).then_inc(out_st, 16)
                    sp.wait_ge(done["sd2"], b + 1)
                    sp.dma_start(d["h3"][b, 0:S, :].rearrange("(t p) c -> p t c", p=TT), h2[:]).then_inc(out_h3, 16)
            run(sp, body)
            sp.wait_ge(out_st, 16 * rounds)
            sp.wait_ge(out_x1, 16 * rounds)
            sp.wait_ge(out_h3, 16 * rounds)
            sp.wait_ge(out_z, 16 * (XS_TILES * 128 // XS_ROWS + 2))

        @block.gpsimd
        def _(pool):
            pool.memset(ident[:], 0.0)
            pool.memset(mhalf[:], -0.5)
            pool.memset(epst[:], EPS)
            pool.memset(zero[:], 0.0)
            pool.drain().then_inc(z_set, 1)
            pool.affine_select(out=ident[:], in_=ident[:], compare_op=ALU.not_equal, fill=1.0, base=0,
                               pattern=[[-1, 128]], channel_multiplier=1)
            pool.memset(va[:].rearrange("p a t h c e -> p (a t h c e)"), 0.0)
            pool.memset(pT[:].rearrange("p u c t n -> p (u c t n)"), 0.0)
            pool.drain()
            pool.memset(va[:, :, :, :, 0, HD:VA].rearrange("p a t h e -> p (a t h) e"), 1.0)
            pool.drain().then_inc(set_up, 1)

            def rstd(var, rs):
                pool.tensor_tensor(rs[:], var, epst[0:TT, :], ALU.add)
                pool.drain()
                return pool.tensor_tensor(rs[:], rs[:], mhalf[0:TT, :], ALU.pow)

            def third_part(b, u, par):
                n = b * UNITS + u
                pool.wait_ge(pt2_done, n + 1)
                ge(pool, av_done, n - PT_RING + 1)
                pool.tensor_tensor(pT[:, u % PT_RING, 2, :, 0:TT], turned[:, u % 3], pT[:, u % PT_RING, 1, :, 0:TT],
                                   ALU.subtract).then_inc(pt3_done, 1)

            def last_part(r, name):
                b, par, m = r.b + 1, 1 - r.par, SPLIT.index(name)
                pool.wait_ge(part2_done, len(SPLIT) * b + m + 1)
                p1, p2, p3, left = split_places(name, par)
                pool.tensor_tensor(p3, left, p2, ALU.subtract).then_inc(part3_done, 1)

            def body(r):
                for s in range(UNITS):
                    at = units(r, s, 4)
                    if at is not None:
                        third_part(*at)
                    if r.pre:
                        for name in SPLIT:
                            if SLOT[name] == s - 2:
                                last_part(r, name)
                    if r.post:
                        b = r.b - 1
                        if s == 7:
                            ge(pool, ready["ot1"], b)
                            pool.wait_ge(o_sum, b + 1)
                            for t in range(NT):
                                i = pool.tensor_tensor(on[:, t, :].rearrange("p (g h e) -> p g h e", g=OG, e=HD),
                                                       oraw[:, :, t * HG:(t + 1) * HG, 0:HD],
                                                       rsum[:, :, t * HG:(t + 1) * HG].unsqueeze(3).broadcast_to([TT, OG, HG, HD]),
                                                       ALU.mult)
                            i.then_inc(on_done, 1)
                        if s == 18:
                            pool.wait_ge(st3_done, b + 1)
                            rstd(mv3[:, :, 1], rs3).then_inc(rs3_done, 1)
                    if r.pre:
                        b = r.b + 1
                        par = 1 - r.par
                        if s == 13:
                            pool.wait_ge(st1_done, b + 1)
                            rstd(mv1[:, :, 1], rs1).then_inc(rs1_done, 1)
                        if s == 14:
                            pool.wait_ge(yn_done, b + 1)
                            ge(pool, xn_done, b)
                            pool.tensor_tensor(yn[:], yn[:], gam[:].unsqueeze(1).broadcast_to([TT, NT, D]), ALU.mult)
                            pool.drain()
                            pool.tensor_tensor(h[:], yn[:], bet[:].unsqueeze(1).broadcast_to([TT, NT, D]), ALU.add)
                            pool.drain().then_inc(h_done, 1)
                        if s == 16:
                            pool.wait_ge(st2_done, b + 1)
                            rstd(mv2[:, :, 1], rs2).then_inc(rs2_done, 1)
                        if s == 20:
                            ge(pool, done["pj2"], b - 1)
                            pool.tensor_tensor(hb[:, par], h[:], pjb[:].unsqueeze(1).broadcast_to([TT, NT, D]),
                                               ALU.add).then_inc(hb_done, 1)
            pool.wait_ge(ld_w, W_ALL)
            run(pool, body)

        @block.tensor
        def _(pe):
            pe.wait_ge(ld_w, W_ALL)
            pe.wait_ge(set_up, 1)

            def scores(b, u, par):
                hh, qt = divmod(u, NT)
                n = b * UNITS + u
                if u == 0:
                    pe.wait_ge(ld_qk, 16 * 2 * len(Q_PART) * (b + 1))
                ge(pe, add_done, n - 1)
                pe.matmul(psS[0:TT, u % 2, 0:S], qst[:, par, hh, qt * TT:(qt + 1) * TT], kst[:, par, hh, :],
                          start=True, stop=True).then_inc(s_ready, 1)

            def turn(b, u, par):
                n = b * UNITS + u
                ge(pe, pt_rest, n - 1)
                pe.wait_ge(exp_done, n + 1)
                for kt in range(NT):
                    mm = pe.transpose(psT[0:TT, u % 2, kt * 128:kt * 128 + TT], prob[:, u % 3, kt * TT:(kt + 1) * TT],
                                      ident[0:TT, 0:TT])
                mm.then_inc(t_ready, 1)

            def values(b, u, par):
                hh, qt = divmod(u, NT)
                if u == 0:
                    pe.wait_ge(part3_done, len(SPLIT) * (b + 1))
                g = hh // HG
                if u % (HG * NT) == 0:
                    ge(pe, o_read, OG * b + g - 1)
                pe.wait_ge(pt3_done, b * UNITS + u + 1)
                at = (qt * HG + hh % HG) * PARTS * VA
                o = psO[:, g % 2, at:at + PARTS * VA]
                for c in range(PARTS):
                    for kt in range(NT):
                        mm = pe.matmul(o, pT[:, u % PT_RING, c, kt, :], va[:, par, kt, hh].rearrange("p c e -> p (c e)"),
                                       start=(c == 0 and kt == 0), stop=(c == PARTS - 1 and kt == NT - 1))
                mm.then_inc(av_done, 1)

            def by_halves(out, lhs, rhs, parts=2):
                for k in range(parts):
                    mm = pe.matmul(out, lhs(k), rhs(k), start=(k == 0), stop=(k == parts - 1))
                return mm

            def job(r, name):
                b = r.batch(name)
                bank = psM[:, BANK[name], :]
                last = r.before(name)
                if last is not None:
                    ge(pe, done[last[0]], last[1])
                kind, n = name[:-1], int(name[-1]) if name[-1].isdigit() else 0
                tt = slice(n * TT, (n + 1) * TT)
                if name.startswith("pw"):
                    oh, sh = int(name[2]), int(name[3])
                    if n == 0 and oh == 0:
                        pe.wait_ge(conv_done, b + 1)
                    lo, hi = (0, S + 1) if sh == 0 else (S + 1, S_IN)
                    mm = by_halves(bank[0:DH, 0:hi - lo], lambda k: wpw[:, k, oh * DH:(oh + 1) * DH],
                                   lambda k: conv[:, k, lo:hi])
                elif kind == "dfa":
                    if n == 0:
                        pe.wait_ge(relu_done, 2 * b + 2)
                    mm = by_halves(bank[0:TT, 0:2 * D], lambda k: hT[:, k, tt], lambda k: dftd[:, k, :])
                elif kind == "dfb":
                    if n == 0:
                        for j in range(3):
                            pe.wait_ge(done[f"dfa{j}"], b + 1)
                    for k in range(NT):
                        pe.matmul(bank[0:TT, 0:D], dftc[:, k, tt], gdft[:, k, 0:D], start=(k == 0), stop=False)
                        mm = pe.matmul(bank[0:TT, 0:D], dfts[:, k, tt], gdft[:, k, D:2 * D], start=False,
                                       stop=(k == NT - 1))
                elif kind in ("xt", "x1t", "ot"):
                    src = {"xt": xn, "x1t": xrow, "ot": on}[kind]
                    pe.wait_ge({"xt": xn_done, "x1t": x1_done, "ot": on_done}[kind], b + 1)
                    for t in range(NT):
                        mm = pe.transpose(bank[0:DH, t * TT:(t + 1) * TT], src[:, t, n * DH:(n + 1) * DH],
                                          ident[0:TT, 0:TT])
                elif kind in ("q", "k"):
                    if name == "q0":
                        pe.wait_ge(done["xt0"], b + 1)
                        pe.wait_ge(done["xt1"], b + 1)
                    w = wq if kind == "q" else wk
                    mm = by_halves(bank[0:DH, 0:S], lambda k: w[:, k, n * DH:(n + 1) * DH], lambda k: xnT[:, k, :])
                elif kind == "v":
                    mm = by_halves(bank[0:TT, 0:D], lambda k: xnT[:, k, tt], lambda k: wv[:, k, :])
                elif kind == "pj":
                    if n == 0:
                        pe.wait_ge(done["ot0"], b + 1)
                        pe.wait_ge(done["ot1"], b + 1)
                    mm = by_halves(bank[0:TT, 0:D], lambda k: oT[:, k, tt], lambda k: wpj[:, k, :])
                elif name == "gate":
                    pe.wait_ge(done["x1t0"], b + 1)
                    pe.wait_ge(done["x1t1"], b + 1)
                    for t in range(NT):
                        mm = by_halves(bank[0:TT, t * EXP:(t + 1) * EXP], lambda k: x1T[:, k, t * TT:(t + 1) * TT],
                                       lambda k: wgt[:, k, :])
                elif name == "sct":
                    pe.wait_ge(sc_done, b + 1)
                    for t in range(NT):
                        mm = pe.transpose(bank[0:EXP, t * TT:(t + 1) * TT], xrow[:, t, D:XROW], ident[0:TT, 0:TT])
                elif kind in ("sg", "su"):
                    w = wsg if kind == "sg" else wsu
                    mm = by_halves(bank[:, 0:S], lambda k: w[:, k, n * 128:(n + 1) * 128], lambda k: x1T[:, k, :])
                else:
                    if n == 0:
                        for j in range(3):
                            pe.wait_ge(done[f"su{j}"], b + 1)
                    mm = by_halves(bank[0:TT, 0:D], lambda k: hs[:, k, tt], lambda k: wsd[:, k, :], NFS)
                mm.then_inc(ready[name], 1)

            def body(r):
                for s in range(UNITS):
                    for lag, step in ((0, scores), (6, values), (2, turn)):
                        at = units(r, s, lag)
                        if at is not None:
                            step(*at)
                    for name in ORDER:
                        if r.has(name) and SLOT[name] == s:
                            job(r, name)
            run(pe, body)

        @block.scalar
        def _(act):
            def exps(b, u, par):
                n = b * UNITS + u
                ge(act, t_ready, n - 2)
                act.wait_ge(add_done, n + 1)
                act.activation(prob[:, u % 3, :], added[:, u % 3, :], ACT.Exp, bias=nmax[:, u % 3:u % 3 + 1],
                               scale=-1.0).then_inc(exp_done, 1)

            def first_part(b, u, par):
                n = b * UNITS + u
                ge(act, av_done, n - PT_RING + 1)
                act.wait_ge(t_ready, n + 1)
                act.copy(pT[:, u % PT_RING, 0, :, 0:TT], turned_bank(u)).then_inc(pt1_done, 1)

            def second_part(b, u, par):
                n = b * UNITS + u
                act.wait_ge(pt_rest, n + 1)
                act.copy(pT[:, u % PT_RING, 1, :, 0:TT], turned[:, u % 3]).then_inc(pt2_done, 1)

            def first_tap(b):
                ge(act, ready["pw11"], b)
                act.wait_ge(ld_x, 16 * b + 16)
                for half in range(2):
                    act.activation(conv[:, half, :], xin[:, half, 0:S_IN], ACT.Identity, bias=bdw[:, half:half + 1],
                                   scale=wdw[:, half, 0:1]).then_inc(tap0_done, 1)

            def relu(b, oh):
                act.wait_ge(done[f"pw{oh}1"], b + 1)
                if oh == 0:
                    ge(act, ready["dfa2"], b)
                act.activation(hT[:, oh, :], pooled[:, oh, :], ACT.Relu, bias=bpw[:, oh:oh + 1]).then_inc(relu_done, 1)

            def empty(r, name):
                b = r.batch(name)
                bank = psM[:, BANK[name], :]
                kind, n = name[:-1], int(name[-1]) if name[-1].isdigit() else 0
                tt = slice(n * TT, (n + 1) * TT)
                act.wait_ge(ready[name], b + 1)
                if kind == "dfa":
                    if n == 0:
                        ge(act, ready["dfb2"], b)
                    i = act.copy(gdft[:, n, :], bank[0:TT, 0:2 * D])
                elif kind == "dfb":
                    if n == 0:
                        ge(act, ready["xt1"], b)
                    i = act.copy(y[:, n, :], bank[0:TT, 0:D])
                elif kind in ("xt", "x1t", "ot"):
                    dst, last = {"xt": (xnT, "v2"), "x1t": (x1T, "su2"), "ot": (oT, "pj2")}[kind]
                    ge(act, ready[last], b)
                    i = act.copy(dst[:, n, :], bank[0:DH, 0:S])
                elif name == "gate":
                    ge(act, sc_done, b)
                    i = act.activation(esc[:].rearrange("p t e -> p (t e)"), bank[0:TT, 0:NT * EXP], ACT.Exp, scale=-1.0)
                i.then_inc(done[name], 1)

            def split_first(r, name):
                b, m = r.b + 1, SPLIT.index(name)
                act.wait_ge(ready[name], b + 1)
                if m == 0:
                    ge(act, out_qk, 32 * b)
                if name == "v0":
                    ge(act, av_done, (b - 1) * UNITS)
                p1, p2, p3, left = split_places(name, 1 - r.par)
                act.mul(p1, split_bank(name), -SCALE if name[0] == "q" else 1.0).then_inc(part1_done, 1)

            def split_second(r, name):
                b = r.b + 1
                act.wait_ge(done[name], b + 1)
                p1, p2, p3, left = split_places(name, 1 - r.par)
                act.copy(p2, left).then_inc(part2_done, 1)

            def tanh(b, n):
                act.wait_ge(ready[f"sg{n}"], b + 1)
                if n > 0:
                    act.wait_ge(done[f"sg{n - 1}"], b + 1)
                else:
                    ge(act, done["sg2"], b)
                act.activation(th[:], psM[:, BANK[f"sg{n}"], 0:S], ACT.Tanh, scale=0.5).then_inc(th_done, 1)

            def body(r):
                for s in range(UNITS):
                    at = units(r, s, 1)
                    if at is not None:
                        exps(*at)
                    at = units(r, s, 2)
                    if at is not None:
                        first_part(*at)
                    at = units(r, s, 3)
                    if at is not None:
                        second_part(*at)
                    for name in SPLIT:
                        if r.pre and SLOT[name] == s - 2:
                            split_second(r, name)
                    for name in ORDER:
                        if r.has(name) and SLOT[name] == s:
                            if name in ON_ACT:
                                empty(r, name)
                            elif name in SPLIT:
                                split_first(r, name)
                            elif name.startswith("sg"):
                                tanh(r.batch(name), int(name[2]))
                            if name in ("pw01", "pw11"):
                                relu(r.batch(name), int(name[2]))
                    if r.conv and s == 5:
                        first_tap(r.b + 2)
            for t, name in WEIGHTS:
                act.dma_start(t[:], d[name]).then_inc(ld_w, 16)
            act.dma_start(rel[:], d["rel"]).then_inc(ld_rel, 16)
            act.wait_ge(ld_taps, 32)
            run(act, body)

        @block.vector
        def _(dve):
            dve.wait_ge(ld_taps, 32)

            def add(b, u, par):
                hh, qt = divmod(u, NT)
                n = b * UNITS + u
                lo = (NT - 1 - qt) * TT
                dve.tensor_tensor_reduce(out=added[:, u % 3, :], in0=psS[0:TT, u % 2, 0:S],
                                         in1=rel[:, hh, lo:lo + S], scale=1.0, scalar=3.0e38, op0=ALU.add,
                                         op1=ALU.min, accum_out=nmax[:, u % 3:u % 3 + 1]).then_inc(add_done, 1)

            def add_waits(b, u, par):
                n = b * UNITS + u
                dve.wait_ge(s_ready, n + 1)
                ge(dve, exp_done, n - 2)

            def leave(b, u, par):
                n = b * UNITS + u
                dve.wait_ge(pt1_done, n + 1)
                ge(dve, pt3_done, n - 2)
                dve.tensor_tensor(turned[:, u % 3], turned_bank(u), pT[:, u % PT_RING, 0, :, 0:TT],
                                  ALU.subtract).then_inc(pt_rest, 1)

            def tap(b, n):
                k, half = 1 + n // 2, n % 2
                if k == 1:
                    dve.wait_ge(tap0_done, 2 * b + half + 1)
                x = xin[:, half, k:k + S_IN]
                w = wdw[:, half, k:k + 1]
                dve.scalar_tensor_tensor(out=conv[:, half, :], in0=x, scalar=w, in1=conv[:, half, :],
                                         op0=ALU.mult, op1=ALU.add)
                i = dve.drain()
                if n == 2 * K - 3:
                    i.then_inc(conv_done, 1)

            def stats(src, st, mv, signal, before=()):
                for s, n in before:
                    ge(dve, s, n)
                for t in range(NT):
                    dve.bn_stats(st[:, t, :], src(t))
                dve.drain()
                for t in range(NT):
                    i = dve.bn_aggr(mv[:, t, :], st[:, t, :])
                i.then_inc(signal, 1)

            def norm(dst, src, mv, rs, signal):
                for t in range(NT):
                    i = dve.tensor_scalar(dst(t), src(t), mv[:, t, 0:1], rs[:, t:t + 1], ALU.subtract, ALU.mult)
                i.then_inc(signal, 1)

            def empty(r, name):
                b = r.batch(name)
                bank = psM[:, BANK[name], :]
                kind, n = name[:-1], int(name[-1]) if name[-1].isdigit() else 0
                dve.wait_ge(ready[name], b + 1)
                par = 1 - r.par
                if name.startswith("pw"):
                    oh, sh = int(name[2]), int(name[3])
                    if sh == 0:
                        ge(dve, relu_done, 2 * b)
                    lo, hi = (0, S + 1) if sh == 0 else (S + 1, S_IN)
                    i = dve.tensor_reduce(pooled[:, oh, lo // 2:hi // 2],
                                          bank[0:DH, 0:hi - lo].rearrange("p (s w) -> p s w", w=2), AX.X, ALU.max)
                elif name in SPLIT:
                    m = SPLIT.index(name)
                    dve.wait_ge(part1_done, len(SPLIT) * b + m + 1)
                    before = m - 3 if m >= 3 else max(k for k in range(len(SPLIT)) if k % 3 == m) - len(SPLIT)
                    ge(dve, part3_done, len(SPLIT) * b + before + 1)
                    p1, p2, p3, left = split_places(name, par)
                    i = dve.scalar_tensor_tensor(out=left, in0=split_bank(name), scalar=-SCALE if name[0] == "q" else 1.0,
                                                 in1=p1, op0=ALU.mult, op1=ALU.subtract)
                elif kind == "pj":
                    if n == 0:
                        dve.wait_ge(hb_done, b + 1)
                        ge(dve, out_h3, 16 * b)
                    i = dve.tensor_tensor(h1[:, n, :], bank[0:TT, 0:D], hb[:, par, n, :], ALU.add)
                elif name == "sct":
                    ge(dve, out_st, 16 * b)
                    i = dve.tensor_copy(sc[:], bank[0:EXP, 0:S])
                elif kind == "sg":
                    if n > 0:
                        dve.wait_ge(done[f"su{n - 1}"], b + 1)
                    else:
                        ge(dve, done["su2"], b)
                    dve.wait_ge(th_done, 3 * b + n + 1)
                    i = dve.scalar_tensor_tensor(out=ga[:], in0=th[:], scalar=1.0, in1=bank[:, 0:S],
                                                 op0=ALU.add, op1=ALU.mult)
                elif kind == "su":
                    if n == 0:
                        ge(dve, ready["sd2"], b)
                    dve.wait_ge(done[f"sg{n}"], b + 1)
                    i = dve.scalar_tensor_tensor(out=hs[:, n, :], in0=ga[:], scalar=0.5, in1=bank[:, 0:S],
                                                 op0=ALU.mult, op1=ALU.mult)
                else:
                    i = dve.tensor_tensor(h2[:, n, :], bank[0:TT, 0:D], h1[:, n, :], ALU.add)
                i.then_inc(done[name], 1)

            def read_o(b, g):
                dve.wait_ge(av_done, b * UNITS + (g + 1) * HG * NT)
                if g == 0:
                    ge(dve, on_done, b)
                dve.tensor_reduce(oraw[:, g], psO[0:TT, g % 2, 0:HG * NT * PARTS * VA].rearrange("p (u c e) -> p u e c", c=PARTS, e=VA),
                                  AX.X, ALU.add)
                dve.drain().then_inc(o_read, 1)
                if g == OG - 1:
                    dve.reciprocal(rsum[:], oraw[:, :, :, HD]).then_inc(o_sum, 1)

            def body(r):
                for s in range(UNITS):
                    if s == 0 and r.attn and not r.tail:
                        dve.wait_ge(ld_rel, 16)
                        dve.tensor_scalar(rel[:], rel[:], -1.0, None, ALU.mult).then_inc(rel_neg, 1)
                        dve.wait_ge(rel_neg, 1)
                    at = units(r, s, 0)
                    if at is not None:
                        add_waits(*at)
                        dve.memset(spare[:, s % 6:s % 6 + 1], 0.0)
                        add(*at)
                    for name in ORDER:
                        if r.has(name) and SLOT[name] == s - 1 and name not in ON_ACT:
                            empty(r, name)
                    at = units(r, s, 7)
                    if at is not None and at[1] % (HG * NT) == HG * NT - 1:
                        read_o(at[0], at[1] // (HG * NT))
                    if r.post:
                        b = r.b - 1
                        if s == 18:
                            for j in range(3):
                                dve.wait_ge(done[f"pj{j}"], b + 1)
                            stats(lambda t: h1[:, t, :], st3, mv3, st3_done)
                        if s == 19:
                            dve.wait_ge(rs3_done, b + 1)
                            ge(dve, out_x1, 16 * b)
                            norm(lambda t: xrow[:, t, 0:D], lambda t: h1[:, t, :], mv3, rs3, x1_done)
                        if s == 24:
                            dve.wait_ge(done["gate"], b + 1)
                            dve.tensor_scalar(esc1[:], esc[:], 1.0, None, ALU.add)
                            dve.drain()
                            dve.reciprocal(xrow[:, :, D:XROW], esc1[:]).then_inc(sc_done, 1)
                    if r.conv and s in TAP_SLOT:
                        tap(r.b + 2, TAP_SLOT.index(s))
                    if r.pre:
                        b = r.b + 1
                        if s == 13:
                            for j in range(3):
                                dve.wait_ge(done[f"dfb{j}"], b + 1)
                            ge(dve, rs1_done, b)
                            stats(lambda t: y[:, t, :], st1, mv1, st1_done)
                        if s == 14:
                            dve.wait_ge(rs1_done, b + 1)
                            ge(dve, h_done, b)
                            norm(lambda t: yn[:, t, :], lambda t: y[:, t, :], mv1, rs1, yn_done)
                        if s == 16:
                            dve.wait_ge(h_done, b + 1)
                            stats(lambda t: h[:, t, :], st2, mv2, st2_done)
                        if s == 17:
                            dve.wait_ge(rs2_done, b + 1)
                            ge(dve, ready["xt1"], b)
                            norm(lambda t: xn[:, t, :], lambda t: h[:, t, :], mv2, rs2, xn_done)
                    at = units(r, s, 2)
                    if at is not None:
                        leave(*at)
            run(dve, body)
        blocks.close()
        clear(nc, sems)





CAP = B * S * 2 // EXP
NC8 = 128 // EXP
CH = B * S // NC8
TC = CH // TT
LO = 32
HI = -(-CAP // LO)
SLOTS = HI * LO
NJ = CAP // TT
NONE = 9999.0
TOP_BIT = 29


def phase2(nc, d, gidx, psS, psT, psO, psM):
    with ExitStack() as ctx:
        def sb(name, shape, dt=F32):
            return ctx.enter_context(nc.sbuf_tensor(name, shape, dt))

        sems = []

        def sem(name):
            sems.append(ctx.enter_context(nc.semaphore(name)))
            return sems[-1]

        sco = sb("sco", [128, CH])
        junk = sb("junk", [128, CH], BF16)
        blk = sb("blk", [128, 128])
        ltri = sb("ltri", [128, 128])
        ident2 = sb("ident2", [128, 128])
        tabA = sb("tabA", [TT, TC, NC8])
        tabB = sb("tabB", [TT, TC, NC8])
        ihi = sb("ihi", [TT, HI], BF16)
        ilo = sb("ilo", [TT, LO], BF16)
        cur = sb("cur", [128, 1], I32)
        cand = sb("cand", [128, 1], I32)
        bit = sb("bit", [128, 1], I32)
        ahead = sb("ahead", [128, 1], I32)
        bitf = sb("bitf", [128, 1])
        take = sb("take", [128, 1], I32)
        cnt = sb("cnt", [128, 1])
        gt = sb("gt", [128, CH])
        eq = sb("eq", [128, CH])
        eqs = sb("eqs", [128, CH])
        cols = sb("cols", [128, 2])
        thr = sb("thr", [128, 1])
        sel = sb("sel", [128, CH])
        rank = sb("rank", [128, CH])
        off = sb("off", [128, 1])
        slot = sb("slot", [128, CH], I32)
        shi = sb("shi", [128, CH], I32)
        slo = sb("slo", [128, CH], I32)
        shif = sb("shif", [128, CH])
        slof = sb("slof", [128, CH])
        posT = sb("posT", [TT, 2, TC, 128], BF16)
        zer = sb("zer", [TT, 512], BF16)
        ohh = sb("ohh", [TT, 2, 128, HI], BF16)
        ohl = sb("ohl", [TT, 2, 128, LO], BF16)
        vals = sb("vals", [TT, 2, 128, 2, LO], BF16)
        lst = sb("lst_sb", [HI, EXP, LO], I32)
        listA = sb("listA", [HI, EXP, LO])

        ld, pool_set, cnt_done, tot_done = sem("ld2"), sem("pool_set"), sem("cnt_done"), sem("tot_done")
        cols_done, sums_done, rank_done, off_done = sem("cols_done"), sem("sums_done"), sem("rank_done"), sem("off_done")
        slot_done, turned, pos_done = sem("slot_done"), sem("turned2"), sem("pos_done")
        hot_done, hi_done, valB_done, valA_done, list_acc, list_done = sem("hot_done"), sem("hi_done"), sem("valB_done"), sem("valA_done"), sem("list_acc"), sem("list_done")
        lst_out, idx_in, dve_set = sem("lst_out"), sem("idx_in"), sem("dve_set")
        def hot(eng, t, which, iota, n, out):
            return eng.tensor_tensor(out, posT[:, which, t, :].unsqueeze(2).broadcast_to([TT, 128, n]),
                                     iota.unsqueeze(1).broadcast_to([TT, 128, n]), ALU.is_equal)

        def chunk_hot(t, c):
            return ohl[:, t % 2].rearrange("p (e c) l -> p e c l", c=NC8)[:, :, c, :]

        def chunk_vals(t, c, v):
            return vals[:, t % 2].rearrange("p (e c) v l -> p e c v l", c=NC8)[:, :, c, v, :]

        blocks = ctx.enter_context(ExitStack())
        block = blocks.enter_context(nc.Block())

        @block.sync
        def _(sp):
            sp.dma_start(sco[:], d["st"].rearrange("e b s -> e (b s)").rearrange("e (c j) -> (e c) j", c=NC8)).then_inc(ld, 16)
            for t, name in ((blk, "blk"), (ltri, "ltri"), (ident2, "idn"), (tabA, "tabA"), (tabB, "tabB")):
                sp.dma_start(t[:], d[name]).then_inc(ld, 16)
            sp.wait_ge(list_done, 1)
            sp.dma_start(d["lst"].rearrange("e (h l) -> h e l", l=LO), lst[:]).then_inc(lst_out, 16)
            sp.wait_ge(lst_out, 16)
            sp.dma_start(gidx[:], d["lst"][:, 0:CAP].rearrange("e (p j) -> p e j", p=TT)).then_inc(idx_in, 16)
            sp.wait_ge(idx_in, 16)

        @block.gpsimd
        def _(pool):
            pool.iota(ihi[:], [[1, HI]], base=0, channel_multiplier=0, allow_small_or_imprecise_dtypes=True)
            pool.iota(ilo[:], [[1, LO]], base=0, channel_multiplier=0, allow_small_or_imprecise_dtypes=True)
            pool.memset(zer[:], 0.0)
            pool.drain().then_inc(pool_set, 1)
            pool.wait_ge(ld, 16 * 6)
            for t in range(TC):
                pool.wait_ge(hot_done, t + 1)
                ge(pool, list_acc, t - 1)
                for c in range(NC8 // 2):
                    i = pool.tensor_tensor(chunk_vals(t, c, 0), chunk_hot(t, c),
                                           tabA[:, t, c:c + 1].unsqueeze(2).broadcast_to([TT, EXP, LO]), ALU.mult)
                i.then_inc(valA_done, 1)

        @block.scalar
        def _(act):
            act.wait_ge(ld, 16 * 6)
            for t in range(TC):
                act.wait_ge(hot_done, t + 1)
                ge(act, list_acc, t - 1)
                for c in range(NC8 // 2, NC8):
                    act.mul(chunk_vals(t, c, 0), chunk_hot(t, c), tabA[:, t, c:c + 1])
                for c in range(NC8):
                    i = act.mul(chunk_vals(t, c, 1), chunk_hot(t, c), tabB[:, t, c:c + 1])
                i.then_inc(valB_done, 1)

        @block.tensor
        def _(pe):
            pe.wait_ge(ld, 16 * 6)
            with pe.Fori(0, TOP_BIT + 1) as i:
                pe.wait_ge(cnt_done, i + 1)
                pe.matmul(psM[:, 0, 0:1], blk[:], cnt[:], start=True, stop=True).then_inc(tot_done, 1)
            pe.wait_ge(cols_done, 1)
            pe.matmul(psM[:, 1, 0:1], blk[:], cols[:, 0:1], start=True, stop=True)
            pe.matmul(psM[:, 1, 1:2], ltri[:], cols[:, 1:2], start=True, stop=True).then_inc(sums_done, 1)
            pe.wait_ge(rank_done, 1)
            pe.matmul(psM[:, 1, 2:3], ltri[:], rank[:, CH - 1:CH], start=True, stop=True).then_inc(off_done, 1)
            pe.wait_ge(slot_done, 1)
            pe.wait_ge(pool_set, 1)
            for n in range(2):
                pe.matmul(psO[0:HI, n, :], zer[:, 0:HI], zer[:, :], start=True, stop=False, skip_group_check=True)
            for t in range(TC):
                ge(pe, pos_done, t - 1)
                pe.transpose(psS[0:TT, t % 2, 0:128], shif[:, t * TT:(t + 1) * TT], ident2[:])
                pe.transpose(psS[0:TT, t % 2, 128:256], slof[:, t * TT:(t + 1) * TT], ident2[:]).then_inc(turned, 1)
            for t in range(TC):
                pe.wait_ge(valB_done, t + 1)
                pe.wait_ge(valA_done, t + 1)
                pe.wait_ge(hi_done, t + 1)
                for e in range(EXP):
                    for c in range(NC8):
                        mm = pe.matmul(psO[0:HI, e // 8, (e % 8) * 2 * LO:(e % 8 + 1) * 2 * LO], ohh[:, t % 2, e * NC8 + c, :],
                                       vals[:, t % 2, e * NC8 + c].rearrange("p v l -> p (v l)"),
                                       start=False, stop=(t == TC - 1 and c == NC8 - 1), skip_group_check=True)
                mm.then_inc(list_acc, 1)

        @block.vector
        def _(dve):
            dve.wait_ge(ld, 16 * 6)
            dve.memset(cur[:], 0)
            dve.memset(bit[:], 1 << TOP_BIT)
            dve.memset(cand[:], 1 << TOP_BIT)
            dve.memset(bitf[:], float(1 << TOP_BIT))
            dve.drain()
            with dve.Fori(0, TOP_BIT + 1) as i:
                dve.tensor_scalar(junk[:], sco[:], cand[:].bitcast(F32), None, ALU.is_ge, ALU.add, accum_out=cnt[:])
                dve.drain().then_inc(cnt_done, 1)
                dve.tensor_scalar(bit[:], bit[:], 1, None, ALU.logical_shift_right)
                dve.drain()
                dve.tensor_tensor(ahead[:], cur[:], bit[:], ALU.bitwise_or)
                dve.wait_ge(tot_done, i + 1)
                dve.tensor_scalar(take[:], psM[:, 0, 0:1], float(CAP), bitf[:], ALU.is_ge, ALU.mult)
                dve.drain()
                dve.tensor_tensor(cand[:], ahead[:], take[:], ALU.bitwise_or)
                dve.tensor_tensor(cur[:], cur[:], take[:], ALU.bitwise_or)
                dve.tensor_scalar(bitf[:], bitf[:], 0.5, None, ALU.mult)
                dve.drain()
            dve.tensor_scalar(gt[:], sco[:], cur[:].bitcast(F32), None, ALU.is_gt, ALU.add, accum_out=cols[:, 0:1])
            dve.tensor_scalar(eq[:], sco[:], cur[:].bitcast(F32), None, ALU.is_equal)
            dve.drain()
            dve.tensor_tensor_scan(eqs[:], eq[:], eq[:], 0.0, ALU.add, ALU.max)
            dve.drain()
            dve.tensor_copy(cols[:, 1:2], eqs[:, CH - 1:CH]).then_inc(cols_done, 1)
            dve.wait_ge(sums_done, 1)
            dve.tensor_scalar(thr[:], psM[:, 1, 0:1], -1.0, float(CAP), ALU.mult, ALU.add)
            dve.drain()
            dve.tensor_tensor(thr[:], thr[:], psM[:, 1, 1:2], ALU.subtract)
            dve.drain()
            dve.scalar_tensor_tensor(out=sel[:], in0=eqs[:], scalar=thr[:], in1=eq[:], op0=ALU.is_le, op1=ALU.mult)
            dve.drain()
            dve.tensor_tensor(sel[:], sel[:], gt[:], ALU.add)
            dve.drain()
            dve.tensor_tensor_scan(rank[:], sel[:], sel[:], 0.0, ALU.add, ALU.max).then_inc(rank_done, 1)
            dve.wait_ge(off_done, 1)
            dve.tensor_scalar(off[:], psM[:, 1, 2:3], -1.0 - NONE, None, ALU.add)
            dve.drain()
            dve.scalar_tensor_tensor(out=rank[:], in0=rank[:], scalar=off[:], in1=sel[:], op0=ALU.add, op1=ALU.mult)
            dve.drain()
            dve.tensor_scalar(slot[:], rank[:], NONE, None, ALU.add)
            dve.drain()
            dve.tensor_scalar(shi[:], slot[:], LO.bit_length() - 1, None, ALU.logical_shift_right)
            dve.tensor_scalar(slo[:], slot[:], LO - 1, None, ALU.bitwise_and)
            dve.drain()
            dve.tensor_copy(shif[:], shi[:])
            dve.tensor_copy(slof[:], slo[:])
            dve.drain().then_inc(slot_done, 1)
            for t in range(TC):
                dve.wait_ge(turned, t + 1)
                dve.tensor_copy(posT[:, :, t, :], psS[0:TT, t % 2, 0:256].rearrange("p (v n) -> p v n", v=2)).then_inc(pos_done, 1)
            dve.wait_ge(pool_set, 1)
            dve.wait_ge(pos_done, TC)

            for t in range(TC):
                ge(dve, valB_done, t - 1)
                ge(dve, valA_done, t - 1)
                hot(dve, t, 1, ilo[:], LO, ohl[:, t % 2]).then_inc(hot_done, 1)
                ge(dve, list_acc, t - 1)
                hot(dve, t, 0, ihi[:], HI, ohh[:, t % 2]).then_inc(hi_done, 1)
            dve.wait_ge(list_acc, TC)
            acc = psO[0:HI, :, :].rearrange("p n (e v l) -> p (n e) v l", v=2, l=LO)
            dve.tensor_scalar(listA[:], acc[:, :, 0, :], 128.0, None, ALU.mult)
            dve.drain()
            dve.tensor_tensor(lst[:], listA[:], acc[:, :, 1, :], ALU.add).then_inc(list_done, 1)
        blocks.close()
        clear(nc, sems)


F = 768
NF = F // 128
NH = 2
HT = CAP // NH
JH = NJ // NH


def phase3(nc, d, gidx, wi, wo, w_in, load_next, psS, psT, psO, psM):
    with ExitStack() as ctx:
        def sb(name, shape, dt=F32):
            return ctx.enter_context(nc.sbuf_tensor(name, shape, dt))

        sems = []

        def sem(name):
            sems.append(ctx.enter_context(nc.semaphore(name)))
            return sems[-1]

        ident3 = sb("ident3", [128, 128])
        wg = sb("wg_sb", [DH, 2, 2, F])
        wu = sb("wu_sb", [DH, 2, 2, F])
        wd = sb("wd_sb", [128, 2, NF, D])
        idx = sb("idx", [TT, 2, NJ], I32)
        xg = sb("xg", [TT, 2, NJ, XROW])
        spare = sb("spare3", [TT, 6, 2])
        scr = sb("scr", [TT, 2, NJ])
        xgT = sb("xgT", [DH, 2, CAP])
        sg = sb("sg_sb", [128, 2, HT])
        hid = sb("hid", [128, NF, CAP])
        yo = sb("yo", [TT, 2, NJ, D])

        ldi, ldw = sem("ldi"), [sem("ldw0"), sem("ldw1")]
        idx_done, scr_done, added = sem("idx_done"), sem("scr_done"), sem("added3")
        gathered = [sem("gathered0"), sem("gathered1")]
        xt_ready, xt_done = sem("xt_ready"), sem("xt_done")
        g_ready, sg_done, hid_done = sem("g_ready"), sem("sg_done"), sem("hid_done")
        y_ready, y_done = sem("y_ready"), sem("y_done")
        NX = 2 * NH
        NP = NF * NH
        blocks = ctx.enter_context(ExitStack())
        block = blocks.enter_context(nc.Block())

        @block.sync
        def _(sp):
            sp.dma_start(ident3[:], d["idn"]).then_inc(ldi, 16)

            def load(e, par):
                sp.dma_start(wg[:, par], d["wg"][e]).then_inc(ldw[par], 16)
                sp.dma_start(wu[:, par], d["wu"][e]).then_inc(ldw[par], 16)
                sp.dma_start(wd[:, par], d["wd"][e]).then_inc(ldw[par], 16)

            load(0, 0)
            load(1, 1)
            with sp.Fori(1, EXP // 2) as i:
                for par in range(2):
                    sp.wait_ge(y_ready, (i * 2 + par - 1) * NJ)
                    load(i * 2 + par, par)
            sp.dma_start(wi[:], d["wi"]).then_inc(w_in, 16)
            sp.dma_start(wo[:], d["wo"]).then_inc(w_in, 16)
            load_next(sp)

        @block.gpsimd
        def _(pool):
            def held(n):
                pool.tensor_tensor(spare[:, n, 1:2], spare[:, n, 0:1], spare[:, n, 0:1], ALU.add)

            pool.memset(spare[:], 0.0)

            def fetch(pair, par):
                e = pair * 2 + par
                """Copy expert e's indices to a fixed place and gather its rows."""
                ge(pool, gathered[par], pair * 16 * NJ)
                pool.tensor_copy(idx[:, par, :], gidx[:, e, :]).then_inc(idx_done, 1)
                pool.wait_ge(idx_done, e + 1)
                ge(pool, xt_done, (e - 1) * NX)
                held(par)
                for j in range(NJ):
                    pool.indirect_dma_start(out=xg[:, par, j, :], out_offset=None,
                                            in_=d["x1"].rearrange("b s c -> (b s) c"),
                                            in_offset=bass.IndirectOffsetOnAxis(ap=idx[:, par, j:j + 1], axis=0)
                                            ).then_inc(gathered[par], 16)

            def scores(pair, par):
                e = pair * 2 + par
                """The scores, for expert e's column of the gathered rows."""
                pool.wait_ge(gathered[par], (pair + 1) * 16 * NJ)
                ge(pool, y_done, (e - 1) * NJ)
                pool.tensor_copy(scr[:, par, :], xg[:, par, :, bass.ds(D + e, 1)].rearrange("p j o -> p (j o)")).then_inc(scr_done, 1)

            def scatter(e, par):
                for j in range(NJ):
                    if j % JH == 0:
                        pool.wait_ge(y_done, e * NJ + j + JH)
                        ge(pool, added, e * NJ * 16)
                        held(2 + 2 * par + j // JH)
                    pool.indirect_dma_start(out=d["h3"].rearrange("b s c -> (b s) c"),
                                            out_offset=bass.IndirectOffsetOnAxis(ap=idx[:, par, j:j + 1], axis=0),
                                            in_=yo[:, par, j, :], in_offset=None, compute_op=ALU.add
                                            ).then_inc(added, 16)

            def pair(i, more):
                for par in range(2):
                    e = i * 2 + par
                    scores(i, par)
                    scatter(e, par)
                    if more:
                        pool.wait_ge(added, (e + 1) * NJ * 16)
                        fetch(i + 1, par)

            fetch(0, 0)
            fetch(0, 1)
            pair(0, True)
            with pool.Fori(1, EXP // 2 - 1) as i:
                pair(i, True)
            pair(EXP // 2 - 1, False)
            pool.wait_ge(added, EXP * NJ * 16)

        @block.tensor
        def _(pe):
            pe.wait_ge(ldi, 16)

            def turn(pair, par):
                e = pair * 2 + par
                """Gathered rows to channels by tokens."""
                pe.wait_ge(gathered[par], (pair + 1) * 16 * NJ)
                for nh in range(NH):
                    for half in range(2):
                        n = e * NX + nh * 2 + half
                        ge(pe, xt_done, n - 1)
                        for j in range(JH):
                            mm = pe.transpose(psO[0:DH, half, j * TT:(j + 1) * TT],
                                              xg[:, par, nh * JH + j, half * DH:(half + 1) * DH], ident3[0:TT, 0:TT])
                        mm.then_inc(xt_ready, 1)

            def expert(pair, par):
                e = pair * 2 + par
                pe.wait_ge(xt_done, (e + 1) * NX)
                pe.wait_ge(ldw[par], (pair + 1) * 48)
                for nh in range(NH):
                    for f in range(NF):
                        n = e * NP + nh * NF + f
                        k = (nh * NF + f) % 2
                        ge(pe, sg_done, n - 1)
                        for half in range(2):
                            pe.matmul(psS[:, k, 0:HT], wg[:, par, half, f * 128:(f + 1) * 128],
                                      xgT[:, half, nh * HT:(nh + 1) * HT], start=(half == 0), stop=(half == 1))
                        ge(pe, hid_done, n - 1)
                        for half in range(2):
                            mm = pe.matmul(psT[:, k, 0:HT], wu[:, par, half, f * 128:(f + 1) * 128],
                                           xgT[:, half, nh * HT:(nh + 1) * HT], start=(half == 0), stop=(half == 1))
                        mm.then_inc(g_ready, 1)

            def down(e, par):
                for j in range(NJ):
                    n = e * NJ + j
                    if j == 0:
                        pe.wait_ge(hid_done, e * NP + NF)
                    if j == JH:
                        pe.wait_ge(hid_done, (e + 1) * NP)
                    ge(pe, y_done, n - 1)
                    for f in range(NF):
                        mm = pe.matmul(psM[0:TT, j % 2, 0:D], hid[:, f, j * TT:(j + 1) * TT], wd[:, par, f, :],
                                       start=(f == 0), stop=(f == NF - 1))
                    mm.then_inc(y_ready, 1)

            def pair(i, more):
                expert(i, 0)
                turn(i, 1)
                down(i * 2, 0)
                expert(i, 1)
                if more:
                    turn(i + 1, 0)
                down(i * 2 + 1, 1)

            turn(0, 0)
            pair(0, True)
            with pe.Fori(1, EXP // 2 - 1) as i:
                pair(i, True)
            pair(EXP // 2 - 1, False)

        @block.scalar
        def _(act):
            def gates(e):
                for n in range(NP):
                    act.wait_ge(g_ready, e * NP + n + 1)
                    ge(act, hid_done, e * NP + max(n - 1, 0))
                    act.activation(sg[:, n % 2, :], psS[:, n % 2, 0:HT], ACT.Silu).then_inc(sg_done, 1)

            gates(0)
            with act.Fori(1, EXP) as e:
                gates(e)

        @block.vector
        def _(dve):
            def xt_copies(e):
                for n in range(NX):
                    nh, half = divmod(n, 2)
                    dve.wait_ge(xt_ready, e * NX + n + 1)
                    if n == 0:
                        ge(dve, g_ready, e * NP)
                    dve.tensor_copy(xgT[:, half, nh * HT:(nh + 1) * HT], psO[0:DH, half, 0:HT]).then_inc(xt_done, 1)

            def hidden(e):
                for n in range(NP):
                    nh, f = divmod(n, NF)
                    dve.wait_ge(sg_done, e * NP + n + 1)
                    if n == 0:
                        ge(dve, y_ready, e * NJ)
                    dve.tensor_tensor(hid[:, f, nh * HT:(nh + 1) * HT], sg[:, n % 2, :], psT[:, n % 2, 0:HT],
                                      ALU.mult).then_inc(hid_done, 1)

            def outs(e, par):
                dve.wait_ge(scr_done, e + 1)
                for j in range(NJ):
                    dve.wait_ge(y_ready, e * NJ + j + 1)
                    if j == 0:
                        ge(dve, added, (e - 1) * NJ * 16)
                    dve.tensor_scalar(yo[:, par, j, :], psM[0:TT, j % 2, 0:D], scr[:, par, j:j + 1], None,
                                      ALU.mult).then_inc(y_done, 1)

            def pair(i, more):
                hidden(i * 2)
                xt_copies(i * 2 + 1)
                outs(i * 2, 0)
                hidden(i * 2 + 1)
                if more:
                    xt_copies(i * 2 + 2)
                outs(i * 2 + 1, 1)

            xt_copies(0)
            pair(0, True)
            with dve.Fori(1, EXP // 2 - 1) as i:
                pair(i, True)
            pair(EXP // 2 - 1, False)
        blocks.close()
        clear(nc, sems)


S8 = 8
TL = -(-S // S8)
NR = 8
ROW = XS_W
C_H, C_P, C_V = D, 2 * D, 2 * D + 1
VEPS = 1e-12


class Consts4:

    def __init__(self, nc, ctx, d):
        def sb(name, shape):
            return ctx.enter_context(nc.sbuf_tensor(name, shape, F32))

        self.d = d
        self.ident = sb("ident4", [128, 128])
        self.wq1 = sb("wq1_sb", [DH, 2, D])
        self.wkv = sb("wkv_sb", [DH, 2, 2 * D])
        self.wp1 = sb("wp1_sb", [DH, 2, D])
        self.bp1 = sb("bp1_sb", [128, D])
        self.wr = sb("wr_sb", [DH, 2, NR])
        self.mask = sb("mask_sb", [128, 128])
        self.place = sb("place_sb", [128, TL])
        self.ld = ctx.enter_context(nc.semaphore("ld4"))
        self.all = [(self.ident, "idn"), (self.wq1, "wq1"), (self.wkv, "wkv"), (self.wp1, "wp1"), (self.bp1, "bp1"),
                    (self.wr, "wr"), (self.mask, "mask"), (self.place, "place")]

    def load(self, sp):
        for t, name in self.all:
            sp.dma_start(t[:], self.d[name]).then_inc(self.ld, 16)


def phase4(nc, d, c4, rows, hot8, psS, psT, psO, psM):
    with ExitStack() as ctx:
        def sb(name, shape, dt=F32):
            return ctx.enter_context(nc.sbuf_tensor(name, shape, dt))

        sems = []

        def sem(name):
            sems.append(ctx.enter_context(nc.semaphore(name)))
            return sems[-1]

        ident, wq1, wkv, wp1, bp1, wr, mask, place = c4.ident, c4.wq1, c4.wkv, c4.wp1, c4.bp1, c4.wr, c4.mask, c4.place
        ld, CONSTS = c4.ld, c4.all
        mh = sb("mh4", [128, H])
        ep = sb("ep4", [128, 1])
        hin = sb("hin", [128, 2, D])
        hb1 = sb("hb1", [128, 4, D])
        sta, mva, rsa = sb("sta", [128, 6]), sb("mva", [128, 2]), sb("rsa", [128, 1])
        xn2 = sb("xn2", [128, D])
        xT = sb("xT4", [DH, 2, 128])
        xq = sb("xq", [DH, 2, 128])
        ksb = sb("ksb", [128, D])
        va = sb("va4", [128, 4, H, 32])
        prod = sb("prod", [128, D])
        s0 = sb("s0", [128, 128])
        sq = sb("sq", [128, D])
        ss = sb("ss", [128, H])
        ssm = sb("ssm", [128, H])
        rn = sb("rn", [128, H])
        vnp = sb("vnp", [128, H, 32])
        vnT = sb("vnT", [128, NG, 128])
        m0 = sb("m0", [H, S8])
        d0 = sb("d0", [H, 128])
        e0 = sb("e0", [128, 128])
        PT = sb("PT", [128, 2, 4, NG, 128])
        oraw = sb("oraw4", [128, NG * 128])
        rs = sb("rs4", [128, H])
        on = sb("on4", [128, D])
        oT = sb("oT4", [DH, 2, 128])
        stc, mvc, rsc = sb("stc", [128, 6]), sb("mvc", [128, 2]), sb("rsc", [128, 1])
        row = sb("row4", [128, 4, ROW])
        x3T = sb("x3T", [DH, 2, 128])
        nlm = sb("nlm", [128, 1])
        er = sb("er", [128, NR])
        es = sb("es", [128, 1])
        eqm = sb("eqm", [128, NR])
        cum = sb("cum", [128, NR])

        names = ["xt", "kv", "q0", "vt", "sc", "et", "av", "back", "ot", "pj", "x3", "lg"]
        ready = {n: sem(f"{n}_rdy4") for n in names}
        pool_set = sem("pool_set4")
        h_in, row_out = ([sem(f"{n}{slot}") for slot in range(k)] for n, k in (("h_in", 2), ("row_out", 4)))
        sta_d, rsa_d, xn_d, hb_d = sem("sta_d"), sem("rsa_d"), sem("xn_d"), sem("hb_d")
        xT_d, k_d, v_d, s0_d, sq_d, ss_d, vnp_d = (sem(n) for n in ("xT_d", "k_d", "v_d", "s0_d", "sq_d", "ss_d", "vnp_d"))
        vt_d, d0_d, e0_d, exp_d, mask_p, mask_v, pt_d = (sem(n) for n in ("vt_d", "d0_d", "e0_d", "exp_d", "mask_p", "mask_v", "pt_d"))
        oraw_d, on_d, oT_d, h4_d, stc_d, rsc_d, row_d = (sem(n) for n in ("oraw_d", "on_d", "oT_d", "h4_d", "stc_d", "rsc_d", "row_d"))
        x3_d, lg_m, lg_e, p_d, pl_d = (sem(n) for n in ("x3_d", "lg_m", "lg_e", "p_d", "pl_d"))

        O0, O1, M0, M1 = psO[:, 0, :], psO[:, 1, :], psM[:, 0, :], psM[:, 1, :]

        def run(eng, step):
            for i in range(7):
                step(i, i % 4, True, i >= 1, i >= 2, i >= 3, i >= 4)
            with eng.Fori(0, (TL - 7) // 4) as k:
                for r in range(4):
                    step(k * 4 + 7 + r, (3 + r) % 4, True, True, True, True, True)
            for i in range(TL, TL + 4):
                step(i, i % 4, False, i <= TL, i <= TL + 1, i <= TL + 2, True)

        blocks = ctx.enter_context(ExitStack())
        block = blocks.enter_context(nc.Block())

        @block.sync
        def _(sp):
            def load(i, r):
                sp.dma_start(hin[:, r % 2, :], d["h3"][:, bass.ds(i * S8, S8), :]).then_inc(h_in[r % 2], 16)

            def store(j, q):
                sp.wait_ge(p_d, j + 1)
                sp.wait_ge(pl_d, j + 1)
                sp.dma_start(rows[:, j, :], row[:, q, :]).then_inc(row_out[q], 16)

            load(0, 0)

            def step(i, r, a, b, e, c, dd):
                if a:
                    ge(sp, hb_d, i)
                    ge(sp, xn_d, i)
                    load(i + 1, (r + 1) % 4)
                if not isinstance(i, int) or i >= 6:
                    store(i - 6, (r + 2) % 4)
            run(sp, step)
            for j in range(TL - 2, TL):
                store(j, j % 4)
            for q in range(4):
                sp.wait_ge(row_out[q], 16 * len(range(q, TL, 4)))

        @block.gpsimd
        def _(pool):
            pool.memset(mh[:], -0.5)
            pool.memset(ep[:], EPS)
            pool.memset(va[:], 0.0)
            pool.drain()
            pool.memset(va[:, :, :, HD:VA], 1.0)
            pool.memset(vnp[:], 0.0)
            pool.memset(s0[:], 0.0)
            pool.memset(e0[:], 0.0)
            pool.memset(row[:], 0.0)
            pool.drain().then_inc(pool_set, 1)
            pool.wait_ge(ld, 16 * len(CONSTS))

            def rstd(var, out):
                pool.tensor_tensor(out, var, ep[:], ALU.add)
                pool.drain()
                return pool.tensor_tensor(out, out, mh[:, 0:1], ALU.pow)

            def first(i):
                pool.wait_ge(sta_d, i + 1)
                rstd(mva[:, 1:2], rsa[:]).then_inc(rsa_d, 1)

            first(0)

            def step(i, r, a, b, e, c, dd):
                if e:
                    j, p = i - 2, r % 2
                    pool.wait_ge(exp_d, 2 * j + 1)
                    pool.tensor_tensor(PT[:, p, 0:2].rearrange("p r g n -> p (r g) n"), PT[:, p, 0:2].rearrange("p r g n -> p (r g) n"),
                                       mask[:].unsqueeze(1).broadcast_to([128, 2 * NG, 128]), ALU.mult).then_inc(mask_p, 1)
                if dd:
                    j = i - 4
                    pool.tensor_copy(row[:, r, C_V:C_V + 1], place[:, bass.ds(j, 1)]).then_inc(pl_d, 1)
                if a:
                    first(i + 1)
                    pool.wait_ge(xn_d, i + 1)
                    ge(pool, h4_d, i - 3)
                    pool.tensor_tensor(hb1[:, r, :], hin[:, r % 2, :], bp1[:], ALU.add).then_inc(hb_d, 1)
                if a:
                    pool.wait_ge(v_d, i + 1)
                    pool.tensor_tensor(sq[:].rearrange("p (h e) -> p h e", e=HD), va[:, r, :, 0:HD], va[:, r, :, 0:HD], ALU.mult).then_inc(sq_d, 1)
                    pool.wait_ge(ss_d, i + 1)
                    pool.tensor_tensor(rn[:], ssm[:], mh[:], ALU.pow)
                    pool.drain()
                    ge(pool, ready["vt"], i)
                    pool.tensor_tensor(vnp[:, :, 0:HD], va[:, r, :, 0:HD], rn[:].unsqueeze(2).broadcast_to([128, H, HD]),
                                       ALU.mult).then_inc(vnp_d, 1)
                if c:
                    pool.wait_ge(stc_d, i - 3 + 1)
                    rstd(mvc[:, 1:2], rsc[:]).then_inc(rsc_d, 1)
            run(pool, step)

        @block.tensor
        def _(pe):
            pe.wait_ge(ld, 16 * len(CONSTS))
            pe.wait_ge(pool_set, 1)

            def two(out, lhs, rhs):
                pe.matmul(out, lhs(0), rhs(0), start=True, stop=False)
                return pe.matmul(out, lhs(1), rhs(1), start=False, stop=True)

            def turn2(out, src):
                pe.transpose(out[0:DH, 0:128], src[:, 0:DH], ident[:])
                return pe.transpose(out[0:DH, 128:256], src[:, DH:D], ident[:])

            def cosines(ps, quads):
                for g in range(NG):
                    for q in quads:
                        v = vnT[32 * q:32 * q + HD, g, :]
                        mm = pe.matmul(ps[:, q % 2, g * 128:(g + 1) * 128], v, v, start=True, stop=True)
                mm.then_inc(ready["sc"], 1)

            def step(i, r, a, b, e, c, dd):
                if c:
                    j, q, p = i - 3, (r + 1) % 4, (r + 1) % 2
                    pe.wait_ge(pt_d, j + 1)
                    ge(pe, h4_d, j)
                    for h in range(H):
                        g, quad = divmod(h, 4)
                        mm = pe.matmul(O0[32 * quad:32 * quad + 32, g * 128:(g + 1) * 128], va[:, q, h, :], PT[:, p, quad, g, :],
                                       start=True, stop=True)
                    mm.then_inc(ready["av"], 1)
                if dd:
                    pe.wait_ge(row_d, i - 4 + 1)
                    ge(pe, x3_d, i - 4)
                    pe.wait_ge(v_d, min(i, TL) if isinstance(i, int) else i)
                    pe.wait_ge(k_d, min(i, TL) if isinstance(i, int) else i)
                    turn2(M0[:, 256:512], row[:, r, :]).then_inc(ready["x3"], 1)
                if a:
                    pe.wait_ge(xn_d, i + 1)
                    ge(pe, v_d, i)
                    ge(pe, k_d, i)
                    turn2(M0, xn2).then_inc(ready["xt"], 1)
                if b:
                    j = i - 1
                    pe.wait_ge(vnp_d, j + 1)
                    pe.wait_ge(s0_d, j + 1)
                    ge(pe, lg_e, i - 4)
                    ge(pe, lg_m, i - 4)
                    for g in range(NG):
                        pe.transpose(O1[:, g * 128:(g + 1) * 128], vnp[:, 4 * g:4 * g + 4, :].rearrange("p h e -> p (h e)"), ident[:])
                    pe.transpose(O1[:, 384:512], s0[:], ident[:]).then_inc(ready["vt"], 1)
                if c:
                    pe.wait_ge(oraw_d, i - 3 + 1)
                    for g in range(NG):
                        mm = pe.transpose(O0[:, g * 128:(g + 1) * 128], oraw[:, g * 128:(g + 1) * 128], ident[:])
                    mm.then_inc(ready["back"], 1)
                if a:
                    pe.wait_ge(xT_d, i + 1)
                    ge(pe, x3_d, i - 4 + 1)
                    two(M0[:, 0:2 * D], lambda k: xT[:, k, :], lambda k: wkv[:, k, :]).then_inc(ready["kv"], 1)
                    ge(pe, pt_d, i - 1)
                    two(M1[:, 0:D], lambda k: xq[:, k, :], lambda k: wq1[:, k, :]).then_inc(ready["q0"], 1)
                if dd:
                    pe.wait_ge(x3_d, i - 4 + 1)
                    if b:
                        pe.wait_ge(d0_d, i - 1 + 1)
                    else:
                        pe.wait_ge(lg_m, i - 4)
                        pe.wait_ge(lg_e, i - 4)
                    two(O1[:, 0:NR], lambda k: x3T[:, k, :], lambda k: wr[:, k, :]).then_inc(ready["lg"], 1)
                if c:
                    pe.wait_ge(on_d, i - 3 + 1)
                    turn2(O0, on).then_inc(ready["ot"], 1)
                if b:
                    pe.wait_ge(vt_d, i - 1 + 1)
                    ge(pe, exp_d, 2 * (i - 1))
                    cosines(psS, (0, 1))
                if c:
                    pe.wait_ge(oT_d, i - 3 + 1)
                    two(O0[:, 0:D], lambda k: oT[:, k, :], lambda k: wp1[:, k, :]).then_inc(ready["pj"], 1)
                if b:
                    cosines(psT, (2, 3))
                    pe.wait_ge(e0_d, i - 1 + 1)
                    if a:
                        pe.wait_ge(s0_d, i + 1)
                    pe.transpose(M1[:, 0:128], e0[:], ident[:]).then_inc(ready["et"], 1)
            run(pe, step)

        @block.scalar
        def _(act):
            def step(i, r, a, b, e, c, dd):
                if e:
                    j = i - 2
                    ge(act, ready["av"], i - 3)
                    for n, ps in ((0, psS), (1, psT)):
                        act.wait_ge(ready["sc"], 2 * j + n + 1)
                        act.activation(PT[:, r % 2, 2 * n:2 * n + 2].rearrange("p r g n -> p r (g n)"), ps[:, :, 0:NG * 128],
                                       ACT.Exp, scale=SCALE).then_inc(exp_d, 1)
                if c:
                    act.wait_ge(ready["av"], i - 3 + 1)
                    ge(act, ready["back"], i - 3)
                    act.copy(oraw[:], O0[:, 0:NG * 128]).then_inc(oraw_d, 1)
                if a:
                    act.wait_ge(ready["xt"], i + 1)
                    ge(act, ready["q0"], i)
                    act.copy(xT[:].rearrange("p k n -> p (k n)"), M0[0:DH, 0:256])
                    act.copy(xq[:].rearrange("p k (b s) -> p k b s", s=S8),
                             M0[0:DH, 0:256].rearrange("p (k n) -> p k n", k=2)[:, :, 0:S8].unsqueeze(2).broadcast_to([DH, 2, B, S8]))
                    act.drain().then_inc(xT_d, 1)
                if dd:
                    act.wait_ge(ready["x3"], i - 4 + 1)
                    ge(act, ready["lg"], i - 4)
                    act.copy(x3T[:].rearrange("p k n -> p (k n)"), M0[0:DH, 256:512]).then_inc(x3_d, 1)
                if a:
                    act.wait_ge(ready["kv"], i + 1)
                    ge(act, ready["av"], i - 3)
                    act.copy(va[:, r, :, 0:HD], M0[:, D:2 * D].rearrange("p (h e) -> p h e", e=HD)).then_inc(v_d, 1)
                    ge(act, s0_d, i)
                    act.copy(ksb[:], M0[:, 0:D]).then_inc(k_d, 1)
                if b:
                    act.wait_ge(d0_d, i - 1 + 1)
                    ge(act, ready["et"], i - 1)
                    act.activation(e0[0:H, :], d0[:], ACT.Exp, scale=SCALE).then_inc(e0_d, 1)
                if c:
                    act.wait_ge(ready["ot"], i - 3 + 1)
                    ge(act, ready["pj"], i - 3)
                    act.copy(oT[:].rearrange("p k n -> p (k n)"), O0[0:DH, 0:256]).then_inc(oT_d, 1)
                if dd:
                    act.wait_ge(lg_m, i - 4 + 1)
                    ge(act, p_d, i - 4)
                    act.activation(er[:], O1[:, 0:NR], ACT.Exp, bias=nlm[:]).then_inc(lg_e, 1)
            run(act, step)

        @block.vector
        def _(dve):
            dve.wait_ge(pool_set, 1)
            dve.wait_ge(ld, 16 * len(CONSTS))

            def stats(i, r, turn):
                dve.wait_ge(h_in[r % 2], turn)
                ge(dve, rsa_d, i)
                dve.bn_stats(sta[:], hin[:, r % 2, :])
                dve.drain()
                dve.bn_aggr(mva[:], sta[:]).then_inc(sta_d, 1)

            def norm(i, r):
                dve.wait_ge(rsa_d, i + 1)
                ge(dve, ready["xt"], i)
                dve.tensor_scalar(xn2[:], hin[:, r % 2, :], mva[:, 0:1], rsa[:], ALU.subtract, ALU.mult).then_inc(xn_d, 1)

            stats(0, 0, 16)
            norm(0, 0)

            def step(i, r, a, b, e, c, dd):
                if a:
                    p = (r + 1) % 2
                    turn = (i + 1 - p) * 8 + 16
                    stats(i + 1, (r + 1) % 4, turn)
                if dd:
                    j = i - 4
                    dve.wait_ge(rsc_d, j + 1)
                    dve.tensor_scalar(row[:, r, 0:D], row[:, r, C_H:C_H + D], mvc[:, 0:1], rsc[:], ALU.subtract, ALU.mult).then_inc(row_d, 1)
                if e:
                    j, p = i - 2, r % 2
                    dve.wait_ge(exp_d, 2 * j + 2)
                    dve.tensor_tensor(PT[:, p, 2:4].rearrange("p r g n -> p (r g) n"), PT[:, p, 2:4].rearrange("p r g n -> p (r g) n"),
                                      mask[:].unsqueeze(1).broadcast_to([128, 2 * NG, 128]), ALU.mult).then_inc(mask_v, 1)
                    dve.wait_ge(mask_v, j + 1)
                    dve.wait_ge(mask_p, j + 1)
                    dve.wait_ge(ready["et"], j + 1)
                    for q in range(4):
                        dve.tensor_tensor(PT[:, p, q, :, 0:S8],
                                          M1[:, 0:H].rearrange("p (g r) -> p g r", r=4)[:, :, q:q + 1].broadcast_to([128, NG, S8]),
                                          mask[:, 0:S8].unsqueeze(1).broadcast_to([128, NG, S8]), ALU.mult)
                    dve.drain().then_inc(pt_d, 1)
                if a:
                    norm(i + 1, (r + 1) % 4)
                if b:
                    j = i - 1
                    dve.wait_ge(ready["vt"], j + 1)
                    ge(dve, ready["sc"], 2 * j)
                    dve.tensor_copy(vnT[:].rearrange("p g n -> p (g n)"), O1[:, 0:NG * 128]).then_inc(vt_d, 1)
                    x = O1[0:H, 384:512].rearrange("p (b s) -> p b s", s=S8)
                    dve.tensor_reduce(m0[:], x.rearrange("p b s -> p s b"), AX.X, ALU.max)
                    dve.drain()
                    ge(dve, e0_d, j)
                    dve.tensor_tensor(d0[:].rearrange("p (b s) -> p b s", s=S8), x, m0[:].unsqueeze(1).broadcast_to([H, B, S8]),
                                      ALU.subtract).then_inc(d0_d, 1)
                if c:
                    j = i - 3
                    dve.wait_ge(ready["back"], j + 1)
                    o = O0[:, 0:NG * 128].rearrange("p (h e) -> p h e", e=32)
                    dve.reciprocal(rs[:], o[:, :, HD])
                    dve.drain()
                    ge(dve, ready["ot"], j)
                    dve.tensor_tensor(on[:].rearrange("p (h e) -> p h e", e=HD), o[:, :, 0:HD],
                                      rs[:].unsqueeze(2).broadcast_to([128, H, HD]), ALU.mult).then_inc(on_d, 1)
                if a:
                    dve.wait_ge(sq_d, i + 1)
                    dve.tensor_reduce(ss[:], sq[:].rearrange("p (h e) -> p h e", e=HD), AX.X, ALU.add)
                    dve.drain()
                    ge(dve, vnp_d, i)
                    dve.tensor_scalar(ssm[:], ss[:], VEPS, None, ALU.max).then_inc(ss_d, 1)
                    dve.wait_ge(k_d, i + 1)
                    dve.wait_ge(ready["q0"], i + 1)
                    dve.tensor_tensor(prod[:], M1[:, 0:D], ksb[:], ALU.mult)
                    dve.drain()
                    ge(dve, ready["vt"], i)
                    dve.tensor_reduce(s0[:, 0:H], prod[:].rearrange("p (h e) -> p h e", e=HD), AX.X, ALU.add).then_inc(s0_d, 1)
                if dd:
                    j = i - 4
                    dve.wait_ge(ready["lg"], j + 1)
                    ge(dve, lg_e, j)
                    dve.tensor_reduce(nlm[:], O1[:, 0:NR], AX.X, ALU.max, negate=True)
                    dve.drain()
                    dve.tensor_scalar(eqm[:], O1[:, 0:NR], nlm[:], 0.0, ALU.add, ALU.is_equal).then_inc(lg_m, 1)
                    dve.drain()
                    dve.tensor_tensor_scan(cum[:], eqm[:], eqm[:], 0.0, ALU.add, ALU.max)
                    dve.drain()
                    dve.scalar_tensor_tensor(out=hot8[:, j, :], in0=cum[:], scalar=1.0, in1=eqm[:], op0=ALU.is_le, op1=ALU.mult)
                    dve.wait_ge(lg_e, j + 1)
                    dve.tensor_reduce(es[:], er[:], AX.X, ALU.add)
                    dve.drain()
                    dve.reciprocal(row[:, r, C_P:C_P + 1], es[:]).then_inc(p_d, 1)
                if c:
                    j, q = i - 3, (r + 1) % 4
                    dve.wait_ge(ready["pj"], j + 1)
                    ge(dve, row_out[q], 4 * (j - q))
                    ge(dve, hb_d, j + 1)
                    dve.tensor_tensor(row[:, q, C_H:C_H + D], O0[:, 0:D], hb1[:, q, :], ALU.add).then_inc(h4_d, 1)
                    dve.drain()
                    dve.bn_stats(stc[:], row[:, q, C_H:C_H + D])
                    dve.drain()
                    dve.bn_aggr(mvc[:], stc[:]).then_inc(stc_d, 1)
            run(dve, step)
        blocks.close()
        clear(nc, sems)


TOK = B * S
LANES = 128
XT5 = XS_TILES


def phase5(nc, d, rows, hot8, wi, wo, w_in, psS, psT, psO, psM):
    with ExitStack() as ctx:
        def sb(name, shape, dt=F32):
            return ctx.enter_context(nc.sbuf_tensor(name, shape, dt))

        def sem(name):
            return ctx.enter_context(nc.semaphore(name))

        ident = sb("ident5", [128, 128])
        before = sb("before", [128, 128])
        ones = sb("ones5", [128, 128])
        tot = sb("tot5", [128, TL, NR])
        inc = sb("inc5", [128, NR, TL])
        cnt = sb("cnt5", [128, NR], I32)
        tls = sb("tls5", [128, NR], I32)
        tlf = sb("tlf5", [128, NR])
        cumt = sb("cumt5", [128, NR])
        base = sb("base5", [128, NR])
        offs = sb("offs5", [128, TL, NR])
        offm = sb("offm5", [128, TL, NR])
        posi = sb("posi5", [128, TL], I32)
        tix = sb("tix5", [128, XT5])
        lte = sb("lte5", [128, XT5, NR])
        tef = sb("tef5", [128, XT5])
        tei = sb("tei5", [128, XT5], I32)
        xr = sb("xr5", [128, 4, ROW])
        xT = sb("xT5", [DH, 2, 128])
        hd = sb("hd5", [128, F])
        hT = sb("hT5", [128, NF, 128])
        spare = sb("spare5", [128, 4, 2])
        yo = sb("yo5", [128, 4, D])
        oidx = sb("oidx5", [128, 4], I32)

        ld, pool_set, sums, cnts, pos_d, te_d = sem("ld5"), sem("pset5"), sem("sums5"), sem("cnts5"), sem("pos_d5"), sem("te_d5")
        sorted_, x_in, out_d = sem("sorted5"), [sem(f"x_in5{n}") for n in range(4)], [sem(f"out_d5{n}") for n in range(4)]
        held = sem("held5")
        xt_r, xt_d, h_r, h_d0, h_d1, t_r, t_d0, t_d1, y_r, y_d = (sem(n + "5") for n in (
            "xt_r", "xt_d", "h_r", "h_d0", "h_d1", "t_r", "t_d0", "t_d1", "y_r", "y_d"))

        def run(eng, step):
            for i in range(8):
                step(i, i % 4, i // 4, True, i >= 1, i >= 2, i >= 3)
            with eng.Fori(2, XT5 // 4) as k:
                for r in range(4):
                    step(k * 4 + r, r, k, True, True, True, True)
            for i in range(XT5, XT5 + 3):
                step(i, i % 4, i // 4, False, i <= XT5, i <= XT5 + 1, True)

        def turn_of(turn, r, lag):
            return turn if r >= lag else turn - 1

        block = ctx.enter_context(nc.Block())

        @block.sync
        def _(sp):
            sp.dma_start(ident[:], d["idn"]).then_inc(ld, 16)
            sp.dma_start(before[:], d["before"]).then_inc(ld, 16)
            sp.wait_ge(sorted_, 16 * TL)

            def step(i, r, turn, a, b, c, dd):
                if a:
                    ge(sp, y_d, i - 3)
                    sp.dma_start(xr[:, r, :], d["xs"][bass.ds(i * 128, 128), :]).then_inc(x_in[r], 16)
            run(sp, step)

        @block.gpsimd
        def _(pool):
            pool.memset(ones[:], 1.0)
            pool.memset(spare[:], 0.0)
            pool.iota(tix[:], [[1, XT5]], base=0, channel_multiplier=0, allow_small_or_imprecise_dtypes=True)
            pool.drain().then_inc(pool_set, 1)
            pool.wait_ge(pos_d, 1)
            for i in range(TL):
                pool.indirect_dma_start(out=d["xs"], out_offset=bass.IndirectOffsetOnAxis(ap=posi[:, i:i + 1], axis=0),
                                        in_=rows[:, i, :], in_offset=None).then_inc(sorted_, 16)

            def step(i, r, turn, a, b, c, dd):
                if dd:
                    q = (r + 1) % 4
                    pool.wait_ge(y_d, i - 3 + 1)
                    ge(pool, held, i - 3)
                    pool.tensor_tensor(spare[:, q, 1:2], spare[:, q, 0:1], spare[:, q, 0:1], ALU.add).then_inc(held, 1)
                    pool.indirect_dma_start(out=d["out"], out_offset=bass.IndirectOffsetOnAxis(ap=oidx[:, q:q + 1], axis=0),
                                            in_=yo[:, q, :], in_offset=None, bounds_check=TOK - 1, oob_is_err=False
                                            ).then_inc(out_d[q], 16)
            run(pool, step)
            for q in range(4):
                pool.wait_ge(out_d[q], 16 * (XT5 // 4))

        @block.tensor
        def _(pe):
            pe.wait_ge(ld, 32)
            pe.wait_ge(pool_set, 1)
            flat = hot8[:].rearrange("p t e -> p (t e)")
            pe.matmul(psS[:, 0, 0:TL * NR], before[:], flat, start=True, stop=True)
            pe.matmul(psT[:, 0, 0:TL * NR], ones[:], flat, start=True, stop=True).then_inc(sums, 1)
            pe.wait_ge(te_d, 1)
            for s, n in w_in:
                pe.wait_ge(s, n)

            def step(i, r, turn, a, b, c, dd):
                if dd:
                    j = i - 3
                    e = pe.value_load(tei[0:1, bass.ds(j, 1)], min_val=0, max_val=NR - 1)
                    pe.wait_ge(t_d0, j + 1)
                    pe.wait_ge(t_d1, j + 1)
                    ge(pe, y_d, j - 1)
                    for f in range(NF):
                        mm = pe.matmul(psO[:, (r + 1) % 2, 0:D], hT[:, f, :], wo[:, f, bass.ds(e * D, D)],
                                       start=(f == 0), stop=(f == NF - 1))
                    mm.then_inc(y_r, 1)
                if c:
                    j = i - 2
                    pe.wait_ge(h_d0, j + 1)
                    pe.wait_ge(h_d1, j + 1)
                    ge(pe, t_d0, j)
                    ge(pe, t_d1, j)
                    for f in range(NF):
                        mm = pe.transpose(psT[:, f // 3, (f % 3) * 128:(f % 3 + 1) * 128], hd[:, f * 128:(f + 1) * 128], ident[:])
                    mm.then_inc(t_r, 1)
                if b:
                    j = i - 1
                    e = pe.value_load(tei[0:1, bass.ds(j, 1)], min_val=0, max_val=NR - 1)
                    pe.wait_ge(xt_d, j + 1)
                    ge(pe, h_d0, j)
                    ge(pe, h_d1, j)
                    for n in range(2):
                        for k in range(2):
                            mm = pe.matmul(psS[:, n, 0:F // 2], xT[:, k, :], wi[:, k, bass.ds(e * F + n * (F // 2), F // 2)],
                                           start=(k == 0), stop=(k == 1))
                    mm.then_inc(h_r, 1)
                if a:
                    pe.wait_ge(x_in[r], 16 * turn + 16)
                    ge(pe, xt_d, i)
                    for k in range(2):
                        mm = pe.transpose(psM[0:DH, 0, k * 128:(k + 1) * 128], xr[:, r, k * DH:(k + 1) * DH], ident[:])
                    mm.then_inc(xt_r, 1)
            run(pe, step)

        @block.scalar
        def _(act):
            def step(i, r, turn, a, b, c, dd):
                if c:
                    act.wait_ge(t_r, i - 2 + 1)
                    ge(act, y_r, i - 2)
                    act.copy(hT[:, 0:3].rearrange("p f n -> p (f n)"), psT[:, 0, 0:3 * 128]).then_inc(t_d0, 1)
                if b:
                    act.wait_ge(h_r, i - 1 + 1)
                    ge(act, t_r, i - 1)
                    act.activation(hd[:, 0:F // 2], psS[:, 0, 0:F // 2], ACT.Relu).then_inc(h_d0, 1)
                if a:
                    act.wait_ge(xt_r, i + 1)
                    ge(act, h_r, i)
                    act.copy(xT[:].rearrange("p k n -> p (k n)"), psM[0:DH, 0, 0:256]).then_inc(xt_d, 1)
            run(act, step)

        @block.vector
        def _(dve):
            dve.wait_ge(pool_set, 1)
            dve.wait_ge(sums, 1)
            dve.tensor_copy(tot[:].rearrange("p t e -> p (t e)"), psT[:, 0, 0:TL * NR])
            dve.drain()
            for e in range(NR):
                dve.tensor_tensor_scan(inc[:, e, :], tot[:, :, e], tot[:, :, e], 0.0, ALU.add, ALU.max)
            dve.drain()
            dve.tensor_scalar(cnt[:], inc[:, :, TL - 1], float(LANES - 1), None, ALU.add)
            dve.drain()
            dve.tensor_scalar(tls[:], cnt[:], LANES.bit_length() - 1, None, ALU.logical_shift_right)
            dve.drain()
            dve.tensor_copy(tlf[:], tls[:])
            dve.drain()
            dve.tensor_tensor_scan(cumt[:], tlf[:], tlf[:], 0.0, ALU.add, ALU.max)
            dve.drain()
            dve.tensor_tensor(base[:], cumt[:], tlf[:], ALU.subtract)
            dve.tensor_tensor(offs[:], inc[:].rearrange("p e t -> p t e"), tot[:], ALU.subtract)
            dve.tensor_tensor(lte[:], cumt[:].unsqueeze(1).broadcast_to([128, XT5, NR]), tix[:].unsqueeze(2).broadcast_to([128, XT5, NR]), ALU.is_le)
            dve.drain()
            dve.tensor_scalar(base[:], base[:], float(LANES), None, ALU.mult)
            dve.tensor_tensor(offs[:].rearrange("p t e -> p (t e)"), offs[:].rearrange("p t e -> p (t e)"), psS[:, 0, 0:TL * NR], ALU.add)
            dve.tensor_reduce(tef[:], lte[:], AX.X, ALU.add)
            dve.drain()
            dve.tensor_tensor(offm[:], offs[:], base[:].unsqueeze(1).broadcast_to([128, TL, NR]), ALU.add)
            dve.tensor_scalar(tei[:], tef[:], float(NR - 1), None, ALU.min)
            dve.drain().then_inc(te_d, 1)
            dve.tensor_tensor(offm[:], offm[:], hot8[:], ALU.mult)
            dve.drain()
            dve.tensor_reduce(offs[:, :, 0], offm[:], AX.X, ALU.add)
            dve.drain()
            dve.tensor_copy(posi[:], offs[:, :, 0]).then_inc(pos_d, 1)

            def step(i, r, turn, a, b, c, dd):
                if dd:
                    j, q = i - 3, (r + 1) % 4
                    dve.wait_ge(y_r, j + 1)
                    ge(dve, out_d[q], 16 * turn_of(turn, r, 3))
                    dve.tensor_scalar(oidx[:, q:q + 1], xr[:, q, C_V:C_V + 1], -1.0, float(TOK), ALU.mult, ALU.add)
                    dve.scalar_tensor_tensor(out=yo[:, q, :], in0=psO[:, q % 2, 0:D], scalar=xr[:, q, C_P:C_P + 1],
                                             in1=xr[:, q, C_H:C_H + D], op0=ALU.mult, op1=ALU.add)
                    dve.drain().then_inc(y_d, 1)
                if c:
                    dve.wait_ge(t_r, i - 2 + 1)
                    ge(dve, y_r, i - 2)
                    dve.tensor_copy(hT[:, 3:6].rearrange("p f n -> p (f n)"), psT[:, 1, 0:3 * 128]).then_inc(t_d1, 1)
                if b:
                    dve.wait_ge(h_r, i - 1 + 1)
                    ge(dve, t_r, i - 1)
                    dve.tensor_scalar(hd[:, F // 2:F], psS[:, 1, 0:F // 2], 0.0, None, ALU.max).then_inc(h_d1, 1)
            run(dve, step)


def program(nc, d):
    with ExitStack() as ctx:
        psS, psT, psO, psM = (ctx.enter_context(nc.psum_tensor(n, [128, 2, 512], F32)) for n in ("psS", "psT", "psO", "psM"))
        phase1(nc, d, psS, psT, psO, psM)
        w_in = ctx.enter_context(nc.semaphore("w_in"))
        wi = ctx.enter_context(nc.sbuf_tensor("wi_sb", [DH, 2, NR * F], F32))
        wo = ctx.enter_context(nc.sbuf_tensor("wo_sb", [128, NF, NR * D], F32))
        c4 = Consts4(nc, ctx, d)
        with nc.sbuf_tensor("gidx", [TT, EXP, NJ], I32) as gidx:
            phase2(nc, d, gidx, psS, psT, psO, psM)
            phase3(nc, d, gidx, wi, wo, w_in, c4.load, psS, psT, psO, psM)
        rows = ctx.enter_context(nc.sbuf_tensor("rows", [128, TL, ROW], F32))
        hot8 = ctx.enter_context(nc.sbuf_tensor("hot8", [128, TL, NR], F32))
        phase4(nc, d, c4, rows, hot8, psS, psT, psO, psM)
        phase5(nc, d, rows, hot8, wi, wo, [(w_in, 32)], psS, psT, psO, psM)


def halves(w):
    return np.ascontiguousarray(w.reshape((2, DH) + w.shape[1:]).swapaxes(0, 1))


def blocks(w, p):
    return np.ascontiguousarray(w.reshape((w.shape[0] // p, p) + w.shape[1:]).swapaxes(0, 1))


def waves(n):
    a = 2 * np.pi * (np.outer(np.arange(n), np.arange(n)) % n) / n
    return np.cos(a).astype(np.float32), np.sin(a).astype(np.float32)


def lay_out(a):
    rep = lambda v, n: np.ascontiguousarray(np.broadcast_to(v, (n, v.shape[-1])))
    x = np.zeros((B, DH, 2, S_IN + 2 * PAD), np.float32)
    x[:, :, :, PAD:PAD + S_IN] = a["x"].reshape(B, S_IN, 2, DH).transpose(0, 3, 2, 1)
    cd, sd = waves(D)
    cs, ss = waves(S)
    qkv, qkv1 = a["L0_attn_qkv_w"], a["L1_attn_w_qkv"]
    rel = a["L0_attn_rel_table"]
    reach = rel.shape[0] // 2
    shift = np.arange(RELW)[None, :] - (NT - 1) * TT - np.arange(TT)[:, None]
    d = {
        "x": x,
        "wdw": halves(a["L0_tok_w_dw"][:, 0, :]), "bdw": halves(a["L0_tok_b_dw"]),
        "wpw": halves(a["L0_tok_w_pw"][:, :, 0].T), "bpw": halves(a["L0_tok_b_pw"]),
        "dftd": halves(np.concatenate([cd, sd], 1)), "dftc": blocks(cs, TT), "dfts": blocks(-ss, TT),
        "gam": rep(a["L0_tok_gamma"], TT), "bet": rep(a["L0_tok_beta"], TT), "pjb": rep(a["L0_attn_proj_b"], TT),
        "wq": halves(qkv[:D].T), "wk": halves(qkv[D:2 * D].T), "wv": halves(qkv[2 * D:].T),
        "wpj": halves(a["L0_attn_proj_w"].T),
        "rel": np.ascontiguousarray(rel[np.clip(shift + reach, 0, 2 * reach)].transpose(0, 2, 1)),
        "wgt": halves(a["L0_ffn_gate_weight"].T),
        "wsg": halves(a["L0_ffn_Ws_g"].T), "wsu": halves(a["L0_ffn_Ws_u"].T), "wsd": blocks(a["L0_ffn_Ws_d"].T, 128),
        "wg": np.ascontiguousarray(a["L0_ffn_Wg"].transpose(0, 2, 1).reshape(EXP, 2, DH, F).transpose(0, 2, 1, 3)),
        "wu": np.ascontiguousarray(a["L0_ffn_Wu"].transpose(0, 2, 1).reshape(EXP, 2, DH, F).transpose(0, 2, 1, 3)),
        "wd": np.ascontiguousarray(a["L0_ffn_Wd"].transpose(0, 2, 1).reshape(EXP, NF, 128, D).transpose(0, 2, 1, 3)),
        "wq1": halves(qkv1[:D].T), "wkv": halves(qkv1[D:].T), "wp1": halves(a["L1_attn_w_proj"].T),
        "bp1": rep(a["L1_attn_b_proj"], 128), "wr": halves(a["L1_ffn_router_w"]),
        "wi": np.ascontiguousarray(a["L1_ffn_wi"].reshape(NR, 2, DH, F).transpose(2, 1, 0, 3).reshape(DH, 2, NR * F)),
        "wo": np.ascontiguousarray(a["L1_ffn_wo"].reshape(NR, NF, 128, D).transpose(2, 1, 0, 3).reshape(128, NF, NR * D)),
    }
    n = np.arange(128)
    same = n[:, None] // NC8 == n // NC8
    earlier = n[:, None] < n
    f32 = np.float32
    d["blk"] = same.astype(f32)
    d["ltri"] = (same & earlier).astype(f32)
    d["before"] = earlier.astype(f32)
    d["idn"] = np.eye(128, dtype=f32)
    t, c = np.meshgrid(np.arange(TC), np.arange(NC8), indexing="ij")
    r = (2 * c + t // NT) * SP + t % NT * TT
    d["tabA"] = np.broadcast_to(r // 128, (TT, TC, NC8)).astype(f32)
    d["tabB"] = (r % 128 + np.arange(TT)[:, None, None]).astype(f32)
    d["mask"] = (n[:, None] % S8 == n % S8).astype(f32)
    b, s = n[:, None] // S8, n[:, None] % S8 + S8 * np.arange(TL)
    d["place"] = np.where(s < S, TOK - (b * S + s), 0).astype(f32)
    return d


_SCRATCH = [("qk", (2, PARTS, D, S), BF16), ("st", (EXP, B, S), F32), ("x1", (B, SP, XROW), F32), ("h3", (B, SP, D), F32),
            ("xs", (XS_TILES * 128, ROW), F32), ("lst", (EXP, SLOTS), I32)]


def kernel(**inputs):
    import concourse.bacc as bacc
    from concourse.bass_utils import run_bass_kernel_spmd as run

    nc = bacc.Bacc("TRN2", target_bir_lowering=False, num_devices=1)
    arrays = lay_out({k: np.asarray(v) for k, v in inputs.items()})
    arrays = {f"in_{k}_dram": np.ascontiguousarray(v) for k, v in arrays.items()}
    d = {k[3:-5]: nc.dram_tensor(k, v.shape, mybir.dt.from_np(v.dtype), kind="ExternalInput").ap() for k, v in arrays.items()}
    for name, shape, dt in _SCRATCH:
        d[name] = nc.dram_tensor(f"{name}_dram", shape, dt, kind="Internal").ap()
    d["out"] = nc.dram_tensor("out_dram", (B * S, D), F32, kind="ExternalOutput").ap()
    program(nc, d)
    r = run(nc, [arrays], core_ids=[0])
    return np.asarray(r.results[0]["out_dram"]).reshape(B, S, D)
```
